# Optimizing a Trainium2 kernel written in Bass

```python
import numpy as np
import jax
import jax.numpy as jnp

def _softmax(x, axis=-1):
    return jax.nn.softmax(x, axis=axis)

def _gelu(x):
    return jax.nn.gelu(x, approximate=True)

def _silu(x):
    return jax.nn.silu(x)

def _sigmoid(x):
    return jax.nn.sigmoid(x)

def _layernorm(x, axis=-1, eps=1e-05):
    m = jnp.mean(x, axis=axis, keepdims=True)
    v = jnp.var(x, axis=axis, keepdims=True)
    return (x - m) / jnp.sqrt(v + eps)

def _scatter_add(tgt, idx, src, axis=0):
    return tgt.at[idx].add(src)

def _segment_sum(src, seg, n):
    return jax.ops.segment_sum(src, seg, n)
kernel_name = 'mk_pixart_resid_d2_seqx_r8_b02793'

def setup_inputs(seed: int=0):
    np.random.seed(seed)
    _w = jnp.asarray

    def _rec_inputs():
        import jax
        import jax.numpy as jnp
        _rk = jax.random.key(seed)
        x = -0.003379 + 0.9984 * jax.random.normal(jax.random.fold_in(_rk, 1), (1, 1024, 128), jnp.float32)
        _lenS = 1024 - jax.random.randint(jax.random.fold_in(_rk, 7), (1,), 0, max(1, 1024 // 4) + 1, jnp.int32)
        _lenS2 = 6404 - jax.random.randint(jax.random.fold_in(_rk, 8), (1,), 0, max(1, 6404 // 4) + 1, jnp.int32)
        cond_1024 = -0.0142567 + 1.00875 * jax.random.normal(jax.random.fold_in(_rk, 11), (1, 128), jnp.float32)
        _ctx_1024P = jax.random.normal(jax.random.fold_in(_rk, 12), (1, 16, 128), jnp.float32)
        _ctx_1024c = jax.random.dirichlet(jax.random.fold_in(_rk, 512), 0.3 * jnp.ones((16,), jnp.float32), (1, 6404))
        _ctx_1024t = jnp.einsum('bsk,bkd->bsd', _ctx_1024c, _ctx_1024P)
        _ctx_1024t = _ctx_1024t * jax.lax.rsqrt(jnp.mean(jnp.square(_ctx_1024t)) + 1e-12) * 0.953939
        ctx_1024 = -5.72187e-05 + 0.999849 * (_ctx_1024t + 0.3 * jax.random.normal(jax.random.fold_in(_rk, 612), (1, 6404, 128), jnp.float32))
        return (x, cond_1024, ctx_1024)
    x, cond_1024, ctx_1024 = _rec_inputs()

    def _L0_xcond_setup():
        import jax, jax.numpy as jnp
        import numpy as np
        B, N, K, D, T = (16, 512, 16, 128, 3)
        EPS_ATTN = 1e-08
        LN_EPS = 1e-05

        def _ln(x, g, b):
            mu = jnp.mean(x, axis=-1, keepdims=True)
            var = jnp.mean(jnp.square(x - mu), axis=-1, keepdims=True)
            return (x - mu) * jax.lax.rsqrt(var + LN_EPS) * g + b
        key = jax.random.key(seed)
        ks = jax.random.split(key, 16)
        w = lambda k, i, o: jax.random.normal(k, (i, o), jnp.float32) * 0.02
        inp = {'x_cls': jax.random.normal(ks[0], (B, D), jnp.float32), 'x': jax.random.normal(ks[1], (B, N, D), jnp.float32), 'noise': jax.random.normal(ks[2], (B, K, D), jnp.float32), 'q_mu': jax.random.normal(ks[3], (1, 1, D), jnp.float32), 'q_logsig': jax.random.normal(ks[4], (1, 1, D), jnp.float32) * 0.02, 'lnkv_g': jnp.ones((D,), jnp.float32), 'lnkv_b': jnp.zeros((D,), jnp.float32), 'lnq_g': jnp.ones((D,), jnp.float32), 'lnq_b': jnp.zeros((D,), jnp.float32), 'lnm_g': jnp.ones((D,), jnp.float32), 'lnm_b': jnp.zeros((D,), jnp.float32), 'lnp_g': jnp.ones((D,), jnp.float32), 'lnp_b': jnp.zeros((D,), jnp.float32), 'wk': w(ks[5], D, D), 'bk': jnp.zeros((D,), jnp.float32), 'wv': w(ks[6], D, D), 'bv': jnp.zeros((D,), jnp.float32), 'wq': w(ks[7], D, D), 'bq': jnp.zeros((D,), jnp.float32), 'wu': w(ks[8], D, D), 'bu': jnp.zeros((D,), jnp.float32), 'w1': w(ks[9], D, D), 'b1': jnp.zeros((D,), jnp.float32), 'w2': w(ks[10], D, D), 'b2': jnp.zeros((D,), jnp.float32)}
        return inp
    _L0_xcond_all = _L0_xcond_setup()
    _L0_xcond_in = {k: v for k, v in _L0_xcond_all.items() if k in ('q_mu', 'q_logsig', 'lnkv_g', 'lnkv_b', 'lnq_g', 'lnq_b', 'lnm_g', 'lnm_b', 'lnp_g', 'lnp_b', 'wk', 'bk', 'wv', 'bv', 'wq', 'bq', 'wu', 'bu', 'w1', 'b1', 'w2', 'b2')}
    del _L0_xcond_all

    def _L0_ffn_setup():
        import math
        import jax, jax.numpy as jnp
        import numpy as np
        B, S, D, H, E, F = (2, 128, 128, 16, 16, 512)
        HEAD = D // H
        MOE_TOKEN_DROPOUT = 0.2
        EPS = 1e-05

        def layer_norm(x, w, b):
            mu = x.mean(-1, keepdims=True)
            var = ((x - mu) ** 2).mean(-1, keepdims=True)
            return (x - mu) * jax.lax.rsqrt(var + EPS) * w + b
        key = jax.random.key(seed)
        ks = jax.random.split(key, 16)
        w = lambda k, shape: jax.random.normal(k, shape, jnp.float32) * 0.02
        return {'hidden_states': jax.random.normal(ks[0], (B, S, D), jnp.float32), 'ln1_w': jnp.ones((D,), jnp.float32), 'ln1_b': jnp.zeros((D,), jnp.float32), 'q_w': w(ks[1], (D, D)), 'q_b': jnp.zeros((D,), jnp.float32), 'k_w': w(ks[2], (D, D)), 'k_b': jnp.zeros((D,), jnp.float32), 'v_w': w(ks[3], (D, D)), 'v_b': jnp.zeros((D,), jnp.float32), 'o_w': w(ks[4], (D, D)), 'o_b': jnp.zeros((D,), jnp.float32), 'ln2_w': jnp.ones((D,), jnp.float32), 'ln2_b': jnp.zeros((D,), jnp.float32), 'router_w': w(ks[5], (D, E)), 'fc1_w': w(ks[6], (E, D, F)), 'fc1_b': jnp.zeros((E, F), jnp.float32), 'fc2_w': w(ks[7], (E, F, D)), 'fc2_b': jnp.zeros((E, D), jnp.float32)}
    _L0_ffn_all = _L0_ffn_setup()
    _L0_ffn_in = {k: v for k, v in _L0_ffn_all.items() if k in ('ln1_w', 'ln1_b', 'q_w', 'q_b', 'k_w', 'k_b', 'v_w', 'v_b', 'o_w', 'o_b', 'ln2_w', 'ln2_b', 'router_w', 'fc1_w', 'fc1_b', 'fc2_w', 'fc2_b')}
    del _L0_ffn_all

    def _L1_xcond_setup():
        import jax, jax.numpy as jnp
        import numpy as np
        DIM = 128
        DIM_HEAD = 64
        HEADS = 16
        INNER = DIM_HEAD * HEADS
        B, N1, N2 = (8, 512, 32)
        EPS = 1e-05

        def layer_norm(x, w, b):
            mu = jnp.mean(x, axis=-1, keepdims=True)
            var = jnp.var(x, axis=-1, keepdims=True)
            return (x - mu) * jax.lax.rsqrt(var + EPS) * w + b
        key = jax.random.key(seed)
        ks = jax.random.split(key, 10)
        return {'x': jax.random.normal(ks[0], (B, N1, DIM), jnp.float32), 'latents': jax.random.normal(ks[1], (B, N2, DIM), jnp.float32), 'shift': jax.random.normal(ks[2], (B, DIM), jnp.float32), 'scale': jax.random.normal(ks[3], (B, DIM), jnp.float32), 'ln1_w': jnp.ones((DIM,), jnp.float32), 'ln1_b': jnp.zeros((DIM,), jnp.float32), 'ln2_w': jnp.ones((DIM,), jnp.float32), 'ln2_b': jnp.zeros((DIM,), jnp.float32), 'Wq': jax.random.normal(ks[4], (INNER, DIM), jnp.float32) * 0.02, 'Wkv': jax.random.normal(ks[5], (2 * INNER, DIM), jnp.float32) * 0.02, 'Wo': jax.random.normal(ks[6], (DIM, INNER), jnp.float32) * 0.02}
    _L1_xcond_all = _L1_xcond_setup()
    _L1_xcond_in = {k: v for k, v in _L1_xcond_all.items() if k in ('ln1_w', 'ln1_b', 'ln2_w', 'ln2_b', 'Wq', 'Wkv', 'Wo')}
    del _L1_xcond_all

    def _L1_ffn_setup():
        import jax, jax.numpy as jnp
        import numpy as np
        key = jax.random.key(seed)
        ks = jax.random.split(key, 6)
        B, L, D, E = (4, 256, 128, 4)
        H = 4 * D
        x = jax.random.normal(ks[0], (B, L, D), dtype=jnp.float32)
        rW1 = jax.random.normal(ks[1], (D, 2 * D), dtype=jnp.float32) * (2.0 / D) ** 0.5
        rb1 = jnp.zeros((2 * D,), dtype=jnp.float32)
        rW2 = jax.random.normal(ks[2], (2 * D, E), dtype=jnp.float32) * (2.0 / (2 * D)) ** 0.5
        rb2 = jnp.zeros((E,), dtype=jnp.float32)
        We1 = jax.random.normal(ks[3], (E, D, H), dtype=jnp.float32) * (2.0 / D) ** 0.5
        be1 = jnp.zeros((E, H), dtype=jnp.float32)
        We2 = jax.random.normal(ks[4], (E, H, D), dtype=jnp.float32) * (2.0 / H) ** 0.5
        be2 = jnp.zeros((E, D), dtype=jnp.float32)
        return {'x': x, 'rW1': rW1, 'rb1': rb1, 'rW2': rW2, 'rb2': rb2, 'We1': We1, 'be1': be1, 'We2': We2, 'be2': be2}
    _L1_ffn_all = _L1_ffn_setup()
    _L1_ffn_in = {k: v for k, v in _L1_ffn_all.items() if k in ('rW1', 'rb1', 'rW2', 'rb2', 'We1', 'be1', 'We2', 'be2')}
    del _L1_ffn_all
    return {'x': x, 'cond_1024': cond_1024, 'ctx_1024': ctx_1024, 'L0_xcond_q_mu': _L0_xcond_in['q_mu'], 'L0_xcond_q_logsig': _L0_xcond_in['q_logsig'], 'L0_xcond_lnkv_g': _L0_xcond_in['lnkv_g'], 'L0_xcond_lnkv_b': _L0_xcond_in['lnkv_b'], 'L0_xcond_lnq_g': _L0_xcond_in['lnq_g'], 'L0_xcond_lnq_b': _L0_xcond_in['lnq_b'], 'L0_xcond_lnm_g': _L0_xcond_in['lnm_g'], 'L0_xcond_lnm_b': _L0_xcond_in['lnm_b'], 'L0_xcond_lnp_g': _L0_xcond_in['lnp_g'], 'L0_xcond_lnp_b': _L0_xcond_in['lnp_b'], 'L0_xcond_wk': _L0_xcond_in['wk'], 'L0_xcond_bk': _L0_xcond_in['bk'], 'L0_xcond_wv': _L0_xcond_in['wv'], 'L0_xcond_bv': _L0_xcond_in['bv'], 'L0_xcond_wq': _L0_xcond_in['wq'], 'L0_xcond_bq': _L0_xcond_in['bq'], 'L0_xcond_wu': _L0_xcond_in['wu'], 'L0_xcond_bu': _L0_xcond_in['bu'], 'L0_xcond_w1': _L0_xcond_in['w1'], 'L0_xcond_b1': _L0_xcond_in['b1'], 'L0_xcond_w2': _L0_xcond_in['w2'], 'L0_xcond_b2': _L0_xcond_in['b2'], 'L0_ffn_ln1_w': _L0_ffn_in['ln1_w'], 'L0_ffn_ln1_b': _L0_ffn_in['ln1_b'], 'L0_ffn_q_w': _L0_ffn_in['q_w'], 'L0_ffn_q_b': _L0_ffn_in['q_b'], 'L0_ffn_k_w': _L0_ffn_in['k_w'], 'L0_ffn_k_b': _L0_ffn_in['k_b'], 'L0_ffn_v_w': _L0_ffn_in['v_w'], 'L0_ffn_v_b': _L0_ffn_in['v_b'], 'L0_ffn_o_w': _L0_ffn_in['o_w'], 'L0_ffn_o_b': _L0_ffn_in['o_b'], 'L0_ffn_ln2_w': _L0_ffn_in['ln2_w'], 'L0_ffn_ln2_b': _L0_ffn_in['ln2_b'], 'L0_ffn_router_w': _L0_ffn_in['router_w'], 'L0_ffn_fc1_w': _L0_ffn_in['fc1_w'], 'L0_ffn_fc1_b': _L0_ffn_in['fc1_b'], 'L0_ffn_fc2_w': _L0_ffn_in['fc2_w'], 'L0_ffn_fc2_b': _L0_ffn_in['fc2_b'], 'L1_xcond_ln1_w': _L1_xcond_in['ln1_w'], 'L1_xcond_ln1_b': _L1_xcond_in['ln1_b'], 'L1_xcond_ln2_w': _L1_xcond_in['ln2_w'], 'L1_xcond_ln2_b': _L1_xcond_in['ln2_b'], 'L1_xcond_Wq': _L1_xcond_in['Wq'], 'L1_xcond_Wkv': _L1_xcond_in['Wkv'], 'L1_xcond_Wo': _L1_xcond_in['Wo'], 'L1_ffn_rW1': _L1_ffn_in['rW1'], 'L1_ffn_rb1': _L1_ffn_in['rb1'], 'L1_ffn_rW2': _L1_ffn_in['rW2'], 'L1_ffn_rb2': _L1_ffn_in['rb2'], 'L1_ffn_We1': _L1_ffn_in['We1'], 'L1_ffn_be1': _L1_ffn_in['be1'], 'L1_ffn_We2': _L1_ffn_in['We2'], 'L1_ffn_be2': _L1_ffn_in['be2']}

def reference(x, cond_1024, ctx_1024, L0_xcond_q_mu, L0_xcond_q_logsig, L0_xcond_lnkv_g, L0_xcond_lnkv_b, L0_xcond_lnq_g, L0_xcond_lnq_b, L0_xcond_lnm_g, L0_xcond_lnm_b, L0_xcond_lnp_g, L0_xcond_lnp_b, L0_xcond_wk, L0_xcond_bk, L0_xcond_wv, L0_xcond_bv, L0_xcond_wq, L0_xcond_bq, L0_xcond_wu, L0_xcond_bu, L0_xcond_w1, L0_xcond_b1, L0_xcond_w2, L0_xcond_b2, L0_ffn_ln1_w, L0_ffn_ln1_b, L0_ffn_q_w, L0_ffn_q_b, L0_ffn_k_w, L0_ffn_k_b, L0_ffn_v_w, L0_ffn_v_b, L0_ffn_o_w, L0_ffn_o_b, L0_ffn_ln2_w, L0_ffn_ln2_b, L0_ffn_router_w, L0_ffn_fc1_w, L0_ffn_fc1_b, L0_ffn_fc2_w, L0_ffn_fc2_b, L1_xcond_ln1_w, L1_xcond_ln1_b, L1_xcond_ln2_w, L1_xcond_ln2_b, L1_xcond_Wq, L1_xcond_Wkv, L1_xcond_Wo, L1_ffn_rW1, L1_ffn_rb1, L1_ffn_rW2, L1_ffn_rb2, L1_ffn_We1, L1_ffn_be1, L1_ffn_We2, L1_ffn_be2):
    import jax
    import jax.numpy as jnp

    def _L0_xcond_ref(x_cls, x, noise, q_mu, q_logsig, lnkv_g, lnkv_b, lnq_g, lnq_b, lnm_g, lnm_b, lnp_g, lnp_b, wk, bk, wv, bv, wq, bq, wu, bu, w1, b1, w2, b2):
        import jax, jax.numpy as jnp
        import numpy as np
        B, N, K, D, T = (16, 512, 16, 128, 3)
        EPS_ATTN = 1e-08
        LN_EPS = 1e-05

        def _ln(x, g, b):
            mu = jnp.mean(x, axis=-1, keepdims=True)
            var = jnp.mean(jnp.square(x - mu), axis=-1, keepdims=True)
            return (x - mu) * jax.lax.rsqrt(var + LN_EPS) * g + b
        scale = D ** (-0.5)
        x_in = _ln(x, lnkv_g, lnkv_b)
        k = x_in @ wk + bk
        v = x_in @ wv + bv
        slots = q_mu + jnp.exp(q_logsig) * noise
        for _ in range(T):
            prev = slots
            q = _ln(slots, lnq_g, lnq_b) @ wq + bq
            logits = jnp.einsum('bnd,bkd->bnk', k, q) / scale
            attn = jax.nn.softmax(logits, axis=-1) + EPS_ATTN
            attn = attn / jnp.sum(attn, axis=1, keepdims=True)
            upd = jnp.einsum('bnk,bnd->bkd', attn, v)
            slots = upd @ wu + bu + prev
            h = _ln(slots, lnm_g, lnm_b) @ w1 + b1
            slots = jax.nn.gelu(h, approximate=False) @ w2 + b2 + slots
            slots = _ln(slots + x_cls[:, None, :], lnp_g, lnp_b)
        return slots

    def _L0_ffn_ref(hidden_states, ln1_w, ln1_b, q_w, q_b, k_w, k_b, v_w, v_b, o_w, o_b, ln2_w, ln2_b, router_w, fc1_w, fc1_b, fc2_w, fc2_b):
        import math
        import jax, jax.numpy as jnp
        import numpy as np
        B, S, D, H, E, F = (2, 128, 128, 16, 16, 512)
        HEAD = D // H
        MOE_TOKEN_DROPOUT = 0.2
        EPS = 1e-05

        def layer_norm(x, w, b):
            mu = x.mean(-1, keepdims=True)
            var = ((x - mu) ** 2).mean(-1, keepdims=True)
            return (x - mu) * jax.lax.rsqrt(var + EPS) * w + b
        b, s, _ = hidden_states.shape
        T = b * s
        neg = jnp.finfo(jnp.float32).min
        resid = hidden_states
        x = layer_norm(hidden_states, ln1_w, ln1_b)
        q = (x @ q_w + q_b) / math.sqrt(HEAD)
        k = x @ k_w + k_b
        v = x @ v_w + v_b
        split = lambda t: t.reshape(b, s, H, HEAD).transpose(0, 2, 1, 3)
        q, k, v = (split(q), split(k), split(v))
        scores = jnp.einsum('bhqd,bhkd->bhqk', q, k)
        causal = jnp.tril(jnp.ones((s, s), bool))
        scores = jnp.where(causal, scores, neg)
        attn = jax.nn.softmax(scores, axis=-1)
        ctx = jnp.einsum('bhqk,bhkd->bhqd', attn, v)
        ctx = ctx.transpose(0, 2, 1, 3).reshape(b, s, D)
        hidden = resid + (ctx @ o_w + o_b)
        resid = hidden
        xt = layer_norm(hidden, ln2_w, ln2_b).reshape(T, D)
        logits = xt @ router_w
        probs = jax.nn.softmax(logits, axis=-1)
        top1 = jnp.argmax(probs, axis=-1)
        m1 = jax.nn.one_hot(top1, E, dtype=jnp.float32)
        logits_no1 = jnp.where(m1 > 0, -jnp.inf, logits)
        top2 = jnp.argmax(logits_no1, axis=-1)
        m2 = jax.nn.one_hot(top2, E, dtype=jnp.float32)
        loc1 = jnp.cumsum(m1, axis=0) - 1.0
        loc2 = jnp.cumsum(m2, axis=0) - 1.0 + m1.sum(axis=0, keepdims=True)
        C = 2 * math.ceil(T / E)
        m1 = m1 * (loc1 < C)
        m2 = m2 * (loc2 < C)
        g1 = (probs * m1).sum(-1)
        g2 = (probs * m2).sum(-1)
        denom = jnp.maximum(g1 + g2, jnp.finfo(jnp.float32).eps)
        g1, g2 = (g1 / denom, g2 / denom)
        slot1 = (loc1 * m1).sum(-1).astype(jnp.int32)
        slot2 = (loc2 * m2).sum(-1).astype(jnp.int32)
        d1 = m1[:, :, None] * jax.nn.one_hot(slot1, C, dtype=jnp.float32)[:, None, :]
        d2 = m2[:, :, None] * jax.nn.one_hot(slot2, C, dtype=jnp.float32)[:, None, :]
        dispatch = d1 + d2
        combine = g1[:, None, None] * d1 + g2[:, None, None] * d2
        xin = jnp.einsum('tec,td->ecd', dispatch, xt)
        h = jnp.einsum('ecd,edf->ecf', xin, fc1_w) + fc1_b[:, None, :]
        h = jax.nn.gelu(h, approximate=False)
        eout = jnp.einsum('ecf,efd->ecd', h, fc2_w) + fc2_b[:, None, :]
        eout = eout * (1.0 - MOE_TOKEN_DROPOUT)
        moe_out = jnp.einsum('tec,ecd->td', combine, eout).reshape(b, s, D)
        return resid + moe_out

    def _L1_xcond_ref(x, latents, shift, scale, ln1_w, ln1_b, ln2_w, ln2_b, Wq, Wkv, Wo):
        import jax, jax.numpy as jnp
        import numpy as np
        DIM = 128
        DIM_HEAD = 64
        HEADS = 16
        INNER = DIM_HEAD * HEADS
        B, N1, N2 = (8, 512, 32)
        EPS = 1e-05

        def layer_norm(x, w, b):
            mu = jnp.mean(x, axis=-1, keepdims=True)
            var = jnp.var(x, axis=-1, keepdims=True)
            return (x - mu) * jax.lax.rsqrt(var + EPS) * w + b
        x = layer_norm(x, ln1_w, ln1_b)
        lat = layer_norm(latents, ln2_w, ln2_b)
        lat = lat * (1.0 + scale[:, None, :]) + shift[:, None, :]
        b, n2, _ = lat.shape
        q = jnp.einsum('bld,ed->ble', lat, Wq)
        kv_in = jnp.concatenate((x, lat), axis=-2)
        kv = jnp.einsum('bld,ed->ble', kv_in, Wkv)
        k, v = jnp.split(kv, 2, axis=-1)

        def to_heads(t):
            bsz, L, _ = t.shape
            return t.reshape(bsz, L, HEADS, DIM_HEAD).transpose(0, 2, 1, 3)
        q, k, v = (to_heads(q), to_heads(k), to_heads(v))
        attn_scale = 1.0 / np.sqrt(np.sqrt(DIM_HEAD)).astype(np.float32)
        logits = jnp.einsum('bhqd,bhkd->bhqk', q * attn_scale, k * attn_scale)
        w = jax.nn.softmax(logits.astype(jnp.float32), axis=-1).astype(logits.dtype)
        out = jnp.einsum('bhqk,bhkd->bhqd', w, v)
        out = out.transpose(0, 2, 1, 3).reshape(b, n2, INNER)
        return jnp.einsum('ble,de->bld', out, Wo)

    def _L1_ffn_ref(x, rW1, rb1, rW2, rb2, We1, be1, We2, be2):
        import jax, jax.numpy as jnp
        import numpy as np
        E = We1.shape[0]
        top_k = min(2, E)
        rh = jax.nn.gelu(x @ rW1 + rb1, approximate=False)
        router_logits = rh @ rW2 + rb2
        router_probs = jax.nn.softmax(router_logits, axis=-1)
        expert_weights, expert_indices = jax.lax.top_k(router_probs, top_k)
        one_hot = jax.nn.one_hot(expert_indices, E, dtype=x.dtype)
        token_mask = one_hot.sum(axis=2)
        combine_w = (one_hot * expert_weights[..., None]).sum(axis=2)
        out = jnp.zeros_like(x)
        for e in range(E):
            xi = x * token_mask[..., e:e + 1]
            h = jax.nn.gelu(xi @ We1[e] + be1[e], approximate=False)
            yo = h @ We2[e] + be2[e]
            out = out + yo * combine_w[..., e:e + 1]
        return out
    x = x + _L0_xcond_ref(cond_1024, ctx_1024, _layernorm(x, axis=-1), L0_xcond_q_mu, L0_xcond_q_logsig, L0_xcond_lnkv_g, L0_xcond_lnkv_b, L0_xcond_lnq_g, L0_xcond_lnq_b, L0_xcond_lnm_g, L0_xcond_lnm_b, L0_xcond_lnp_g, L0_xcond_lnp_b, L0_xcond_wk, L0_xcond_bk, L0_xcond_wv, L0_xcond_bv, L0_xcond_wq, L0_xcond_bq, L0_xcond_wu, L0_xcond_bu, L0_xcond_w1, L0_xcond_b1, L0_xcond_w2, L0_xcond_b2)
    x = x + _L0_ffn_ref(_layernorm(x, axis=-1), L0_ffn_ln1_w, L0_ffn_ln1_b, L0_ffn_q_w, L0_ffn_q_b, L0_ffn_k_w, L0_ffn_k_b, L0_ffn_v_w, L0_ffn_v_b, L0_ffn_o_w, L0_ffn_o_b, L0_ffn_ln2_w, L0_ffn_ln2_b, L0_ffn_router_w, L0_ffn_fc1_w, L0_ffn_fc1_b, L0_ffn_fc2_w, L0_ffn_fc2_b)
    x = x + _L1_xcond_ref(ctx_1024, _layernorm(x, axis=-1), cond_1024, cond_1024, L1_xcond_ln1_w, L1_xcond_ln1_b, L1_xcond_ln2_w, L1_xcond_ln2_b, L1_xcond_Wq, L1_xcond_Wkv, L1_xcond_Wo)
    x = x + _L1_ffn_ref(_layernorm(x, axis=-1), L1_ffn_rW1, L1_ffn_rb1, L1_ffn_rW2, L1_ffn_rb2, L1_ffn_We1, L1_ffn_be1, L1_ffn_We2, L1_ffn_be2)
    return x

_drawn_inputs = setup_inputs


def setup_inputs(seed=0):
    import zlib

    import numpy as np

    out = dict(_drawn_inputs(seed))
    spreads = {'L0_xcond_lnkv_g': (1.0, 0.6),
     'L0_xcond_lnkv_b': (0.0, 0.579),
     'L0_xcond_lnq_g': (1.0, 0.6),
     'L0_xcond_lnq_b': (0.0, 2.0),
     'L0_xcond_lnm_g': (1.0, 0.6),
     'L0_xcond_lnm_b': (0.0, 0.8),
     'L0_xcond_lnp_g': (1.0, 0.2),
     'L0_xcond_lnp_b': (0.0, 0.1),
     'L0_xcond_bk': (0.0, 0.8),
     'L0_xcond_bv': (0.0, 0.34),
     'L0_xcond_bq': (0.0, 2.0),
     'L0_xcond_bu': (0.0, 0.1),
     'L0_xcond_b1': (0.0, 0.624),
     'L0_xcond_b2': (0.0, 0.1),
     'L0_ffn_ln1_w': (1.0, 0.6),
     'L0_ffn_ln1_b': (0.0, 0.621),
     'L0_ffn_q_b': (0.0, 0.8),
     'L0_ffn_k_b': (0.0, 2.0),
     'L0_ffn_v_b': (0.0, 0.441),
     'L0_ffn_o_b': (0.0, 0.1),
     'L0_ffn_ln2_w': (1.0, 0.6),
     'L0_ffn_ln2_b': (0.0, 0.404),
     'L0_ffn_fc1_b': (0.0, 0.751),
     'L0_ffn_fc2_b': (0.0, 0.274),
     'L1_xcond_ln1_w': (1.0, 0.6),
     'L1_xcond_ln1_b': (0.0, 0.8),
     'L1_xcond_ln2_w': (1.0, 0.6),
     'L1_xcond_ln2_b': (0.0, 0.8),
     'L1_ffn_rb1': (0.0, 0.1),
     'L1_ffn_rb2': (0.0, 0.1),
     'L1_ffn_be1': (0.0, 0.378),
     'L1_ffn_be2': (0.0, 0.364)}
    factors = {'L0_xcond_q_logsig': 6.625,
     'L0_xcond_wk': 2.755,
     'L0_xcond_wq': 2.674,
     'L0_ffn_q_w': 8.0,
     'L0_ffn_k_w': 8.0,
     'L0_ffn_fc1_w': 3.089,
     'L0_ffn_fc2_w': 2.731,
     'L1_xcond_Wq': 8.0}
    for name, (base, spread) in spreads.items():
        noise = np.random.default_rng([zlib.crc32(name.encode()), seed]).standard_normal(out[name].shape)
        drawn = base * np.exp(spread * noise) if base else spread * noise
        out[name] = jnp.asarray(drawn.astype(out[name].dtype))
    for name, factor in factors.items():
        out[name] = (out[name] * factor).astype(out[name].dtype)
    return out
```

```python
import concourse.bass as bass
from concourse import mybir
from contextlib import ExitStack

F32 = mybir.dt.float32
F32R = mybir.dt.float32r
U32 = mybir.dt.uint32
ALU = mybir.AluOpType
ACT = mybir.ActivationFunctionType
AX = mybir.AxisListType.X
ds = bass.ds

P = 128
D = 128
TOKENS = 1024
TT = TOKENS // P
CTX = 6404
CT = CTX // P
REST = CTX - CT * P
EPS = 1e-5
NEG = -1e30

ITERATIONS = 3
EPS_ATTN = 1e-8
SLOT_SCALE = float(D) ** 0.5
PREP = 5

H0 = 16
HD0 = D // H0
GROUP = 4
NG = H0 // GROUP
E0 = 16
F0 = 512
FB0 = F0 // P
CAP = 2 * (-(-TOKENS // E0))
KEEP = 1.0 - 0.2

H1 = 16
HD1 = 64
KEYS = CTX + TOKENS
STEP = 2 * P
NS = KEYS // STEP
LAST = KEYS - NS * STEP
STEPS = NS + 1
assert STEPS % 2 == 0
LAT0 = CT * P
REST0 = LAT0 + TOKENS
assert CAP == P and REST0 == NS * STEP and LAST == REST and LAST % 2 == 0

E1 = 4
F1 = 512
FB1 = F1 // P
R1 = 256
RB1 = R1 // P

COLS = ["L0_xcond_lnkv_g", "L0_xcond_lnkv_b", "L0_xcond_bk", "L0_xcond_lnq_g", "L0_xcond_lnq_b", "L0_xcond_bq",
        "L0_xcond_lnm_g", "L0_xcond_lnm_b", "L0_xcond_b1", "L0_ffn_ln1_w", "L0_ffn_ln1_b", "L0_ffn_q_b",
        "L0_ffn_k_b", "L1_xcond_ln1_w", "L1_xcond_ln1_b", "L1_xcond_ln2_w", "L1_xcond_ln2_b", "cond_1024",
        "L1_ffn_rb1", "L1_ffn_be1", "L0_ffn_fc1_b"]
COL_N = [1] * 18 + [RB1, E1 * FB1, E0 * FB0]
ROWS = ["L0_xcond_q_mu", "L0_xcond_q_logsig", "L0_xcond_bv", "L0_xcond_bu", "L0_xcond_b2", "L0_xcond_lnp_g",
        "L0_xcond_lnp_b", "cond_1024", "L0_ffn_v_b", "L0_ffn_o_b", "L0_ffn_ln2_w", "L0_ffn_ln2_b"]
SQUARE = ["L0_xcond_wk", "L0_xcond_wv", "L0_xcond_wq", "L0_xcond_wu", "L0_xcond_w1", "L0_xcond_w2",
          "L0_ffn_q_w", "L0_ffn_k_w", "L0_ffn_v_w", "L0_ffn_o_w"]


class Signal:

    def __init__(self, sem):
        self.sem, self.total = sem, 0

    def at(self, n):
        return self.total + n

    def link(self, engine, instruction):
        self.total += 1
        instruction.then_inc(self.sem, 1)
        engine.wait_ge(self.sem, self.total)


class Core:

    def __init__(self, nc, ctx):
        self.nc, self.ctx, self.signals, self.names = nc, ctx, {}, 0
        self.ps = ctx.enter_context(nc.psum_tensor("banks", [P, 8, 512], F32))

    def sb(self, name, shape, dtype=F32, ctx=None):
        self.names += 1
        return (ctx or self.ctx).enter_context(self.nc.sbuf_tensor(f"{name}_{self.names}", shape, dtype))

    def sig(self, name):
        if name not in self.signals:
            self.signals[name] = Signal(self.ctx.enter_context(self.nc.semaphore(name)))
        return self.signals[name]

    def col(self, name, n=0):
        at = sum(COL_N[:COLS.index(name)]) + n
        return self.cols[:, at:at + 1]

    def row(self, name, parts=P):
        return self.rows[0:parts, ROWS.index(name), :]

    def row_of_tiles(self, name, tiles):
        return self.row(name).unsqueeze(1).to_broadcast([P, tiles, D])

    def square(self, name):
        return self.squares[:, SQUARE.index(name), :]


def load_constants(k, A):
    loaded, made = k.sig("constants_loaded"), k.sig("constants_made")
    with k.nc.Block() as block:
        @block.sync
        def _(sp):
            sp.dma_start(k.cols[:], A["cols"]).then_inc(loaded.sem, 16)
            sp.dma_start(k.rows[:], A["rows"].partition_broadcast(P)).then_inc(loaded.sem, 16)
            sp.dma_start(k.squares[:], A["squares"]).then_inc(loaded.sem, 16)
            sp.dma_start(k.x[:], A["x"][0].rearrange("(t p) d -> p t d", p=P)).then_inc(loaded.sem, 16)
            sp.wait_ge(loaded.sem, loaded.at(64))

        @block.gpsimd
        def _(pool):
            pool.memset(k.ident[:], 0.0).then_inc(made.sem, 1)
            pool.memset(k.ones[:], 1.0).then_inc(made.sem, 1)
            pool.memset(k.half[:], -0.5).then_inc(made.sem, 1)
            pool.wait_ge(made.sem, made.at(3))
            pool.affine_select(out=k.ident[:], in_=k.ident[:], compare_op=ALU.not_equal, fill=1.0, base=0,
                               pattern=[[-1, P]], channel_multiplier=1).then_inc(made.sem, 1)
            pool.wait_ge(made.sem, made.at(4))
    loaded.total += 64
    made.total += 4


def layernorm_rows(k, src, dst, parts=P, tiles=TT, gain=None, shift=None):
    step, squared, rooted = k.sig("norm_step"), k.sig("norm_squared"), k.sig("norm_rooted")
    mean, var, rstd = (k.stat[0:parts, n, 0:tiles] for n in range(3))
    square = k.scratch[0:parts, 0:tiles * D].rearrange("p (t d) -> p t d", d=D)
    over = [parts, tiles, D]
    centered, var_ready = step.at(3), step.at(5)
    with k.nc.Block() as block:
        @block.vector
        def _(v):
            step.link(v, v.reduce_sum(mean, src, axis=AX))
            step.link(v, v.tensor_scalar(mean, mean, 1.0 / D, None, ALU.mult))
            step.link(v, v.tensor_tensor(dst, src, mean.unsqueeze(2).to_broadcast(over), ALU.subtract))
            v.wait_ge(squared.sem, squared.at(1))
            step.link(v, v.reduce_sum(var, square, axis=AX))
            step.link(v, v.tensor_scalar(var, var, 1.0 / D, EPS, ALU.mult, ALU.add))
            v.wait_ge(rooted.sem, rooted.at(1))
            step.link(v, v.tensor_tensor(dst, dst, rstd.unsqueeze(2).to_broadcast(over), ALU.mult))
            if gain is not None:
                step.link(v, v.tensor_tensor(dst, dst, gain.unsqueeze(1).to_broadcast(over), ALU.mult))
                step.link(v, v.tensor_tensor(dst, dst, shift.unsqueeze(1).to_broadcast(over), ALU.add))

        @block.scalar
        def _(act):
            act.wait_ge(step.sem, centered)
            act.activation(square, dst, ACT.Square).then_inc(squared.sem, 1)

        @block.gpsimd
        def _(pool):
            pool.wait_ge(step.sem, var_ready)
            pool.tensor_tensor(rstd, var, k.half[0:parts, 0:tiles], ALU.pow).then_inc(rooted.sem, 1)
    squared.total += 1
    rooted.total += 1


def transpose_rows(k, src, dst, gain=None, shift=None):
    turned, kept = k.sig("turned"), k.sig("turned_kept")
    with k.nc.Block() as block:
        @block.tensor
        def _(pe):
            for t in range(TT):
                pe.transpose(k.ps[:, t // 4, t % 4 * P:(t % 4 + 1) * P], src[:, t, :],
                             k.ident[:]).then_inc(turned.sem, 1)

        @block.vector
        def _(v):
            v.wait_ge(turned.sem, turned.at(4))
            if gain is None:
                v.tensor_copy(dst[:, 0:512], k.ps[:, 0, :]).then_inc(kept.sem, 1)
            else:
                v.tensor_scalar(dst[:, 0:512], k.ps[:, 0, :], gain, shift, ALU.mult, ALU.add).then_inc(kept.sem, 1)

        @block.scalar
        def _(act):
            act.wait_ge(turned.sem, turned.at(TT))
            if gain is None:
                act.activation(dst[:, 512:1024], k.ps[:, 1, :], ACT.Copy).then_inc(kept.sem, 1)
            else:
                act.activation(dst[:, 512:1024], k.ps[:, 1, :], ACT.Identity, bias=shift,
                               scale=gain).then_inc(kept.sem, 1)
    turned.total += TT
    kept.total += 2


def project_columns(k, w, src, take):
    ready, taken = k.sig("columns_ready"), k.sig("columns_taken")
    with k.nc.Block() as block:
        @block.tensor
        def _(pe):
            for half in range(2):
                pe.matmul(k.ps[:, half, :], w, src[:, half * 512:(half + 1) * 512], start=True,
                          stop=True).then_inc(ready.sem, 1)

        @block.vector
        def _(v):
            for half in range(2):
                v.wait_ge(ready.sem, ready.at(half + 1))
                take(v, half, k.ps[:, half, :])
    ready.total += 2


def project_rows(k, src, w, take):
    ready = k.sig("rows_ready")
    with k.nc.Block() as block:
        @block.tensor
        def _(pe):
            for t in range(TT):
                pe.matmul(k.ps[:, t // 4, t % 4 * P:(t % 4 + 1) * P], src[:, t * P:(t + 1) * P], w, start=True,
                          stop=True).then_inc(ready.sem, 1)

        @block.vector
        def _(v):
            v.wait_ge(ready.sem, ready.at(TT))
            take(v, k.ps[:, 0:2, :].rearrange("p b (t d) -> p (b t) d", d=D))
    ready.total += TT


def keep(k, v, instruction):
    k.sig("vector_step").link(v, instruction)


def split_columns(k, v, bank, bias, scale, whole, high, low):
    keep(k, v, v.tensor_scalar(whole, bank, bias, scale, ALU.add, ALU.mult))
    keep(k, v, v.tensor_copy(high, whole))
    keep(k, v, v.tensor_tensor(low, whole, high.bitcast(F32), ALU.subtract))



def load_context(k, A, rows, rest):
    loaded = k.sig("context_loaded")
    with k.nc.Block() as block:
        @block.sync
        def _(sp):
            sp.dma_start(rows[:], A["ctx_1024"][0, 0:CT * P, :].rearrange("(p t) d -> p t d", t=CT)) \
              .then_inc(loaded.sem, 16)
            sp.dma_start(rest[0:REST, 0, :], A["ctx_1024"][0, CT * P:CTX, :]).then_inc(loaded.sem, 16)
            sp.wait_ge(loaded.sem, loaded.at(32))
    loaded.total += 32
    layernorm_rows(k, rows[:], rows[:], P, CT)
    layernorm_rows(k, rest[0:REST], rest[0:REST], REST, 1)


def slot_keys_values(k, rows, rest, k_high, k_low, values):
    nc = k.nc
    staged_s, turned_s, kept_s = k.sig("rows_staged"), k.sig("context_turned"), k.sig("context_kept")
    input_s, keys_s, values_s = k.sig("input_ready"), k.sig("keys_ready"), k.sig("values_ready")
    high_s, low_s, stored_s = k.sig("keys_high"), k.sig("keys_low"), k.sig("values_stored")
    N = CT // PREP
    W = PREP * P
    with ExitStack() as ctx:
        staged = k.sb("staged_rows", [P, 2, PREP, D], ctx=ctx)
        inputs = k.sb("slot_inputs", [P, 2, W], ctx=ctx)
        turned = k.ps[:, 0:2, :].rearrange("p b c -> p (b c)")
        keys = k.ps[:, 2:4, :].rearrange("p b c -> p (b c)")
        vals = k.ps[:, 4:6, :].rearrange("p b c -> p (b c)")

        def pieces(width):
            return [(a, min(a + 512, width)) for a in range(0, width, 512)]

        with nc.Block() as block:
            def scalar_step(act, i, r, tiles, parts, first, early):
                width = (tiles - 1) * P + parts
                at = REST0 if i is None else i * W
                to = CT * P if i is None else i * W
                n = N if i is None else i
                if not early:
                    act.wait_ge(turned_s.sem, turned_s.at(0) + n - 1)
                act.activation(staged[0:parts, r, 0:tiles, :],
                               rest[0:parts, 0:1, :] if i is None else rows[:, ds(i * PREP, PREP), :],
                               ACT.Copy).then_inc(staged_s.sem, 1)
                act.wait_ge(turned_s.sem, turned_s.at(1) + n)
                act.activation(k.zT[:, ds(at, width)], turned[:, 0:width], ACT.Copy).then_inc(kept_s.sem, 1)
                act.wait_ge(keys_s.sem, keys_s.at(1) + n)
                act.activation(k_high[:, ds(to, width)], keys[:, 0:width], ACT.Identity,
                               bias=k.col("L0_xcond_bk")).then_inc(high_s.sem, 1)

            def tensor_step(pe, i, r, tiles, parts, first, early):
                width = (tiles - 1) * P + parts
                n = N if i is None else i
                pe.wait_ge(staged_s.sem, staged_s.at(1) + n)
                if not first:
                    pe.wait_ge(kept_s.sem, kept_s.at(0) + n)
                    pe.wait_ge(input_s.sem, input_s.at(0) + n)
                for t in range(tiles):
                    last = pe.transpose(turned[:, t * P:t * P + parts], staged[0:parts, r, t, :],
                                        k.ident[0:parts, 0:parts])
                last.then_inc(turned_s.sem, 1)
                pe.wait_ge(input_s.sem, input_s.at(1) + n)
                if not first:
                    pe.wait_ge(high_s.sem, high_s.at(0) + n)
                    pe.wait_ge(low_s.sem, low_s.at(0) + n)
                for a, b in pieces(width):
                    last = pe.matmul(keys[:, a:b], k.square("L0_xcond_wk"), inputs[:, r, a:b], start=True, stop=True)
                last.then_inc(keys_s.sem, 1)
                if not first:
                    pe.wait_ge(stored_s.sem, stored_s.at(0) + n)
                for t in range(tiles):
                    last = pe.matmul(vals[0:parts, t * P:(t + 1) * P], inputs[:, r, t * P:t * P + parts],
                                     k.square("L0_xcond_wv"), start=True, stop=True)
                last.then_inc(values_s.sem, 1)

            def vector_step(v, i, r, tiles, parts, first, early):
                width = (tiles - 1) * P + parts
                to = CT * P if i is None else i * W
                n = N if i is None else i
                v.wait_ge(kept_s.sem, kept_s.at(1) + n)
                if not early:
                    v.wait_ge(values_s.sem, values_s.at(0) + n - 1)
                v.tensor_scalar(inputs[:, r, 0:width], turned[:, 0:width], k.col("L0_xcond_lnkv_g"),
                                k.col("L0_xcond_lnkv_b"), ALU.mult, ALU.add).then_inc(input_s.sem, 1)
                v.wait_ge(high_s.sem, high_s.at(1) + n)
                high = k_high[:, ds(to, width)]
                v.scalar_tensor_tensor(out=k_low[:, ds(to, width)], in0=keys[:, 0:width],
                                       scalar=k.col("L0_xcond_bk"), in1=high.bitcast(F32), op0=ALU.add,
                                       op1=ALU.subtract).then_inc(low_s.sem, 1)
                v.wait_ge(values_s.sem, values_s.at(1) + n)
                v.tensor_tensor(values[0:parts, ds(CT if i is None else i * PREP, tiles), :],
                                vals[0:parts, 0:tiles * D].rearrange("p (t d) -> p t d", d=D),
                                k.row("L0_xcond_bv", parts).unsqueeze(1).to_broadcast([parts, tiles, D]),
                                ALU.add).then_inc(stored_s.sem, 1)

            def steps(engine, step):
                step(engine, 0, 0, PREP, P, True, True)
                step(engine, 1, 1, PREP, P, False, True)
                with engine.Fori(1, N // 2) as m:
                    i = m * 2
                    step(engine, i, 0, PREP, P, False, False)
                    step(engine, i + 1, 1, PREP, P, False, False)
                step(engine, None, 0, 1, REST, False, False)

            @block.scalar
            def _(act):
                steps(act, scalar_step)

            @block.tensor
            def _(pe):
                steps(pe, tensor_step)

            @block.vector
            def _(v):
                steps(v, vector_step)
        for s in (staged_s, turned_s, kept_s, input_s, keys_s, values_s, high_s, low_s, stored_s):
            s.total += N + 1


def value_sum(k, values, vsum):
    summed = k.sig("values_summed")
    with ExitStack() as ctx:
        part = k.sb("values_part", [P, D], ctx=ctx)
        with k.nc.Block() as block:
            @block.vector
            def _(v):
                keep(k, v, v.reduce_sum(part[:], values[:, 0:CT, :].rearrange("p t d -> p d t"), axis=AX))
                keep(k, v, v.tensor_tensor(part[0:REST], part[0:REST], values[0:REST, CT, :], ALU.add))
        with k.nc.Block() as block:
            @block.tensor
            def _(pe):
                pe.matmul(k.ps[:, 0, 0:1], part[:], k.ones[:, 0:1], start=True, stop=True).then_inc(summed.sem, 1)

            @block.vector
            def _(v):
                v.wait_ge(summed.sem, summed.at(1))
                keep(k, v, v.tensor_scalar(vsum[:], k.ps[:, 0, 0:1], EPS_ATTN, None, ALU.mult))
        summed.total += 1


def slot_scores_and_updates(k, k_high, k_low, values, q_high, q_low, total):
    nc = k.nc
    staged_s, scores_s, probs_s = k.sig("key_staged"), k.sig("scores_ready"), k.sig("probs_ready")
    max_s, bias_s, recip_s = k.sig("slot_max"), k.sig("slot_bias"), k.sig("slot_recip")
    total_s, scaled_s, update_s = k.sig("total_added"), k.sig("value_scaled"), k.sig("update_added")
    with ExitStack() as ctx:
        key = k.sb("key_tile", [P, 2, 2, P], F32R, ctx=ctx)
        probs = k.sb("slot_probs", [P, 2, TOKENS], ctx=ctx)
        value = k.sb("value_tile", [P, 2, D], ctx=ctx)
        small = k.sb("slot_small", [P, 2, 4], ctx=ctx)
        scores = [k.ps[:, 2 * r:2 * r + 2, :] for r in range(2)]
        update = k.ps[:, 4:6, :]

        with nc.Block() as block:
            @block.gpsimd
            def _(pool):
                def stage(i, r, parts=P, first=False):
                    if not first:
                        pool.wait_ge(scores_s.sem, scores_s.at(-1) + i)
                    for n, source in enumerate((k_high, k_low)):
                        pool.tensor_copy(key[:, r, n, 0:parts], source[:, ds(i * P, parts)]).then_inc(staged_s.sem, 1)

                def scale(i, r, parts=P, first=False):
                    pool.wait_ge(recip_s.sem, recip_s.at(1) + i)
                    if not first:
                        pool.wait_ge(update_s.sem, update_s.at(-1) + i)
                    pool.tensor_tensor(value[0:parts, r, :], values[0:parts, ds(i, 1), :].squeeze(1),
                                       small[0:parts, r, 3:4].to_broadcast([parts, D]),
                                       ALU.mult).then_inc(scaled_s.sem, 1)

                stage(0, 0, first=True)
                stage(1, 1, first=True)
                for i in range(2):
                    scale(i, i, first=True)
                    stage(i + 2, i)
                with pool.Fori(1, CT // 2 - 1) as m:
                    i = m * 2
                    for r in range(2):
                        scale(i + r, r)
                        stage(i + r + 2, r)
                scale(CT - 2, 0)
                stage(CT, 0, REST)
                scale(CT - 1, 1)
                scale(CT, 0, REST)

            @block.tensor
            def _(pe):
                def score(i, r, first=False):
                    pe.wait_ge(staged_s.sem, staged_s.at(2) + i * 2)
                    if not first:
                        pe.wait_ge(probs_s.sem, probs_s.at(-1) + i)
                    for c in range(2):
                        cols = slice(c * 512, (c + 1) * 512)
                        pe.matmul(scores[r][:, c, :], key[:, r, 0, :], q_high[:, cols], start=True, stop=False)
                        pe.matmul(scores[r][:, c, :], key[:, r, 1, :], q_high[:, cols], start=False, stop=False)
                        last = pe.matmul(scores[r][:, c, :], key[:, r, 0, :], q_low[:, cols], start=False, stop=True)
                    last.then_inc(scores_s.sem, 1)

                def add(i, r, parts=P, first=False, final=False):
                    pe.wait_ge(scaled_s.sem, scaled_s.at(1) + i)
                    pe.wait_ge(probs_s.sem, probs_s.at(1) + i)
                    for c in range(2):
                        last = pe.matmul(update[:, c, :], value[0:parts, r, :], probs[0:parts, r, c * 512:(c + 1) * 512],
                                         start=first, stop=final)
                    last.then_inc(update_s.sem, 1)

                score(0, 0, first=True)
                score(1, 1, first=True)
                add(0, 0, first=True)
                with pe.Fori(0, CT // 2 - 1) as m:
                    i = m * 2 + 1
                    score(i + 1, 0)
                    add(i, 1)
                    score(i + 2, 1)
                    add(i + 1, 0)
                score(CT, 0)
                add(CT - 1, 1)
                add(CT, 0, REST, final=True)

            @block.vector
            def _(v):
                def bound(i, r, parts=P):
                    v.wait_ge(scores_s.sem, scores_s.at(1) + i)
                    v.reduce_max(small[0:parts, r, 0:1], scores[r][0:parts].rearrange("p b c -> p (b c)"),
                                 axis=AX).then_inc(max_s.sem, 1)
                    v.wait_ge(max_s.sem, max_s.at(1) + i)
                    v.tensor_scalar(small[0:parts, r, 1:2], small[0:parts, r, 0:1], -SLOT_SCALE, None,
                                    ALU.mult).then_inc(bias_s.sem, 1)

                def invert(i, r, parts=P, first=False):
                    v.wait_ge(probs_s.sem, probs_s.at(1) + i)
                    if not first:
                        v.wait_ge(scaled_s.sem, scaled_s.at(-1) + i)
                    v.reciprocal(small[0:parts, r, 3:4], small[0:parts, r, 2:3]).then_inc(recip_s.sem, 1)

                def count(i, r, parts=P):
                    v.wait_ge(recip_s.sem, recip_s.at(1) + i)
                    v.wait_ge(total_s.sem, total_s.at(1) + i)
                    v.scalar_tensor_tensor(out=total[0:parts], in0=probs[0:parts, r, :], scalar=small[0:parts, r, 3:4],
                                           in1=total[0:parts], op0=ALU.mult, op1=ALU.add).then_inc(total_s.sem, 1)

                v.memset(total[:], 0.0).then_inc(total_s.sem, 1)
                bound(0, 0)
                for i, first in ((1, True), (2, True)):
                    invert(i - 1, (i - 1) % 2, first=first)
                    bound(i, i % 2)
                    count(i - 1, (i - 1) % 2)
                with v.Fori(1, CT // 2 - 1) as m:
                    i = m * 2 + 1
                    for r in (1, 0):
                        n = i if r else i + 1
                        invert(n - 1, 1 - r)
                        bound(n, r)
                        count(n - 1, 1 - r)
                invert(CT - 2, 0)
                bound(CT - 1, 1)
                count(CT - 2, 0)
                invert(CT - 1, 1)
                bound(CT, 0, REST)
                count(CT - 1, 1)
                invert(CT, 0, REST)
                count(CT, 0, REST)

            @block.scalar
            def _(act):
                def exponential(i, r, parts=P, first=False):
                    act.wait_ge(bias_s.sem, bias_s.at(1) + i)
                    if not first:
                        act.wait_ge(update_s.sem, update_s.at(-1) + i)
                        act.wait_ge(total_s.sem, total_s.at(0) + i)
                    act.activation(probs[0:parts, r, :], scores[r][0:parts].rearrange("p b c -> p (b c)"), ACT.Exp,
                                   bias=small[0:parts, r, 1:2], scale=SLOT_SCALE,
                                   accum_out=small[0:parts, r, 2:3]).then_inc(probs_s.sem, 1)

                exponential(0, 0, first=True)
                exponential(1, 1, first=True)
                with act.Fori(1, CT // 2) as m:
                    i = m * 2
                    exponential(i, 0)
                    exponential(i + 1, 1)
                exponential(CT, 0, REST)
        for s in (scores_s, probs_s, max_s, bias_s, recip_s, scaled_s, update_s):
            s.total += CT + 1
        staged_s.total += 2 * (CT + 1)
        total_s.total += CT + 2


def slot_normalise(k, total, vsum, update):
    summed = k.sig("total_summed")
    with k.nc.Block() as block:
        @block.tensor
        def _(pe):
            for c in range(2):
                pe.matmul(k.ps[:, c, :], k.ones[:], total[:, c * 512:(c + 1) * 512], start=True,
                          stop=True).then_inc(summed.sem, 1)

        @block.vector
        def _(v):
            whole = k.ps[:, 0:2, :].rearrange("p b c -> p (b c)")
            added = k.ps[:, 4:6, :].rearrange("p b c -> p (b c)")
            v.wait_ge(summed.sem, summed.at(2))
            keep(k, v, v.tensor_scalar(update[:], whole, CTX * EPS_ATTN, None, ALU.add))
            keep(k, v, v.reciprocal(update[:], update[:]))
            keep(k, v, v.scalar_tensor_tensor(out=update[:], in0=added, scalar=vsum[:], in1=update[:], op0=ALU.add,
                                              op1=ALU.mult))
    summed.total += 2


def gelu_columns(k, w, src, bias, dst):
    ready, done = k.sig("hidden_ready"), k.sig("hidden_done")
    with k.nc.Block() as block:
        @block.tensor
        def _(pe):
            for half in range(2):
                pe.matmul(k.ps[:, half, :], w, src[:, half * 512:(half + 1) * 512], start=True,
                          stop=True).then_inc(ready.sem, 1)

        @block.scalar
        def _(act):
            for half in range(2):
                act.wait_ge(ready.sem, ready.at(half + 1))
                act.activation(dst[:, half * 512:(half + 1) * 512], k.ps[:, half, :], ACT.Gelu,
                               bias=bias).then_inc(done.sem, 1)
    ready.total += 2
    done.total += 2


def slot_attention(k, A, whole=True):
    with ExitStack() as ctx:
        k_high = k.sb("k_high", [P, CTX], F32R, ctx=ctx)
        k_low = k.sb("k_low", [P, CTX], F32R, ctx=ctx)
        values = k.sb("values", [P, CT + 1, D], ctx=ctx)
        with ExitStack() as inner:
            rows = k.sb("context_rows", [P, CT, D], ctx=inner)
            rest = k.sb("context_rest", [P, 1, D], ctx=inner)
            k.scratch = k.sb("norm_scratch_context", [P, CT * D], ctx=inner)
            load_context(k, A, rows, rest)
            slot_keys_values(k, rows, rest, k_high, k_low, values)
        k.scratch = k.norm_scratch
        if not whole:
            return
        slots = k.sb("slots", [P, TT, D], ctx=ctx)
        normed = k.sb("slots_normed", [P, TT, D], ctx=ctx)
        turned = k.sb("slots_turned", [P, TOKENS], ctx=ctx)
        q_high = k.sb("q_high", [P, TOKENS], F32R, ctx=ctx)
        q_low = k.sb("q_low", [P, TOKENS], F32R, ctx=ctx)
        total = k.sb("attention_total", [P, TOKENS], ctx=ctx)
        vsum = k.sb("value_sum", [P, 1], ctx=ctx)
        sigma = k.sb("slot_sigma", [P, D], ctx=ctx)
        value_sum(k, values, vsum)
        layernorm_rows(k, k.x[:], normed[:])
        exp_s = k.sig("sigma_ready")
        with k.nc.Block() as block:
            @block.scalar
            def _(act):
                act.activation(sigma[:], k.row("L0_xcond_q_logsig"), ACT.Exp).then_inc(exp_s.sem, 1)

            @block.vector
            def _(v):
                v.wait_ge(exp_s.sem, exp_s.at(1))
                over = [P, TT, D]
                keep(k, v, v.tensor_tensor(slots[:], normed[:], sigma[:].unsqueeze(1).to_broadcast(over), ALU.mult))
                keep(k, v, v.tensor_tensor(slots[:], slots[:], k.row_of_tiles("L0_xcond_q_mu", TT), ALU.add))
        exp_s.total += 1

        def take_queries(v, half, bank):
            cols = slice(half * 512, (half + 1) * 512)
            split_columns(k, v, bank, k.col("L0_xcond_bq"), 1.0, turned[:, cols], q_high[:, cols], q_low[:, cols])

        def take_slots(bias):
            def take(v, rows):
                keep(k, v, v.tensor_tensor(slots[:], slots[:], rows, ALU.add))
                keep(k, v, v.tensor_tensor(slots[:], slots[:], k.row_of_tiles(bias, TT), ALU.add))
            return take

        for _ in range(ITERATIONS):
            layernorm_rows(k, slots[:], normed[:])
            transpose_rows(k, normed, total, k.col("L0_xcond_lnq_g"), k.col("L0_xcond_lnq_b"))
            project_columns(k, k.square("L0_xcond_wq"), total, take_queries)
            slot_scores_and_updates(k, k_high, k_low, values, q_high, q_low, total)
            slot_normalise(k, total, vsum, turned)
            project_rows(k, turned, k.square("L0_xcond_wu"), take_slots("L0_xcond_bu"))
            layernorm_rows(k, slots[:], normed[:])
            transpose_rows(k, normed, turned, k.col("L0_xcond_lnm_g"), k.col("L0_xcond_lnm_b"))
            gelu_columns(k, k.square("L0_xcond_w1"), turned, k.col("L0_xcond_b1"), total)
            project_rows(k, total, k.square("L0_xcond_w2"), take_slots("L0_xcond_b2"))
            with k.nc.Block() as block:
                @block.vector
                def _(v):
                    keep(k, v, v.tensor_tensor(normed[:], slots[:], k.row_of_tiles("cond_1024", TT), ALU.add))
            layernorm_rows(k, normed[:], slots[:], gain=k.row("L0_xcond_lnp_g"), shift=k.row("L0_xcond_lnp_b"))
        with k.nc.Block() as block:
            @block.vector
            def _(v):
                keep(k, v, v.tensor_tensor(k.x[:], k.x[:], slots[:], ALU.add))



def causal_attention(k, xaT, values, context):
    nc = k.nc
    parts = nc.dram_tensor("query_key_parts", [4, P, TOKENS], F32, kind="Internal").ap()
    S = {name: k.sig("causal_" + name) for name in (
        "parted", "loaded_even", "loaded_odd", "cleared", "fill", "peak", "negated", "turned", "shift", "score", "expd",
        "added", "kept", "back", "inverted", "context", "grouped")}
    ITEMS = GROUP * TT
    LOADED, LOADS = ("loaded_even", "loaded_odd"), 6 * 16

    def inc(name, instruction):
        instruction.then_inc(S[name].sem, 1)

    def wait(engine, name, n, g=0, per=0):
        engine.wait_ge(S[name].sem, S[name].at(n) + g * per)

    with ExitStack() as ctx:
        queries = [k.sb("queries", [P, GROUP, TOKENS], F32R, ctx=ctx) for _ in range(2)]
        keys = [k.sb("keys", [P, GROUP, TOKENS], F32R, ctx=ctx) for _ in range(2)]
        with ExitStack() as inner:
            whole = k.sb("split_whole", [P, TOKENS], ctx=inner)
            split = k.sb("split_parts", [P, 4, TOKENS], F32R, ctx=inner)
            for n, (w, b, scale) in enumerate((("L0_ffn_q_w", "L0_ffn_q_b", float(HD0) ** -0.5),
                                               ("L0_ffn_k_w", "L0_ffn_k_b", 1.0))):
                def take(v, half, bank):
                    cols = slice(half * 512, (half + 1) * 512)
                    split_columns(k, v, bank, k.col(b), scale, whole[:, cols], split[:, 2 * n, cols],
                                  split[:, 2 * n + 1, cols])
                project_columns(k, k.square(w), xaT, take)

            with nc.Block() as block:
                @block.sync
                def _(sp):
                    sp.dma_start(parts.rearrange("n p t -> p n t"), split[:].bitcast(F32)).then_inc(S["parted"].sem, 16)
                    sp.wait_ge(S["parted"].sem, 16)

                @block.vector
                def _(v):
                    for tile in queries + keys:
                        inc("cleared", v.memset(tile[:].bitcast(F32), 0.0))
                    wait(v, "cleared", 4)
                    for tile in keys:
                        inc("cleared", v.memset(tile[64:65].bitcast(F32), 1.0))
                    wait(v, "cleared", 6)
            S["cleared"].total += 6

        probs = k.sb("causal_probs", [P, 2, GROUP, TOKENS], ctx=ctx)
        value = k.sb("causal_value", [P, TT, 2, GROUP * 32], ctx=ctx)
        peaks = k.sb("causal_peaks", [P, GROUP, 64 + TT], ctx=ctx)
        out_sb = k.sb("causal_out", [P, TOKENS], ctx=ctx)
        inverse = k.sb("causal_inverse", [P, TT, GROUP], ctx=ctx)
        mask = k.sb("causal_mask", [P, 2, P], F32R, ctx=ctx)
        ident = k.sb("identity_r", [P, P], F32R, ctx=ctx)
        whole_mask = k.sb("whole_mask", [P, 2, P], ctx=ctx)
        spread = [k.ps[:, 2 * r:2 * r + 2, :].rearrange("p b c -> p (b c)") for r in range(2)]
        turned = k.ps[:, 4:6, :]
        out = k.ps[:, 6:8, :]

        with nc.Block() as block:
            @block.gpsimd
            def _(pool):
                pool.memset(whole_mask[:], 0.0).then_inc(S["cleared"].sem, 1)
                wait(pool, "cleared", 1)
                for n, sign in enumerate((1, -1)):
                    pool.affine_select(out=whole_mask[:, n, :], in_=whole_mask[:, n, :], compare_op=ALU.is_ge,
                                       fill=NEG, base=0, pattern=[[-sign, P]],
                                       channel_multiplier=sign).then_inc(S["cleared"].sem, 1)
                wait(pool, "cleared", 3)
                pool.tensor_copy(mask[:], whole_mask[:]).then_inc(S["cleared"].sem, 1)
                pool.tensor_copy(ident[:], k.ident[:]).then_inc(S["cleared"].sem, 1)
                pool.memset(peaks[:], 0.0).then_inc(S["cleared"].sem, 1)
                wait(pool, "cleared", 6)
        S["cleared"].total += 6

        def load(sp, g):
            r = g % 2
            if g >= 2:
                wait(sp, "score", ITEMS * (g - 1))
                wait(sp, "added", TT * (g - 1))
            for tile, order in ((queries[r], (0, 1, 0)), (keys[r], (2, 2, 3))):
                for n, part in enumerate(order):
                    sp.dma_start(tile[n * HD0:(n + 1) * HD0].bitcast(F32), parts[part, g * 32:(g + 1) * 32, :]
                                 .rearrange("(h r) t -> r h t", r=HD0)) \
                      .then_inc(S[LOADED[r]].sem, 16)

        def pieces(a, b):
            return [(x, min(b, (x // 512 + 1) * 512)) for x in [a] + [c for c in (512,) if a < c < b]]

        def fill(pe, g, r):
            for n in range(ITEMS):
                h, t = n // TT, n % TT
                if n >= 2:
                    wait(pe, "peak", n - 1, g, ITEMS)
                else:
                    wait(pe, "expd", 0, g, ITEMS)
                width = (t + 1) * P
                for a, b in pieces(0, width):
                    pe.matmul(spread[n % 2][:, a:b], queries[r][:, h, t * P:(t + 1) * P], keys[r][:, h, a:b],
                              start=True, stop=b < width)
                inc("fill", pe.matmul(spread[n % 2][:, width - P:width], ident[:], mask[:, 0, :], start=False, stop=True))
                if t == 1 and h:
                    turn_peaks(pe, g, h - 1)
            turn_peaks(pe, g, GROUP - 1)

        def turn_peaks(pe, g, h):
            wait(pe, "negated", h + 1, g, GROUP)
            if h:
                wait(pe, "shift", h, g, GROUP)
            else:
                wait(pe, "context", 0, g, 1)
            for t in range(TT):
                last = pe.transpose(turned[0:65, t // 4, t % 4 * P:(t % 4 + 1) * P], peaks[:, h, t:t + 65], k.ident[:])
            inc("turned", last)

        def tensor_group(pe, g, r):
            wait(pe, LOADED[r], LOADS - r * LOADS // 2, g, LOADS // 2)
            fill(pe, g, r)
            wait(pe, "shift", GROUP, g, GROUP)
            for j in range(TT + 1):
                if j < TT:
                    for h in range(GROUP):
                        n = GROUP * j + h
                        if n >= 2:
                            wait(pe, "expd", n - 1, g, ITEMS)
                        else:
                            wait(pe, "peak", ITEMS, g, ITEMS)
                        width = TOKENS - j * P
                        for a, b in pieces(0, width):
                            last = pe.matmul(spread[n % 2][:, a:b], keys[r][:, h, j * P:(j + 1) * P],
                                             queries[r][:, h, j * P + a:j * P + b], start=True, stop=a > 0)
                            if a == 0:
                                last = pe.matmul(spread[n % 2][:, 0:P], ident[:], mask[:, 1, :], start=False, stop=True)
                        inc("score", last)
                if j:
                    add(pe, g, r, j - 1)
            wait(pe, "kept", 1, g, 1)
            for t in range(TT):
                last = pe.transpose(turned[:, t // 4, t % 4 * P:(t % 4 + 1) * P], out_sb[:, t * P:(t + 1) * P],
                                    k.ident[:])
            inc("back", last)

        def add(pe, g, r, j):
            wait(pe, "expd", GROUP * (j + 1), g, ITEMS)
            if j == 0:
                wait(pe, "kept", 0, g, 1)
                wait(pe, "grouped", 1, g, 1)
            for a, b in pieces(j * P, TOKENS):
                for h in range(GROUP):
                    last = pe.matmul(out[32 * h:32 * h + 32, a // 512, a % 512:(b - 1) % 512 + 1],
                                     value[:, j, r, 32 * h:32 * h + 32], probs[:, j % 2, h, a - j * P:b - j * P],
                                     start=j == 0, stop=j == (3 if a < 512 else TT - 1))
            inc("added", last)

        def scalar_group(act, g, r):
            for h in range(GROUP):
                wait(act, "turned", h + 1, g, GROUP)
                inc("shift", act.activation(queries[r][64:65, h, :].rearrange("p (b c) -> p b c", b=2),
                                            turned[64:65], ACT.Copy))
            for n in range(ITEMS):
                j, h = n // GROUP, n % GROUP
                wait(act, "score", n + 1, g, ITEMS)
                if h == 0:
                    wait(act, "added", max(j - 1, 0), g, TT)
                width = TOKENS - j * P
                inc("expd", act.activation(probs[:, j % 2, h, 0:width], spread[n % 2][:, 0:width], ACT.Exp))
            wait(act, "added", TT, g, TT)
            wait(act, "back", 0, g, 1)
            inc("kept", act.activation(out_sb[:].rearrange("p (b c) -> p b c", b=2), out, ACT.Copy))

        def vector_group(v, g, r):
            for n in range(ITEMS):
                h, t = n // TT, n % TT
                wait(v, "fill", n + 1, g, ITEMS)
                if n == 0:
                    wait(v, "turned", 0, g, GROUP)
                inc("peak", v.reduce_max(peaks[:, h, 64 + t:65 + t], spread[n % 2][:, 0:(t + 1) * P], axis=AX))
                if t == TT - 1:
                    wait(v, "peak", n + 1, g, ITEMS)
                    inc("negated", v.tensor_scalar(peaks[:, h, 64:64 + TT], peaks[:, h, 64:64 + TT], -1.0, None,
                                                   ALU.mult))
            wait(v, "back", 1, g, 1)
            rows = turned.rearrange("p b (t h c) -> p (b t) h c", t=4, h=GROUP)
            inc("inverted", v.reciprocal(inverse[:], rows[:, :, :, HD0]))
            wait(v, "inverted", 1, g, 1)
            inc("context", v.tensor_tensor(
                context[:, :, ds(g * GROUP * HD0, GROUP * HD0)].rearrange("p t (h c) -> p t h c", h=GROUP),
                rows[:, :, :, 0:HD0], inverse[:].unsqueeze(3).to_broadcast([P, TT, GROUP, HD0]), ALU.mult))

        def pool_group(pool, g, r):
            wait(pool, "added", 0, g, TT)
            inc("grouped", pool.tensor_copy(value[:, :, r, :], values[:, :, ds(g * GROUP * 32, GROUP * 32)]))

        def groups(engine, part):
            with engine.Fori(0, NG // 2) as i:
                for r in range(2):
                    part(engine, i * 2 + r, r)

        with nc.Block() as block:
            @block.sync
            def _(sp):
                for g in range(NG):
                    load(sp, g)

            @block.tensor
            def _(pe):
                groups(pe, tensor_group)

            @block.scalar
            def _(act):
                groups(act, scalar_group)

            @block.vector
            def _(v):
                groups(v, vector_group)

            @block.gpsimd
            def _(pool):
                groups(pool, pool_group)



def route(k, xt, xtT, router, weights, scatter, gather):
    nc = k.nc
    with ExitStack() as ctx:
        sb = lambda name, shape, dtype=F32: k.sb(name, shape, dtype, ctx=ctx)
        logits = sb("logits", [P, TT, E0])
        best = sb("best", [P, TT, 8])
        place = sb("best_place", [P, TT, 8], U32)
        placef = sb("best_placef", [P, TT, 2])
        probs = sb("router_probs", [P, TT, E0])
        total = sb("router_total", [P, TT, 1])
        chosen = sb("chosen", [P, TT, 2 * E0])
        before = sb("chosen_before", [P, TT + 1, 2 * E0])
        location = sb("location", [P, TT, 2 * E0])
        product = sb("route_product", [P, TT, 2 * E0])
        kept = sb("kept", [P, TT, 2])
        slot = sb("slot", [P, TT, 2])
        spare = sb("spare", [P, TT, 2])
        expert = sb("expert_number", [P, E0])
        upper = sb("upper", [P, P])
        made, ready = k.sig("route_constants"), k.sig("route_counted")
        exp_s = k.sig("route_exponential")

        with nc.Block() as block:
            @block.gpsimd
            def _(pool):
                pool.iota(expert[:], [[1, E0]], base=0, channel_multiplier=0,
                          allow_small_or_imprecise_dtypes=True).then_inc(made.sem, 1)
                pool.iota(spare[:], [[2 * P, TT], [1, 2]], base=E0 * CAP, channel_multiplier=2,
                          allow_small_or_imprecise_dtypes=True).then_inc(made.sem, 1)
                pool.memset(upper[:], 1.0).then_inc(made.sem, 1)
                pool.wait_ge(made.sem, made.at(3))
                pool.affine_select(out=upper[:], in_=upper[:], compare_op=ALU.is_ge, fill=0.0, base=0,
                                   pattern=[[1, P]], channel_multiplier=-1).then_inc(made.sem, 1)
                pool.wait_ge(made.sem, made.at(4))

            @block.tensor
            def _(pe):
                for t in range(TT):
                    pe.matmul(k.ps[:, 0, t * E0:(t + 1) * E0], xtT[:, t * P:(t + 1) * P], router[:], start=True,
                              stop=True).then_inc(ready.sem, 1)

            @block.vector
            def _(v):
                v.wait_ge(ready.sem, ready.at(TT))
                keep(k, v, v.tensor_copy(logits[:].rearrange("p t e -> p (t e)"), k.ps[:, 0, 0:TT * E0]))
                for t in range(TT):
                    keep(k, v, v.max(best[:, t, :], logits[:, t, :]))
                    keep(k, v, v.max_index(place[:, t, :], best[:, t, :], logits[:, t, :]))
                keep(k, v, v.tensor_copy(placef[:], place[:, :, 0:2]))
                keep(k, v, v.tensor_tensor(probs[:], logits[:], best[:, :, 0:1].to_broadcast([P, TT, E0]),
                                           ALU.subtract))
        made.total += 4
        ready.total += TT

        with nc.Block() as block:
            @block.scalar
            def _(act):
                act.activation(probs[:], probs[:], ACT.Exp).then_inc(exp_s.sem, 1)

            @block.vector
            def _(v):
                for n in range(2):
                    keep(k, v, v.tensor_tensor(chosen[:, :, n * E0:(n + 1) * E0],
                                               expert[:].unsqueeze(1).to_broadcast([P, TT, E0]),
                                               placef[:, :, n:n + 1].to_broadcast([P, TT, E0]), ALU.is_equal))
                keep(k, v, v.memset(before[:, 0, :], 0.0))
                for t in range(TT):
                    keep(k, v, v.tensor_tensor(before[:, t + 1, :], before[:, t, :], chosen[:, t, :], ALU.add))
                keep(k, v, v.tensor_tensor(before[:, 0:TT, E0:2 * E0], before[:, 0:TT, E0:2 * E0],
                                           before[:, TT:TT + 1, 0:E0].to_broadcast([P, TT, E0]), ALU.add))
                v.wait_ge(exp_s.sem, exp_s.at(1))
                keep(k, v, v.reduce_sum(total[:].squeeze(2), probs[:], axis=AX))
                keep(k, v, v.reciprocal(total[:], total[:]))
                keep(k, v, v.tensor_tensor(probs[:], probs[:], total[:].to_broadcast([P, TT, E0]), ALU.mult))
        exp_s.total += 1

        with nc.Block() as block:
            @block.tensor
            def _(pe):
                pe.matmul(k.ps[:, 1, 0:TT * 2 * E0], upper[:], chosen[:].rearrange("p t e -> p (t e)"), start=True,
                          stop=False)
                pe.matmul(k.ps[:, 1, 0:TT * 2 * E0], k.ones[:], before[:, 0:TT, :].rearrange("p t e -> p (t e)"),
                          start=False, stop=True).then_inc(ready.sem, 1)

            @block.vector
            def _(v):
                both = lambda tile: tile[:].rearrange("p t (n e) -> p t n e", n=2)
                v.wait_ge(ready.sem, ready.at(1))
                keep(k, v, v.tensor_scalar(location[:].rearrange("p t e -> p (t e)"), k.ps[:, 1, 0:TT * 2 * E0], -1.0,
                                           None, ALU.add))
                keep(k, v, v.scalar_tensor_tensor(out=chosen[:].rearrange("p t e -> p (t e)"),
                                                  in0=location[:].rearrange("p t e -> p (t e)"), scalar=float(CAP),
                                                  in1=chosen[:].rearrange("p t e -> p (t e)"), op0=ALU.is_lt,
                                                  op1=ALU.mult))
                keep(k, v, v.tensor_tensor(product[:], location[:], chosen[:], ALU.mult))
                keep(k, v, v.reduce_sum(slot[:], both(product), axis=AX))
                keep(k, v, v.reduce_sum(kept[:], both(chosen), axis=AX))
                for n in range(2):
                    keep(k, v, v.tensor_tensor(product[:, :, n * E0:(n + 1) * E0], probs[:],
                                               chosen[:, :, n * E0:(n + 1) * E0], ALU.mult))
                keep(k, v, v.reduce_sum(weights[:], both(product), axis=AX))
                keep(k, v, v.tensor_tensor(total[:], weights[:, :, 0:1], weights[:, :, 1:2], ALU.add))
                keep(k, v, v.tensor_scalar(total[:], total[:], float(2.0 ** -23), None, ALU.max))
                keep(k, v, v.reciprocal(total[:], total[:]))
                keep(k, v, v.tensor_tensor(weights[:], weights[:], total[:].to_broadcast([P, TT, 2]), ALU.mult))
                flat = lambda tile: tile[:].rearrange("p t n -> p (t n)")
                keep(k, v, v.scalar_tensor_tensor(out=flat(slot), in0=flat(placef), scalar=float(CAP), in1=flat(slot),
                                                  op0=ALU.mult, op1=ALU.add))
                keep(k, v, v.tensor_tensor(slot[:], slot[:], kept[:], ALU.mult))
                keep(k, v, v.tensor_copy(gather[:], slot[:]))
                keep(k, v, v.tensor_scalar(kept[:], kept[:], -1.0, 1.0, ALU.mult, ALU.add))
                keep(k, v, v.tensor_tensor(spare[:], spare[:], kept[:], ALU.mult))
                keep(k, v, v.tensor_tensor(slot[:], slot[:], spare[:], ALU.add))
                keep(k, v, v.tensor_copy(scatter[:], slot[:]))
        ready.total += 1


def sixteen_experts(k, A, xt, weights, scatter, gather, back):
    nc = k.nc
    sent = nc.dram_tensor("experts_in", [E0 * CAP + 2 * TOKENS, D], F32, kind="Internal").ap()
    got = nc.dram_tensor("experts_out", [E0 * CAP, D], F32, kind="Internal").ap()
    S = {name: k.sig("expert_" + name) for name in (
        "zeroed", "sent", "loaded_even", "loaded_odd", "turned", "input", "up", "gelu", "down", "biased", "scaled", "stored_even", "stored_odd", "back")}
    LOADED, LOADS = ("loaded_even", "loaded_odd"), 4 * 16
    STORED = ("stored_even", "stored_odd")
    with ExitStack() as ctx:
        zeros = k.sb("expert_zeros", [P, E0 * CAP * D // P], ctx=ctx)
        rows = k.sb("expert_rows", [P, 2, D], ctx=ctx)
        inputs = k.sb("expert_input", [P, 2, P], ctx=ctx)
        w1 = k.sb("expert_w1", [P, 2, F0], ctx=ctx)
        w2 = k.sb("expert_w2", [P, 2, FB0, D], ctx=ctx)
        b2 = k.sb("expert_b2", [P, 2, D], ctx=ctx)
        hidden = k.sb("expert_hidden", [P, 2, FB0, P], ctx=ctx)
        biased = k.sb("expert_biased", [P, 2, D], ctx=ctx)
        result = k.sb("expert_result", [P, 2, D], ctx=ctx)
        with nc.Block() as block:
            @block.vector
            def _(v):
                keep(k, v, v.memset(zeros[:], 0.0))
        with nc.Block() as block:
            @block.sync
            def _(sp):
                sp.dma_start(sent[0:E0 * CAP, :].rearrange("(p r) d -> p (r d)", p=P), zeros[:]) \
                  .then_inc(S["zeroed"].sem, 16)
                sp.wait_ge(S["zeroed"].sem, 16)

            @block.gpsimd
            def _(pool):
                pool.wait_ge(S["zeroed"].sem, 16)
                for t in range(TT):
                    for n in range(2):
                        pool.indirect_dma_start(
                            out=sent, out_offset=bass.IndirectOffsetOnAxis(ap=scatter[:, t, n:n + 1], axis=0),
                            in_=xt[:, t, :], in_offset=None).then_inc(S["sent"].sem, 16)
                pool.wait_ge(S["sent"].sem, 2 * TT * 16)

        def at(name, e, n, per=1):
            return S[name].at(n) + e * per

        def run(engine, step):
            step(engine, 0, 0, True)
            step(engine, 1, 1, True)
            with engine.Fori(1, E0 // 2) as m:
                for r in range(2):
                    step(engine, m * 2 + r, r, False)

        def sync_step(sp, e, r, first):
            if not first:
                sp.wait_ge(S["scaled"].sem, at("scaled", e, -1))
            for tile, source in ((rows[:, r, :], sent[ds(e * CAP, CAP), :]),
                                 (w1[:, r, :], A["fc1"][ds(e, 1)].squeeze(0)),
                                 (w2[:, r], A["fc2"][ds(e, 1)].squeeze(0)),
                                 (b2[:, r, :], A["fc2_b"][ds(e, 1)].squeeze(0).partition_broadcast(P))):
                sp.dma_start(tile, source).then_inc(S[LOADED[r]].sem, 16)

        def tensor_step(pe, e, r, first):
            pe.wait_ge(S[LOADED[r]].sem, at(LOADED[r], e, LOADS - r * LOADS // 2, LOADS // 2))
            pe.transpose(k.ps[:, r, 0:P], rows[:, r, :], k.ident[:]).then_inc(S["turned"].sem, 1)
            pe.wait_ge(S["input"].sem, at("input", e, 1))
            if not first:
                pe.wait_ge(S["gelu"].sem, at("gelu", e, -1))
            for f in range(FB0):
                last = pe.matmul(k.ps[:, 2 + r, f * P:(f + 1) * P], w1[:, r, f * P:(f + 1) * P], inputs[:, r, :],
                                 start=True, stop=True)
            last.then_inc(S["up"].sem, 1)
            pe.wait_ge(S["gelu"].sem, at("gelu", e, 1))
            if not first:
                pe.wait_ge(S["biased"].sem, at("biased", e, -1))
            for f in range(FB0):
                last = pe.matmul(k.ps[:, 4 + r, 0:D], hidden[:, r, f, :], w2[:, r, f, :], start=f == 0,
                                 stop=f == FB0 - 1)
            last.then_inc(S["down"].sem, 1)

        def vector_step(v, e, r, first):
            v.wait_ge(S["turned"].sem, at("turned", e, 1))
            v.tensor_copy(inputs[:, r, :], k.ps[:, r, 0:P]).then_inc(S["input"].sem, 1)
            v.wait_ge(S["down"].sem, at("down", e, 1))
            v.tensor_tensor(biased[:, r, :], k.ps[:, 4 + r, 0:D], b2[:, r, :], ALU.add).then_inc(S["biased"].sem, 1)
            v.wait_ge(S["biased"].sem, at("biased", e, 1))
            if not first:
                v.wait_ge(S[STORED[r]].sem, at(STORED[r], e, -8 * r, 8))
            v.tensor_scalar(result[:, r, :], biased[:, r, :], KEEP, None, ALU.mult).then_inc(S["scaled"].sem, 1)

        def scalar_step(act, e, r, first):
            act.wait_ge(S["up"].sem, at("up", e, 1))
            for f in range(FB0):
                last = act.activation(hidden[:, r, f, :], k.ps[:, 2 + r, f * P:(f + 1) * P], ACT.Gelu,
                                      bias=k.cols[:, ds(e * FB0 + sum(COL_N[:-1]) + f, 1)])
            last.then_inc(S["gelu"].sem, 1)

        def pool_step(pool, e, r, first):
            pool.wait_ge(S["scaled"].sem, at("scaled", e, 1))
            pool.dma_start(got[ds(e * CAP, CAP), :], result[:, r, :]).then_inc(S[STORED[r]].sem, 16)

        with nc.Block() as block:
            @block.sync
            def _(sp):
                run(sp, sync_step)

            @block.tensor
            def _(pe):
                run(pe, tensor_step)

            @block.vector
            def _(v):
                run(v, vector_step)

            @block.scalar
            def _(act):
                run(act, scalar_step)

            @block.gpsimd
            def _(pool):
                run(pool, pool_step)
                for name in STORED:
                    pool.wait_ge(S[name].sem, 16 * E0 // 2)
                for t in range(TT):
                    for n in range(2):
                        pool.indirect_dma_start(
                            out=back[:, t, n, :], out_offset=None, in_=got,
                            in_offset=bass.IndirectOffsetOnAxis(ap=gather[:, t, n:n + 1], axis=0)) \
                            .then_inc(S["back"].sem, 16)
                pool.wait_ge(S["back"].sem, 2 * TT * 16)


def causal_layer(k, A):
    with ExitStack() as outer:
        hidden = k.sb("hidden", [P, TT, D], ctx=outer)
        normed = k.sb("hidden_normed", [P, TT, D], ctx=outer)
        turned = k.sb("hidden_turned", [P, TOKENS], ctx=outer)
        layernorm_rows(k, k.x[:], hidden[:])
        layernorm_rows(k, hidden[:], normed[:])
        transpose_rows(k, normed, turned, k.col("L0_ffn_ln1_w"), k.col("L0_ffn_ln1_b"))
        with ExitStack() as ctx:
            values = k.sb("values_by_head", [P, TT, H0 * 32], ctx=ctx)
            context = k.sb("attention_context", [P, TT, D], ctx=ctx)
            with k.nc.Block() as block:
                @block.vector
                def _(v):
                    keep(k, v, v.memset(values[:], 0.0))
                    keep(k, v, v.memset(values[:].rearrange("p t (h c) -> p t h c", h=H0)[:, :, :, HD0:HD0 + 1], 1.0))

            def take_values(v, rows):
                to = values[:].rearrange("p t (h c) -> p t h c", h=H0)
                for t in range(TT):
                    keep(k, v, v.tensor_tensor(to[:, t, :, 0:HD0], rows[:, t, :].rearrange("p (h c) -> p h c", h=H0),
                                               k.row("L0_ffn_v_b").rearrange("p (h c) -> p h c", h=H0), ALU.add))
            project_rows(k, turned, k.square("L0_ffn_v_w"), take_values)
            causal_attention(k, turned, values, context)
            transpose_rows(k, context, turned)

        def take_output(v, rows):
            keep(k, v, v.tensor_tensor(hidden[:], hidden[:], rows, ALU.add))
            keep(k, v, v.tensor_tensor(hidden[:], hidden[:], k.row_of_tiles("L0_ffn_o_b", TT), ALU.add))
        project_rows(k, turned, k.square("L0_ffn_o_w"), take_output)
        layernorm_rows(k, hidden[:], normed[:], gain=k.row("L0_ffn_ln2_w"), shift=k.row("L0_ffn_ln2_b"))
        transpose_rows(k, normed, turned)
        with ExitStack() as ctx:
            weights = k.sb("expert_weights", [P, TT, 2], ctx=ctx)
            scatter = k.sb("scatter_rows", [P, TT, 2], U32, ctx=ctx)
            gather = k.sb("gather_rows", [P, TT, 2], U32, ctx=ctx)
            router = k.sb("router", [P, E0], ctx=ctx)
            back = k.sb("experts_back", [P, TT, 2, D], ctx=ctx)
            loaded = k.sig("router_loaded")
            with k.nc.Block() as block:
                @block.sync
                def _(sp):
                    sp.dma_start(router[:], A["router0"]).then_inc(loaded.sem, 16)
                    sp.wait_ge(loaded.sem, 16)
            route(k, normed, turned, router, weights, scatter, gather)
            sixteen_experts(k, A, normed, weights, scatter, gather, back)
            with k.nc.Block() as block:
                @block.vector
                def _(v):
                    over = [P, TT, D]
                    keep(k, v, v.tensor_tensor(k.x[:], k.x[:], hidden[:], ALU.add))
                    for n in range(2):
                        keep(k, v, v.tensor_tensor(normed[:], back[:, :, n, :],
                                                   weights[:, :, n:n + 1].to_broadcast(over), ALU.mult))
                        keep(k, v, v.tensor_tensor(k.x[:], k.x[:], normed[:], ALU.add))



def dense_experts(k, A):
    nc = k.nc
    S = {name: k.sig("dense_" + name) for name in (
        "loaded", "router_up", "router_gelu", "router_down", "up", "gelu", "down", "added", "counted")}
    with ExitStack() as ctx:
        sb = lambda name, shape, dtype=F32: k.sb(name, shape, dtype, ctx=ctx)
        normed = sb("dense_normed", [P, TT, D])
        y = sb("dense_turned", [P, TOKENS])
        rw1 = sb("router_w1", [P, R1])
        rw2 = sb("router_w2", [P, RB1, E1])
        rb2 = sb("router_b2", [P, E1])
        be2 = sb("dense_b2", [E1, D])
        w1 = sb("dense_w1", [P, E1, F1])
        w2 = sb("dense_w2", [P, E1, FB1, D])
        hidden = sb("dense_hidden", [P, 2, FB1, TOKENS])
        logits = sb("dense_logits", [P, TT, 8])
        best = sb("dense_best", [P, TT, 8])
        place = sb("dense_place", [P, TT, 8], U32)
        placef = sb("dense_placef", [P, TT, 2])
        probs = sb("dense_probs", [P, TT, E1])
        total = sb("dense_total", [P, TT, 1])
        chosen = sb("dense_chosen", [P, 2, TT, E1])
        expert = sb("dense_expert", [P, E1])
        weights_t = sb("dense_weights_turned", [E1, TOKENS])
        layernorm_rows(k, k.x[:], normed[:])
        transpose_rows(k, normed, y)
        with nc.Block() as block:
            @block.sync
            def _(sp):
                for tile, source in ((rw1[:], A["rW1"]), (rw2[:], A["rW2"]),
                                     (rb2[:], A["rb2"][0].partition_broadcast(P)), (be2[:], A["be2"]),
                                     (w1[:], A["We1"].rearrange("e d f -> d e f")),
                                     (w2[:], A["We2"].rearrange("e p f d -> p e f d"))):
                    sp.dma_start(tile, source).then_inc(S["loaded"].sem, 16)
                sp.wait_ge(S["loaded"].sem, 96)

            @block.gpsimd
            def _(pool):
                pool.iota(expert[:], [[1, E1]], base=0, channel_multiplier=0,
                          allow_small_or_imprecise_dtypes=True).then_inc(S["counted"].sem, 1)
        with nc.Block() as block:
            @block.tensor
            def _(pe):
                for f in range(RB1):
                    for c in range(2):
                        pe.matmul(k.ps[:, 2 * f + c, :], rw1[:, f * P:(f + 1) * P], y[:, c * 512:(c + 1) * 512],
                                  start=True, stop=True).then_inc(S["router_up"].sem, 1)
                pe.wait_ge(S["router_gelu"].sem, RB1)
                for t in range(TT):
                    for f in range(RB1):
                        last = pe.matmul(k.ps[:, 4, t * E1:(t + 1) * E1], hidden[:, 0, f, t * P:(t + 1) * P],
                                         rw2[:, f, :], start=f == 0, stop=f == RB1 - 1)
                last.then_inc(S["router_down"].sem, 1)

            @block.scalar
            def _(act):
                for f in range(RB1):
                    act.wait_ge(S["router_up"].sem, 2 * f + 2)
                    act.activation(hidden[:, 0, f, :].rearrange("p (b c) -> p b c", b=2), k.ps[:, 2 * f:2 * f + 2, :],
                                   ACT.Gelu, bias=k.col("L1_ffn_rb1", f)).then_inc(S["router_gelu"].sem, 1)

            @block.vector
            def _(v):
                keep(k, v, v.memset(logits[:], NEG))
                v.wait_ge(S["router_down"].sem, 1)
                keep(k, v, v.tensor_tensor(logits[:, :, 0:E1],
                                           k.ps[:, 4, 0:TT * E1].rearrange("p (t e) -> p t e", e=E1),
                                           rb2[:].unsqueeze(1).to_broadcast([P, TT, E1]), ALU.add))
                for t in range(TT):
                    keep(k, v, v.max(best[:, t, :], logits[:, t, :]))
                    keep(k, v, v.max_index(place[:, t, :], best[:, t, :], logits[:, t, :]))
                keep(k, v, v.tensor_copy(placef[:], place[:, :, 0:2]))
                keep(k, v, v.tensor_tensor(probs[:], logits[:, :, 0:E1], best[:, :, 0:1].to_broadcast([P, TT, E1]),
                                           ALU.subtract))
                for n in range(2):
                    keep(k, v, v.tensor_tensor(chosen[:, n], expert[:].unsqueeze(1).to_broadcast([P, TT, E1]),
                                               placef[:, :, n:n + 1].to_broadcast([P, TT, E1]), ALU.is_equal))
                keep(k, v, v.tensor_tensor(chosen[:, 0], chosen[:, 0], chosen[:, 1], ALU.add))
        with nc.Block() as block:
            @block.scalar
            def _(act):
                act.activation(probs[:], probs[:], ACT.Exp).then_inc(S["counted"].sem, 1)

            @block.vector
            def _(v):
                v.wait_ge(S["counted"].sem, 2)
                keep(k, v, v.reduce_sum(total[:].squeeze(2), probs[:], axis=AX))
                keep(k, v, v.reciprocal(total[:], total[:]))
                keep(k, v, v.tensor_tensor(probs[:], probs[:], total[:].to_broadcast([P, TT, E1]), ALU.mult))
                keep(k, v, v.tensor_tensor(probs[:], probs[:], chosen[:, 0], ALU.mult))
        with nc.Block() as block:
            @block.tensor
            def _(pe):
                for t in range(TT):
                    pe.transpose(k.ps[0:E1, t // 4, t % 4 * P:(t % 4 + 1) * P], probs[:, t, :],
                                 k.ident[:]).then_inc(S["down"].sem, 1)

            @block.vector
            def _(v):
                v.wait_ge(S["down"].sem, TT)
                keep(k, v, v.tensor_copy(weights_t[:].rearrange("e (b c) -> e b c", b=2), k.ps[0:E1, 0:2, :]))
        S["down"].total += TT

        def take_bias(v, rows):
            keep(k, v, v.tensor_tensor(k.x[:], k.x[:], rows, ALU.add))
        project_rows(k, weights_t, be2[:], take_bias)

        with nc.Block() as block:
            @block.tensor
            def _(pe):
                def up(e):
                    for f in range(FB1):
                        n = FB1 * e + f
                        if n >= 2:
                            pe.wait_ge(S["gelu"].sem, n - 1)
                        for c in range(2):
                            last = pe.matmul(k.ps[:, 2 * (f % 2) + c, :], w1[:, e, f * P:(f + 1) * P],
                                             y[:, c * 512:(c + 1) * 512], start=True, stop=True)
                        last.then_inc(S["up"].sem, 1)

                def down(e):
                    pe.wait_ge(S["gelu"].sem, FB1 * (e + 1))
                    if e >= 2:
                        pe.wait_ge(S["added"].sem, TT * (e - 1))
                    for t in range(TT):
                        for f in range(FB1):
                            last = pe.matmul(k.ps[:, 4 + 2 * (e % 2) + t // 4, t % 4 * P:(t % 4 + 1) * P],
                                             hidden[:, e % 2, f, t * P:(t + 1) * P], w2[:, e, f, :], start=f == 0,
                                             stop=f == FB1 - 1)
                        if t % 4 == 3:
                            last.then_inc(S["down"].sem, 1)
                up(0)
                for e in range(1, E1):
                    up(e)
                    down(e - 1)
                down(E1 - 1)

            @block.scalar
            def _(act):
                for e in range(E1):
                    for f in range(FB1):
                        act.wait_ge(S["up"].sem, FB1 * e + f + 1)
                        if e >= 2:
                            act.wait_ge(S["down"].sem, S["down"].at(2 * (e - 1)))
                        act.activation(hidden[:, e % 2, f, :].rearrange("p (b c) -> p b c", b=2),
                                       k.ps[:, 2 * (f % 2):2 * (f % 2) + 2, :], ACT.Gelu,
                                       bias=k.col("L1_ffn_be1", e * FB1 + f)).then_inc(S["gelu"].sem, 1)

            @block.vector
            def _(v):
                for e in range(E1):
                    for t in range(TT):
                        v.wait_ge(S["down"].sem, S["down"].at(2 * e + t // 4 + 1))
                        if e:
                            v.wait_ge(S["added"].sem, TT * (e - 1) + t + 1)
                        v.scalar_tensor_tensor(out=k.x[:, t, :],
                                               in0=k.ps[:, 4 + 2 * (e % 2) + t // 4, t % 4 * P:(t % 4 + 1) * P],
                                               scalar=probs[:, t, e:e + 1], in1=k.x[:, t, :], op0=ALU.mult,
                                               op1=ALU.add).then_inc(S["added"].sem, 1)



def latents_turned(k):
    with ExitStack() as ctx:
        normed = k.sb("latents_normed", [P, TT, D], ctx=ctx)
        layernorm_rows(k, k.x[:], normed[:])
        layernorm_rows(k, normed[:], normed[:])
        transpose_rows(k, normed, k.zT[:, LAT0:REST0], k.col("L1_xcond_ln2_w"), k.col("L1_xcond_ln2_b"))
    with k.nc.Block() as block:
        @block.vector
        def _(v):
            modulation, lat = k.stat[:, 0, 0:1], k.zT[:, LAT0:REST0]
            keep(k, v, v.tensor_scalar(modulation, k.col("cond_1024"), 1.0, None, ALU.add))
            keep(k, v, v.tensor_scalar(lat, lat, modulation, k.col("cond_1024"), ALU.mult, ALU.add))
            for part in (k.zT[:, 0:LAT0], k.zT[:, REST0:KEYS]):
                keep(k, v, v.tensor_scalar(part, part, k.col("L1_xcond_ln1_w"), k.col("L1_xcond_ln1_b"),
                                           ALU.mult, ALU.add))


def perceiver_attention(k, A, rows):
    nc = k.nc
    S = {name: k.sig(name) for name in (
        "weights", "staged", "vsource", "kproj", "khigh", "klow", "vproj", "vready", "vodd",
        "score", "expd", "pv", "counted", "fill", "peak", "qproj", "qhigh", "qlow", "peaked", "shifted",
        "shift_row", "totals", "denominators", "inverted", "normed", "output", "summed")}
    per = {name: n * STEPS for name, n in (
        ("staged", 2), ("kproj", 1), ("khigh", 1), ("klow", 1), ("vready", 1), ("score", 4), ("expd", 4),
        ("pv", 2), ("counted", 2), ("fill", 4), ("peak", 4))}

    with ExitStack() as ctx:
        keys = [k.sb("keys", [P, STEPS * STEP], F32R, ctx=ctx) for _ in range(2)]
        key_a = k.sb("key_high_low", [P, 2, STEP], F32R, ctx=ctx)
        key_b = k.sb("key_high_one", [P, 2, STEP], F32R, ctx=ctx)
        source = k.sb("value_source", [P, 2, STEP], ctx=ctx)
        value = k.sb("value_step", [P, 2, 2, HD1], ctx=ctx)
        value_odd = k.sb("value_odd_head", [P, STEPS, 2 * HD1], ctx=ctx)
        q_a = [k.sb("query_high_high", [P, TOKENS], F32R, ctx=ctx) for _ in range(2)]
        q_b = [k.sb("query_low_shift", [P, TOKENS], F32R, ctx=ctx) for _ in range(2)]
        probs = k.sb("probs", [P, 4, 512], ctx=ctx)
        total = k.sb("probs_total", [P, 4, 512], ctx=ctx)
        inverse = k.sb("inverse_total", [P, 2, 512], ctx=ctx)
        head = k.sb("head_normed", [P, 2, 512], ctx=ctx)
        peaks = k.sb("peaks", [P, TT, STEPS], ctx=ctx)
        peak = k.sb("peak_columns", [P, 64 + TT], ctx=ctx)
        wq = k.sb("wq", [P, 2, P], ctx=ctx)
        wk = k.sb("wk", [P, 2, P], ctx=ctx)
        wo = k.sb("wo", [P, 2, P], ctx=ctx)
        wv = k.sb("wv", [P, P], ctx=ctx)
        scores = k.ps[:, 0:2, :]
        out = k.ps[:, 2:4, :]
        fills = k.ps[:, 4:6, :]
        kbank, vbank = k.ps[:, 6, :], k.ps[:, 7, :]
        latents = k.zT[:, LAT0:REST0]

        cleared = k.sig("cleared")
        with nc.Block() as block:
            @block.vector
            def _(v):
                v.memset(key_b[:].bitcast(F32), 0.0).then_inc(cleared.sem, 1)
                v.memset(key_a[:].bitcast(F32), 0.0).then_inc(cleared.sem, 1)
                v.memset(peak[:], 0.0).then_inc(cleared.sem, 1)
                for q in q_b:
                    v.memset(q[:].bitcast(F32), 0.0).then_inc(cleared.sem, 1)
                v.wait_ge(cleared.sem, cleared.at(5))
                v.memset(key_b[64:65].bitcast(F32), 1.0).then_inc(cleared.sem, 1)
                for tile in keys:
                    v.memset(tile[:, KEYS:STEPS * STEP].bitcast(F32), 0.0).then_inc(cleared.sem, 1)
                v.memset(value_odd[:, NS, :], 0.0).then_inc(cleared.sem, 1)
                v.wait_ge(cleared.sem, cleared.at(9))
                v.sem_inc(S["score"].sem, 4)
        cleared.total += 9
        S["score"].total += 4

        def at(name, h, j, n):
            return S[name].at(n) + h * per[name] + j * (per[name] // STEPS)

        def inc(name, instruction):
            instruction.then_inc(S[name].sem, 1)

        def wait(engine, name, value):
            engine.wait_ge(S[name].sem, value)

        def width(j):
            return (LAST if isinstance(j, int) and j == NS else STEP)


        def stage_keys(pool, h, hp, j, r):
            wait(pool, "score", at("score", h, j, -4))
            for rows_, tile in ((slice(0, P), key_a), (slice(0, HD1), key_b)):
                inc("staged", pool.tensor_copy(tile[rows_, r, :], keys[hp][rows_, ds(j * STEP, STEP)]))

        def stage_odd_value(pool, h, j, r):
            wait(pool, "pv", at("pv", h, j, -2))
            inc("vready", pool.tensor_copy(value[:, r].rearrange("p a d -> p (a d)"),
                                           value_odd[:, ds(j, 1), :].squeeze(1)))

        def stage_source(act, pair, j, r, first=False):
            w = width(j)
            if not first:
                wait(act, "vproj", S["vproj"].at(-1) + pair * STEPS + j)
            inc("vsource", act.activation(source[:, r, 0:w], k.zT[:, ds(j * STEP, w)], ACT.Copy))

        def keep_values(act, pair, h, j, r, first=False):
            rows_ = width(j) // 2
            made = vbank[0:rows_, 0:2 * P].rearrange("p (a h d) -> p a h d", a=2, h=2)
            wait(act, "vproj", S["vproj"].at(1) + pair * STEPS + j)
            if not first:
                wait(act, "pv", at("pv", h, j, -2))
            inc("vready", act.activation(value[0:rows_, r], made[:, :, 0, :], ACT.Copy))
            inc("vodd", act.activation(value_odd[0:rows_, ds(j, 1), :].rearrange("p o (a d) -> p (o a) d", a=2),
                                       made[:, :, 1, :], ACT.Copy))

        def make_values(pe, pair, j, r, first=False):
            rows_ = width(j) // 2
            wait(pe, "vsource", S["vsource"].at(1) + pair * STEPS + j)
            if not first:
                wait(pe, "vodd", S["vodd"].at(0) + pair * STEPS + j)
            for a in range(2):
                last = pe.matmul(vbank[0:rows_, a * P:(a + 1) * P], source[:, r, a * rows_:(a + 1) * rows_], wv[:],
                                 start=True, stop=True)
            inc("vproj", last)

        def make_scores(pe, h, hp, j, r, c, first):
            rows_ = width(j) // 2
            wait(pe, "staged", at("staged", h, j, 2))
            for a in range(2):
                if not first or c:
                    wait(pe, "expd", at("expd", h, j, 2 * c + a - 1))
                cols = slice(c * 512, (c + 1) * 512)
                tile = slice(a * rows_, a * rows_ + P) if rows_ < P else slice(a * P, (a + 1) * P)
                pe.matmul(scores[:, a, :], key_a[:, r, tile], q_a[hp][:, cols], start=True, stop=False)
                inc("score", pe.matmul(scores[:, a, :], key_b[:, r, tile], q_b[hp][:, cols], start=False, stop=True))

        def add_products(pe, h, j, r, c, first, final):
            rows_ = width(j) // 2
            wait(pe, "vready", at("vready", h, j, 1))
            wait(pe, "expd", at("expd", h, j, 2 * c + 2))
            for a in range(2):
                last = pe.matmul(out[a * HD1:(a + 1) * HD1, c, :], value[0:rows_, r, a, :], probs[0:rows_, 2 * c + a, :],
                                 start=first, stop=final)
            inc("pv", last)

        def fill_peaks(pe, g, gp, j, part, first):
            w = width(j)
            if part == 0:
                wait(pe, "khigh", at("khigh", g, j, 1))
                wait(pe, "klow", at("klow", g, j, 1))
            for b in range(2):
                if not first or part:
                    wait(pe, "peak", at("peak", g, j, 2 * part + b - 1))
                for n in range(2):
                    t = 4 * part + 2 * b + n
                    last = pe.matmul(fills[:, b, n * STEP:n * STEP + w], q_a[gp][:, t * P:(t + 1) * P],
                                     keys[gp][:, ds(j * STEP, w)], start=True, stop=True)
                inc("fill", last)

        def make_keys(pe, g, gp, j, first):
            w = width(j)
            if not first:
                wait(pe, "khigh", at("khigh", g, j, 0))
                wait(pe, "klow", at("klow", g, j, 0))
            inc("kproj", pe.matmul(kbank[:, 0:w], wk[:, gp, :], k.zT[:, ds(j * STEP, w)], start=True, stop=True))

        def tensor_step(pe, pair, h, hp, g, gp, j, r, first=False):
            final = width(j) == LAST
            for c in range(2):
                if h is not None:
                    make_scores(pe, h, hp, j, r, c, first)
                    if c:
                        add_products(pe, h, j, r, 0, first, final)
                    elif not first:
                        add_products(pe, h, j - 1, 1 - r, 1, isinstance(j, int) and j == 1, False)
                if g is not None and not first:
                    fill_peaks(pe, g, gp, j - 1, c, isinstance(j, int) and j == 1)
            if g is not None:
                make_keys(pe, g, gp, j, first)
            if h is not None and hp == 0 and not final:
                make_values(pe, pair, j + 1, 1 - r)

        def scalar_step(act, pair, h, hp, g, gp, j, r, first=False):
            final = width(j) == LAST
            rows_ = width(j) // 2
            if h is not None:
                if hp == 0 and not final:
                    stage_source(act, pair, j + 1, 1 - r, first)
                for c in range(2):
                    for a in range(2):
                        wait(act, "score", at("score", h, j, 2 * c + a + 1))
                        if not first:
                            wait(act, "pv", at("pv", h, j, c - 1))
                            wait(act, "counted", at("counted", h, j, c - 1))
                        inc("expd", act.activation(probs[0:rows_, 2 * c + a, :], scores[0:rows_, a, :], ACT.Exp,
                                                   scale=1.0 / 8.0))
            if g is not None:
                w = width(j)
                wait(act, "kproj", at("kproj", g, j, 1))
                inc("khigh", act.activation(keys[gp][:, ds(j * STEP, w)], kbank[:, 0:w], ACT.Copy))
            if h is not None and hp == 0 and not final:
                keep_values(act, pair, h, j + 1, 1 - r, first)

        def vector_step(v, h, hp, g, gp, j, r, first=False):
            w = width(j)
            if g is not None and not first:
                for f in range(2):
                    read_peak(v, g, j - 1, f)
            if h is not None:
                count(v, h, j, 0, w // 2, first)
            if g is not None and not first:
                for f in range(2, 4):
                    read_peak(v, g, j - 1, f)
            if h is not None:
                count(v, h, j, 1, w // 2, first)
            if g is not None:
                low = keys[gp][HD1:P, ds(j * STEP, w)]
                wait(v, "khigh", at("khigh", g, j, 1))
                inc("klow", v.tensor_tensor(low, kbank[HD1:P, 0:w], low.bitcast(F32), ALU.subtract))

        def read_peak(v, g, j, f):
            w = width(j)
            wait(v, "fill", at("fill", g, j, f + 1))
            inc("peak", v.reduce_max(peaks[:, 2 * f:2 * f + 2, ds(j, 1)].rearrange("p t o -> p (t o)"),
                                     fills[:, f % 2, :].rearrange("p (n w) -> p n w", n=2)[:, :, 0:w], axis=AX))

        def count(v, h, j, c, rows_, first):
            wait(v, "expd", at("expd", h, j, 2 * c + 2))
            units = slice(2 * c, 2 * c + 2)
            if first:
                inc("counted", v.tensor_copy(total[:, units, :], probs[:, units, :]))
            else:
                wait(v, "counted", at("counted", h, j, c - 1))
                inc("counted", v.tensor_tensor(total[0:rows_, units, :], total[0:rows_, units, :],
                                               probs[0:rows_, units, :], ALU.add))


        def load_weights(sp, h, slot, pair=None):
            if pair is not None:
                sp.dma_start(wv[:], A["wv"][ds(pair, 1)].squeeze(0)).then_inc(S["weights"].sem, 16)
            for tile, name in ((wq, "wq"), (wk, "wk"), (wo, "wo")):
                sp.dma_start(tile[:, slot, :], A[name][ds(h, 1)].squeeze(0)).then_inc(S["weights"].sem, 16)

        def tensor_between(pe, pair, h, hp, g, gp, n):
            if h is not None:
                add_products(pe, h, NS, NS % 2, 1, False, True)
            if g is not None:
                for part in range(2):
                    fill_peaks(pe, g, gp, NS, part, False)
            if h is not None:
                wait(pe, "totals", S["totals"].at(2) + n * 2)
                if g is not None:
                    wait(pe, "klow", at("klow", g, NS, 1))
                if hp == 0:
                    wait(pe, "vodd", S["vodd"].at(STEPS) + pair * STEPS)
                for c in range(2):
                    last = pe.matmul(k.ps[:, 6 + c, :], k.ones[:], total[:, 2 * c, :], start=True, stop=True)
                inc("denominators", last)
            if g is not None:
                wait(pe, "peaked", S["peaked"].at(2) + g * 2)
                for t in range(TT):
                    last = pe.transpose(fills[0:65, t // 4, t % 4 * P:(t % 4 + 1) * P], peak[:, t:t + 65], k.ident[:])
                inc("shifted", last)
            if h is not None:
                wait(pe, "normed", S["normed"].at(1) + n)
                for t in range(TT):
                    last = pe.matmul(k.ps[:, 6 + t // 4, t % 4 * P:(t % 4 + 1) * P],
                                     head[:, t // 4, t % 4 * P:(t % 4 + 1) * P], wo[:, hp, :], start=True, stop=True)
                inc("output", last)

        def scalar_between(act, h, hp, g, gp, n):
            if g is not None:
                wait(act, "shifted", S["shifted"].at(1) + g)
                inc("shift_row", act.activation(q_b[gp][64:65, :], fills[64:65].rearrange("p b c -> p (b c)"), ACT.Copy))

        def vector_between(v, h, hp, g, gp, n):
            if h is not None:
                for c in range(2):
                    wait(v, "counted", at("counted", h, NS, c + 1))
                    inc("totals", v.tensor_tensor(total[:, 2 * c, :], total[:, 2 * c, :], total[:, 2 * c + 1, :],
                                                  ALU.add))
            if g is not None:
                for f in range(4):
                    read_peak(v, g, NS, f)
                wait(v, "peak", at("peak", g, NS, 4))
                inc("peaked", v.reduce_max(peak[:, 64:64 + TT], peaks[:], axis=AX))
                wait(v, "peaked", S["peaked"].at(1) + g * 2)
                inc("peaked", v.tensor_scalar(peak[:, 64:64 + TT], peak[:, 64:64 + TT], -1.0, None, ALU.mult))
            if h is not None:
                wait(v, "denominators", S["denominators"].at(1) + n)
                inc("inverted", v.reciprocal(inverse[:], k.ps[:, 6:8, :]))
                wait(v, "inverted", S["inverted"].at(1) + n)
                wait(v, "pv", at("pv", h, NS, 2))
                inc("normed", v.tensor_tensor(head[:], out, inverse[:], ALU.mult))
                wait(v, "output", S["output"].at(1) + n)
                wait(v, "summed", S["summed"].at(0) + n)
                inc("summed", v.tensor_tensor(rows[:], rows[:],
                                              k.ps[:, 6:8, :].rearrange("p b (t d) -> p (b t) d", d=D), ALU.add))

        def tensor_queries(pe, h, hp, weights):
            wait(pe, "weights", weights)
            for c in range(2):
                last = pe.matmul(fills[:, c, :], wq[:, hp, :], latents[:, c * 512:(c + 1) * 512], start=True, stop=True)
            inc("qproj", last)

        def scalar_queries(act, h, hp):
            wait(act, "qproj", S["qproj"].at(1) + h)
            inc("qhigh", act.activation(q_a[hp][:].rearrange("p (b c) -> p b c", b=2), fills, ACT.Copy))

        def vector_queries(v, h, hp):
            wait(v, "qhigh", S["qhigh"].at(1) + h)
            inc("qlow", v.tensor_tensor(q_b[hp][0:HD1, :].rearrange("p (b c) -> p b c", b=2), fills[0:HD1],
                                        q_a[hp][0:HD1, :].rearrange("p (b c) -> p b c", b=2).bitcast(F32),
                                        ALU.subtract))

        PAIRS = H1 // 2
        WEIGHTS_FIRST, WEIGHTS_EVEN, WEIGHTS_ODD = 7 * 16, 3 * 16, 4 * 16

        def run(engine, head_part):
            head_part(engine, None, None, 1, 0, 0, 0)
            with engine.Fori(0, PAIRS - 1) as i:
                head_part(engine, i, i * 2, 0, i * 2 + 1, 1, i * 2)
                head_part(engine, i, i * 2 + 1, 1, i * 2 + 2, 0, i * 2 + 1)
            n = H1 - 2
            head_part(engine, PAIRS - 1, n, 0, n + 1, 1, n)
            head_part(engine, PAIRS - 1, n + 1, 1, None, 0, n + 1)

        def steps(engine, step):
            step(0, 0, True)
            step(1, 1, False)
            with engine.Fori(1, NS // 2) as m:
                step(m * 2, 0, False)
                step(m * 2 + 1, 1, False)
            step(NS - 1, 0, False)
            step(NS, 1, False)

        with nc.Block() as block:
            @block.sync
            def _(sp):
                def part(sp, pair, h, hp, g, gp, n):
                    if h is None:
                        load_weights(sp, 0, 0, 0)
                        load_weights(sp, 1, 1)
                        return
                    if g is None:
                        return
                    wait(sp, "output", S["output"].at(1) + n)
                    if hp == 0:
                        load_weights(sp, h + 2, hp)
                    else:
                        load_weights(sp, h + 2, hp, pair + 1)
                part(sp, None, None, 1, 0, 0, 0)
                with sp.Fori(0, PAIRS - 1) as i:
                    part(sp, i, i * 2, 0, i * 2 + 1, 1, i * 2)
                    part(sp, i, i * 2 + 1, 1, i * 2 + 2, 0, i * 2 + 1)

            @block.gpsimd
            def _(pool):
                def part(pool, pair, h, hp, g, gp, n):
                    if h is None:
                        return
                    with pool.Fori(0, STEPS // 2) as m:
                        wait(pool, "khigh", at("khigh", h, NS, 1))
                        wait(pool, "klow", at("klow", h, NS, 1))
                        if hp == 1:
                            wait(pool, "vodd", S["vodd"].at(STEPS) + pair * STEPS)
                        for r in range(2):
                            stage_keys(pool, h, hp, m * 2 + r, r)
                            if hp == 1:
                                stage_odd_value(pool, h, m * 2 + r, r)
                run(pool, part)

            @block.tensor
            def _(pe):
                def part(pe, pair, h, hp, g, gp, n):
                    if h is None:
                        tensor_queries(pe, 0, 0, S["weights"].at(WEIGHTS_FIRST))
                    elif g is not None:
                        tensor_queries(pe, g, gp, S["weights"].at(WEIGHTS_FIRST)
                                       + pair * (WEIGHTS_EVEN + WEIGHTS_ODD) + hp * WEIGHTS_EVEN)
                    if h is not None and hp == 0:
                        make_values(pe, pair, 0, 0, first=True)
                    if g is not None:
                        wait(pe, "qlow", S["qlow"].at(1) + g)
                    steps(pe, lambda j, r, first: tensor_step(pe, pair, h, hp, g, gp, j, r, first))
                    tensor_between(pe, pair, h, hp, g, gp, n)
                    if h is not None:
                        wait(pe, "summed", S["summed"].at(1) + n)
                    if g is not None:
                        wait(pe, "shift_row", S["shift_row"].at(1) + g)
                run(pe, part)

            @block.scalar
            def _(act):
                def part(act, pair, h, hp, g, gp, n):
                    if g is not None:
                        scalar_queries(act, g, gp)
                    if h is not None and hp == 0:
                        stage_source(act, pair, 0, 0, first=True)
                        keep_values(act, pair, h, 0, 0, first=True)
                    steps(act, lambda j, r, first: scalar_step(act, pair, h, hp, g, gp, j, r, first))
                    scalar_between(act, h, hp, g, gp, n)
                run(act, part)

            @block.vector
            def _(v):
                def part(v, pair, h, hp, g, gp, n):
                    if g is not None:
                        vector_queries(v, g, gp)
                    steps(v, lambda j, r, first: vector_step(v, h, hp, g, gp, j, r, first))
                    vector_between(v, h, hp, g, gp, n)
                run(v, part)
        for name, n in per.items():
            S[name].total += H1 * n


def build(nc, A, out, stages=(1, 2, 3, 4)):
    with ExitStack() as ctx:
        k = Core(nc, ctx)
        k.cols = k.sb("column_parameters", [P, sum(COL_N)])
        k.rows = k.sb("row_parameters", [P, len(ROWS), D])
        k.squares = k.sb("square_weights", [P, len(SQUARE), D])
        k.ident = k.sb("identity", [P, P])
        k.ones = k.sb("ones", [P, P])
        k.half = k.sb("minus_half", [P, CT])
        k.stat = k.sb("row_statistics", [P, 3, CT])
        k.norm_scratch = k.sb("norm_scratch", [P, TT * D])
        k.x = k.sb("x_rows", [P, TT, D])
        k.zT = k.sb("keys_normed_turned", [P, KEYS])
        load_constants(k, A)
        slot_attention(k, A, 1 in stages)
        if 2 in stages:
            causal_layer(k, A)
        if 3 in stages:
            latents_turned(k)
            perceiver_attention(k, A, k.x)
        if 4 in stages:
            dense_experts(k, A)
        stored = k.sig("stored")
        with nc.Block() as block:
            @block.sync
            def _(sp):
                sp.dma_start(out[0].rearrange("(t p) d -> p t d", p=P), k.x[:]).then_inc(stored.sem, 16)
                sp.wait_ge(stored.sem, 16)



def kernel(**inputs):
    import numpy as np
    import concourse.bacc as bacc
    from concourse.bass_utils import run_bass_kernel_spmd

    a = {name: np.asarray(value) for name, value in inputs.items()}

    def heads(w, n):
        t = w.reshape(n, HD1, D).transpose(0, 2, 1)
        return np.concatenate([t, t], axis=2)

    laid = {
        "x": a["x"],
        "ctx_1024": a["ctx_1024"],
        "cols": np.concatenate([a[name].reshape(n, P) for name, n in zip(COLS, COL_N)]).T,
        "rows": np.stack([a[name].reshape(D) for name in ROWS]),
        "squares": np.stack([a[name] for name in SQUARE], axis=1),
        "router0": a["L0_ffn_router_w"],
        "fc1": a["L0_ffn_fc1_w"],
        "fc2": a["L0_ffn_fc2_w"].reshape(E0, FB0, P, D).transpose(0, 2, 1, 3),
        "fc2_b": a["L0_ffn_fc2_b"],
        "wq": heads(a["L1_xcond_Wq"], H1),
        "wk": heads(a["L1_xcond_Wkv"][0:H1 * HD1], H1),
        "wv": a["L1_xcond_Wkv"][H1 * HD1:].reshape(H1 // 2, 2 * HD1, D).transpose(0, 2, 1),
        "wo": np.concatenate([a["L1_xcond_Wo"].T.reshape(H1, HD1, D)] * 2, axis=1),
        "rW1": a["L1_ffn_rW1"],
        "rW2": a["L1_ffn_rW2"].reshape(RB1, P, E1).transpose(1, 0, 2),
        "rb2": a["L1_ffn_rb2"].reshape(1, E1),
        "We1": a["L1_ffn_We1"],
        "We2": a["L1_ffn_We2"].reshape(E1, FB1, P, D).transpose(0, 2, 1, 3),
        "be2": a["L1_ffn_be2"],
    }
    nc = bacc.Bacc("TRN2", target_bir_lowering=False, num_devices=1)
    arrays, views = {}, {}
    for name, value in laid.items():
        value = np.ascontiguousarray(value)
        arrays["in_" + name] = value
        views[name] = nc.dram_tensor("in_" + name, value.shape, mybir.dt.from_np(value.dtype),
                                     kind="ExternalInput").ap()
    out = nc.dram_tensor("out", (1, TOKENS, D), F32, kind="ExternalOutput").ap()
    build(nc, views, out)
    result = run_bass_kernel_spmd(nc, [arrays], core_ids=[0])
    return result.results[0]["out"]
```

```python
import concourse.bass as bass
from concourse import mybir
from contextlib import ExitStack

F32 = mybir.dt.float32
F32R = mybir.dt.float32r
U32 = mybir.dt.uint32
ALU = mybir.AluOpType
ACT = mybir.ActivationFunctionType
AX = mybir.AxisListType.X
ds = bass.ds

P = 128
D = 128
TOKENS = 1024
TT = TOKENS // P
CTX = 6404
CT = CTX // P
REST = CTX - CT * P
EPS = 1e-5
NEG = -1e30

ITERATIONS = 3
EPS_ATTN = 1e-8
SLOT_SCALE = float(D) ** 0.5
PREP = 5

H0 = 16
HD0 = D // H0
GROUP = 4
NG = H0 // GROUP
E0 = 16
F0 = 512
FB0 = F0 // P
CAP = 2 * (-(-TOKENS // E0))
KEEP = 1.0 - 0.2

H1 = 16
HD1 = 64
KEYS = CTX + TOKENS
STEP = 2 * P
NS = KEYS // STEP
LAST = KEYS - NS * STEP
STEPS = NS + 1
assert STEPS % 2 == 0
LAT0 = CT * P
REST0 = LAT0 + TOKENS
assert CAP == P and REST0 == NS * STEP and LAST == REST and LAST % 2 == 0

E1 = 4
F1 = 512
FB1 = F1 // P
R1 = 256
RB1 = R1 // P

COLS = ["L0_xcond_lnkv_g", "L0_xcond_lnkv_b", "L0_xcond_bk", "L0_xcond_lnq_g", "L0_xcond_lnq_b", "L0_xcond_bq",
        "L0_xcond_lnm_g", "L0_xcond_lnm_b", "L0_xcond_b1", "L0_ffn_ln1_w", "L0_ffn_ln1_b", "L0_ffn_q_b",
        "L0_ffn_k_b", "L1_xcond_ln1_w", "L1_xcond_ln1_b", "L1_xcond_ln2_w", "L1_xcond_ln2_b", "cond_1024",
        "L1_ffn_rb1", "L1_ffn_be1", "L0_ffn_fc1_b"]
COL_N = [1] * 18 + [RB1, E1 * FB1, E0 * FB0]
ROWS = ["L0_xcond_q_mu", "L0_xcond_q_logsig", "L0_xcond_bv", "L0_xcond_bu", "L0_xcond_b2", "L0_xcond_lnp_g",
        "L0_xcond_lnp_b", "cond_1024", "L0_ffn_v_b", "L0_ffn_o_b", "L0_ffn_ln2_w", "L0_ffn_ln2_b"]
SQUARE = ["L0_xcond_wk", "L0_xcond_wv", "L0_xcond_wq", "L0_xcond_wu", "L0_xcond_w1", "L0_xcond_w2",
          "L0_ffn_q_w", "L0_ffn_k_w", "L0_ffn_v_w", "L0_ffn_o_w"]


class Signal:

    def __init__(self, sem):
        self.sem, self.total = sem, 0

    def at(self, n):
        return self.total + n

    def link(self, engine, instruction):
        self.total += 1
        instruction.then_inc(self.sem, 1)
        engine.wait_ge(self.sem, self.total)


class Core:

    def __init__(self, nc, ctx):
        self.nc, self.ctx, self.signals, self.names = nc, ctx, {}, 0
        self.ps = ctx.enter_context(nc.psum_tensor("banks", [P, 8, 512], F32))

    def sb(self, name, shape, dtype=F32, ctx=None):
        self.names += 1
        return (ctx or self.ctx).enter_context(self.nc.sbuf_tensor(f"{name}_{self.names}", shape, dtype))

    def sig(self, name):
        if name not in self.signals:
            self.signals[name] = Signal(self.ctx.enter_context(self.nc.semaphore(name)))
        return self.signals[name]

    def col(self, name, n=0):
        at = sum(COL_N[:COLS.index(name)]) + n
        return self.cols[:, at:at + 1]

    def row(self, name, parts=P):
        return self.rows[0:parts, ROWS.index(name), :]

    def row_of_tiles(self, name, tiles):
        return self.row(name).unsqueeze(1).to_broadcast([P, tiles, D])

    def square(self, name):
        return self.squares[:, SQUARE.index(name), :]


def load_constants(k, A):
    loaded, made = k.sig("constants_loaded"), k.sig("constants_made")
    with k.nc.Block() as block:
        @block.sync
        def _(sp):
            sp.dma_start(k.cols[:], A["cols"]).then_inc(loaded.sem, 16)
            sp.dma_start(k.rows[:], A["rows"].partition_broadcast(P)).then_inc(loaded.sem, 16)
            sp.dma_start(k.squares[:], A["squares"]).then_inc(loaded.sem, 16)
            sp.dma_start(k.x[:], A["x"][0].rearrange("(t p) d -> p t d", p=P)).then_inc(loaded.sem, 16)
            sp.wait_ge(loaded.sem, loaded.at(64))

        @block.gpsimd
        def _(pool):
            pool.memset(k.ident[:], 0.0).then_inc(made.sem, 1)
            pool.memset(k.ones[:], 1.0).then_inc(made.sem, 1)
            pool.memset(k.half[:], -0.5).then_inc(made.sem, 1)
            pool.wait_ge(made.sem, made.at(3))
            pool.affine_select(out=k.ident[:], in_=k.ident[:], compare_op=ALU.not_equal, fill=1.0, base=0,
                               pattern=[[-1, P]], channel_multiplier=1).then_inc(made.sem, 1)
            pool.wait_ge(made.sem, made.at(4))
    loaded.total += 64
    made.total += 4


def layernorm_rows(k, src, dst, parts=P, tiles=TT, gain=None, shift=None):
    step, squared, rooted = k.sig("norm_step"), k.sig("norm_squared"), k.sig("norm_rooted")
    mean, var, rstd = (k.stat[0:parts, n, 0:tiles] for n in range(3))
    square = k.scratch[0:parts, 0:tiles * D].rearrange("p (t d) -> p t d", d=D)
    over = [parts, tiles, D]
    centered, var_ready = step.at(3), step.at(5)
    with k.nc.Block() as block:
        @block.vector
        def _(v):
            step.link(v, v.reduce_sum(mean, src, axis=AX))
            step.link(v, v.tensor_scalar(mean, mean, 1.0 / D, None, ALU.mult))
            step.link(v, v.tensor_tensor(dst, src, mean.unsqueeze(2).to_broadcast(over), ALU.subtract))
            v.wait_ge(squared.sem, squared.at(1))
            step.link(v, v.reduce_sum(var, square, axis=AX))
            step.link(v, v.tensor_scalar(var, var, 1.0 / D, EPS, ALU.mult, ALU.add))
            v.wait_ge(rooted.sem, rooted.at(1))
            step.link(v, v.tensor_tensor(dst, dst, rstd.unsqueeze(2).to_broadcast(over), ALU.mult))
            if gain is not None:
                step.link(v, v.tensor_tensor(dst, dst, gain.unsqueeze(1).to_broadcast(over), ALU.mult))
                step.link(v, v.tensor_tensor(dst, dst, shift.unsqueeze(1).to_broadcast(over), ALU.add))

        @block.scalar
        def _(act):
            act.wait_ge(step.sem, centered)
            act.activation(square, dst, ACT.Square).then_inc(squared.sem, 1)

        @block.gpsimd
        def _(pool):
            pool.wait_ge(step.sem, var_ready)
            pool.tensor_tensor(rstd, var, k.half[0:parts, 0:tiles], ALU.pow).then_inc(rooted.sem, 1)
    squared.total += 1
    rooted.total += 1


def transpose_rows(k, src, dst, gain=None, shift=None):
    turned, kept = k.sig("turned"), k.sig("turned_kept")
    with k.nc.Block() as block:
        @block.tensor
        def _(pe):
            for t in range(TT):
                pe.transpose(k.ps[:, t // 4, t % 4 * P:(t % 4 + 1) * P], src[:, t, :],
                             k.ident[:]).then_inc(turned.sem, 1)

        @block.vector
        def _(v):
            v.wait_ge(turned.sem, turned.at(4))
            if gain is None:
                v.tensor_copy(dst[:, 0:512], k.ps[:, 0, :]).then_inc(kept.sem, 1)
            else:
                v.tensor_scalar(dst[:, 0:512], k.ps[:, 0, :], gain, shift, ALU.mult, ALU.add).then_inc(kept.sem, 1)

        @block.scalar
        def _(act):
            act.wait_ge(turned.sem, turned.at(TT))
            if gain is None:
                act.activation(dst[:, 512:1024], k.ps[:, 1, :], ACT.Copy).then_inc(kept.sem, 1)
            else:
                act.activation(dst[:, 512:1024], k.ps[:, 1, :], ACT.Identity, bias=shift,
                               scale=gain).then_inc(kept.sem, 1)
    turned.total += TT
    kept.total += 2


def project_columns(k, w, src, take):
    ready, taken = k.sig("columns_ready"), k.sig("columns_taken")
    with k.nc.Block() as block:
        @block.tensor
        def _(pe):
            for half in range(2):
                pe.matmul(k.ps[:, half, :], w, src[:, half * 512:(half + 1) * 512], start=True,
                          stop=True).then_inc(ready.sem, 1)

        @block.vector
        def _(v):
            for half in range(2):
                v.wait_ge(ready.sem, ready.at(half + 1))
                take(v, half, k.ps[:, half, :])
    ready.total += 2


def project_rows(k, src, w, take):
    ready = k.sig("rows_ready")
    with k.nc.Block() as block:
        @block.tensor
        def _(pe):
            for t in range(TT):
                pe.matmul(k.ps[:, t // 4, t % 4 * P:(t % 4 + 1) * P], src[:, t * P:(t + 1) * P], w, start=True,
                          stop=True).then_inc(ready.sem, 1)

        @block.vector
        def _(v):
            v.wait_ge(ready.sem, ready.at(TT))
            take(v, k.ps[:, 0:2, :].rearrange("p b (t d) -> p (b t) d", d=D))
    ready.total += TT


def keep(k, v, instruction):
    k.sig("vector_step").link(v, instruction)


def split_columns(k, v, bank, bias, scale, whole, high, low):
    keep(k, v, v.tensor_scalar(whole, bank, bias, scale, ALU.add, ALU.mult))
    keep(k, v, v.tensor_copy(high, whole))
    keep(k, v, v.tensor_tensor(low, whole, high.bitcast(F32), ALU.subtract))



def load_context(k, A, rows, rest):
    loaded = k.sig("context_loaded")
    with k.nc.Block() as block:
        @block.sync
        def _(sp):
            sp.dma_start(rows[:], A["ctx_1024"][0, 0:CT * P, :].rearrange("(p t) d -> p t d", t=CT)) \
              .then_inc(loaded.sem, 16)
            sp.dma_start(rest[0:REST, 0, :], A["ctx_1024"][0, CT * P:CTX, :]).then_inc(loaded.sem, 16)
            sp.wait_ge(loaded.sem, loaded.at(32))
    loaded.total += 32
    layernorm_rows(k, rows[:], rows[:], P, CT)
    layernorm_rows(k, rest[0:REST], rest[0:REST], REST, 1)


def slot_keys_values(k, rows, rest, k_high, k_low, values):
    nc = k.nc
    staged_s, turned_s, kept_s = k.sig("rows_staged"), k.sig("context_turned"), k.sig("context_kept")
    input_s, keys_s, values_s = k.sig("input_ready"), k.sig("keys_ready"), k.sig("values_ready")
    high_s, low_s, stored_s = k.sig("keys_high"), k.sig("keys_low"), k.sig("values_stored")
    N = CT // PREP
    W = PREP * P
    with ExitStack() as ctx:
        staged = k.sb("staged_rows", [P, 2, PREP, D], ctx=ctx)
        inputs = k.sb("slot_inputs", [P, 2, W], ctx=ctx)
        turned = k.ps[:, 0:2, :].rearrange("p b c -> p (b c)")
        keys = k.ps[:, 2:4, :].rearrange("p b c -> p (b c)")
        vals = k.ps[:, 4:6, :].rearrange("p b c -> p (b c)")

        def pieces(width):
            return [(a, min(a + 512, width)) for a in range(0, width, 512)]

        with nc.Block() as block:
            def scalar_step(act, i, r, tiles, parts, first, early):
                width = (tiles - 1) * P + parts
                at = REST0 if i is None else i * W
                to = CT * P if i is None else i * W
                n = N if i is None else i
                if not early:
                    act.wait_ge(turned_s.sem, turned_s.at(0) + n - 1)
                act.activation(staged[0:parts, r, 0:tiles, :],
                               rest[0:parts, 0:1, :] if i is None else rows[:, ds(i * PREP, PREP), :],
                               ACT.Copy).then_inc(staged_s.sem, 1)
                act.wait_ge(turned_s.sem, turned_s.at(1) + n)
                act.activation(k.zT[:, ds(at, width)], turned[:, 0:width], ACT.Copy).then_inc(kept_s.sem, 1)
                act.wait_ge(keys_s.sem, keys_s.at(1) + n)
                act.activation(k_high[:, ds(to, width)], keys[:, 0:width], ACT.Identity,
                               bias=k.col("L0_xcond_bk")).then_inc(high_s.sem, 1)

            def tensor_step(pe, i, r, tiles, parts, first, early):
                width = (tiles - 1) * P + parts
                n = N if i is None else i
                pe.wait_ge(staged_s.sem, staged_s.at(1) + n)
                if not first:
                    pe.wait_ge(kept_s.sem, kept_s.at(0) + n)
                    pe.wait_ge(input_s.sem, input_s.at(0) + n)
                for t in range(tiles):
                    last = pe.transpose(turned[:, t * P:t * P + parts], staged[0:parts, r, t, :],
                                        k.ident[0:parts, 0:parts])
                last.then_inc(turned_s.sem, 1)
                pe.wait_ge(input_s.sem, input_s.at(1) + n)
                if not first:
                    pe.wait_ge(high_s.sem, high_s.at(0) + n)
                    pe.wait_ge(low_s.sem, low_s.at(0) + n)
                for a, b in pieces(width):
                    last = pe.matmul(keys[:, a:b], k.square("L0_xcond_wk"), inputs[:, r, a:b], start=True, stop=True)
                last.then_inc(keys_s.sem, 1)
                if not first:
                    pe.wait_ge(stored_s.sem, stored_s.at(0) + n)
                for t in range(tiles):
                    last = pe.matmul(vals[0:parts, t * P:(t + 1) * P], inputs[:, r, t * P:t * P + parts],
                                     k.square("L0_xcond_wv"), start=True, stop=True)
                last.then_inc(values_s.sem, 1)

            def vector_step(v, i, r, tiles, parts, first, early):
                width = (tiles - 1) * P + parts
                to = CT * P if i is None else i * W
                n = N if i is None else i
                v.wait_ge(kept_s.sem, kept_s.at(1) + n)
                if not early:
                    v.wait_ge(values_s.sem, values_s.at(0) + n - 1)
                v.tensor_scalar(inputs[:, r, 0:width], turned[:, 0:width], k.col("L0_xcond_lnkv_g"),
                                k.col("L0_xcond_lnkv_b"), ALU.mult, ALU.add).then_inc(input_s.sem, 1)
                v.wait_ge(high_s.sem, high_s.at(1) + n)
                high = k_high[:, ds(to, width)]
                v.scalar_tensor_tensor(out=k_low[:, ds(to, width)], in0=keys[:, 0:width],
                                       scalar=k.col("L0_xcond_bk"), in1=high.bitcast(F32), op0=ALU.add,
                                       op1=ALU.subtract).then_inc(low_s.sem, 1)
                v.wait_ge(values_s.sem, values_s.at(1) + n)
                v.tensor_tensor(values[0:parts, ds(CT if i is None else i * PREP, tiles), :],
                                vals[0:parts, 0:tiles * D].rearrange("p (t d) -> p t d", d=D),
                                k.row("L0_xcond_bv", parts).unsqueeze(1).to_broadcast([parts, tiles, D]),
                                ALU.add).then_inc(stored_s.sem, 1)

            def steps(engine, step):
                step(engine, 0, 0, PREP, P, True, True)
                step(engine, 1, 1, PREP, P, False, True)
                with engine.Fori(1, N // 2) as m:
                    i = m * 2
                    step(engine, i, 0, PREP, P, False, False)
                    step(engine, i + 1, 1, PREP, P, False, False)
                step(engine, None, 0, 1, REST, False, False)

            @block.scalar
            def _(act):
                steps(act, scalar_step)

            @block.tensor
            def _(pe):
                steps(pe, tensor_step)

            @block.vector
            def _(v):
                steps(v, vector_step)
        for s in (staged_s, turned_s, kept_s, input_s, keys_s, values_s, high_s, low_s, stored_s):
            s.total += N + 1


def value_sum(k, values, vsum):
    summed = k.sig("values_summed")
    with ExitStack() as ctx:
        part = k.sb("values_part", [P, D], ctx=ctx)
        with k.nc.Block() as block:
            @block.vector
            def _(v):
                keep(k, v, v.reduce_sum(part[:], values[:, 0:CT, :].rearrange("p t d -> p d t"), axis=AX))
                keep(k, v, v.tensor_tensor(part[0:REST], part[0:REST], values[0:REST, CT, :], ALU.add))
        with k.nc.Block() as block:
            @block.tensor
            def _(pe):
                pe.matmul(k.ps[:, 0, 0:1], part[:], k.ones[:, 0:1], start=True, stop=True).then_inc(summed.sem, 1)

            @block.vector
            def _(v):
                v.wait_ge(summed.sem, summed.at(1))
                keep(k, v, v.tensor_scalar(vsum[:], k.ps[:, 0, 0:1], EPS_ATTN, None, ALU.mult))
        summed.total += 1


def slot_scores_and_updates(k, k_high, k_low, values, q_high, q_low, total):
    nc = k.nc
    staged_s, scores_s, probs_s = k.sig("key_staged"), k.sig("scores_ready"), k.sig("probs_ready")
    max_s, bias_s, recip_s = k.sig("slot_max"), k.sig("slot_bias"), k.sig("slot_recip")
    total_s, scaled_s, update_s = k.sig("total_added"), k.sig("value_scaled"), k.sig("update_added")
    RING = 3
    with ExitStack() as ctx:
        key = k.sb("key_tile", [P, RING, 2, P], F32R, ctx=ctx)
        probs = k.sb("slot_probs", [P, RING, TOKENS], ctx=ctx)
        value = k.sb("value_tile", [P, RING, D], ctx=ctx)
        small = k.sb("slot_small", [P, RING, 4], ctx=ctx)
        scores = [k.ps[:, bank:bank + 2, :] for bank in (0, 2, 6)]
        update = k.ps[:, 4:6, :]

        def early(i):
            return isinstance(i, int) and i < RING

        def run(engine, step):
            for i in range(RING):
                step(i, i, P)
            with engine.Fori(1, CT // RING) as m:
                for r in range(RING):
                    step(m * RING + r, r, P)
            for i in range(CT // RING * RING, CT + 1):
                step(i, i % RING, P if i < CT else REST)

        def tile_before(i, r):
            return i - 1, (r - 1) % RING

        with nc.Block() as block:
            @block.gpsimd
            def _(pool):
                def stage(i, r, parts):
                    if not early(i):
                        pool.wait_ge(scores_s.sem, scores_s.at(1 - RING) + i)
                    for n, source in enumerate((k_high, k_low)):
                        pool.tensor_copy(key[:, r, n, 0:parts], source[:, ds(i * P, parts)]).then_inc(staged_s.sem, 1)

                def step(i, r, parts):
                    pool.wait_ge(recip_s.sem, recip_s.at(1) + i)
                    if not early(i):
                        pool.wait_ge(update_s.sem, update_s.at(1 - RING) + i)
                    pool.tensor_tensor(value[0:parts, r, :], values[0:parts, ds(i, 1), :].squeeze(1),
                                       small[0:parts, r, 3:4].to_broadcast([parts, D]),
                                       ALU.mult).then_inc(scaled_s.sem, 1)
                    if not isinstance(i, int) or i + RING <= CT:
                        stage(i + RING, r, REST if isinstance(i, int) and i + RING == CT else P)

                for i in range(RING):
                    stage(i, i, P)
                for i in range(RING):
                    step(i, i, P)
                assert CT // RING * RING + RING > CT
                with pool.Fori(1, CT // RING - 1) as m:
                    for r in range(RING):
                        step(m * RING + r, r, P)
                for i in range((CT // RING - 1) * RING, CT + 1):
                    step(i, i % RING, P if i < CT else REST)

            @block.tensor
            def _(pe):
                def score(i, r):
                    pe.wait_ge(staged_s.sem, staged_s.at(2) + i * 2)
                    if not early(i):
                        pe.wait_ge(probs_s.sem, probs_s.at(1 - RING) + i)
                    for c in range(2):
                        cols = slice(c * 512, (c + 1) * 512)
                        pe.matmul(scores[r][:, c, :], key[:, r, 0, :], q_high[:, cols], start=True, stop=False)
                        pe.matmul(scores[r][:, c, :], key[:, r, 1, :], q_high[:, cols], start=False, stop=False)
                        last = pe.matmul(scores[r][:, c, :], key[:, r, 0, :], q_low[:, cols], start=False, stop=True)
                    last.then_inc(scores_s.sem, 1)

                def add(i, r, parts):
                    first, final = isinstance(i, int) and i == 0, isinstance(i, int) and i == CT
                    pe.wait_ge(scaled_s.sem, scaled_s.at(1) + i)
                    pe.wait_ge(probs_s.sem, probs_s.at(1) + i)
                    for c in range(2):
                        last = pe.matmul(update[:, c, :], value[0:parts, r, :], probs[0:parts, r, c * 512:(c + 1) * 512],
                                         start=first, stop=final)
                    last.then_inc(update_s.sem, 1)

                def step(i, r, parts):
                    score(i, r)
                    if not isinstance(i, int) or i >= 2:
                        add(i - 2, (r - 2) % RING, P)

                run(pe, step)
                add(CT - 1, (CT - 1) % RING, P)
                add(CT, CT % RING, REST)

            @block.vector
            def _(v):
                def bound(i, r, parts):
                    v.wait_ge(scores_s.sem, scores_s.at(1) + i)
                    v.reduce_max(small[0:parts, r, 0:1], scores[r][0:parts].rearrange("p b c -> p (b c)"),
                                 axis=AX).then_inc(max_s.sem, 1)
                    v.wait_ge(max_s.sem, max_s.at(1) + i)
                    v.tensor_scalar(small[0:parts, r, 1:2], small[0:parts, r, 0:1], -SLOT_SCALE, None,
                                    ALU.mult).then_inc(bias_s.sem, 1)

                def invert(i, r, parts):
                    v.wait_ge(probs_s.sem, probs_s.at(1) + i)
                    if not early(i):
                        v.wait_ge(scaled_s.sem, scaled_s.at(1 - RING) + i)
                    v.reciprocal(small[0:parts, r, 3:4], small[0:parts, r, 2:3]).then_inc(recip_s.sem, 1)

                def count(i, r, parts):
                    v.wait_ge(recip_s.sem, recip_s.at(1) + i)
                    v.wait_ge(total_s.sem, total_s.at(1) + i)
                    v.scalar_tensor_tensor(out=total[0:parts], in0=probs[0:parts, r, :], scalar=small[0:parts, r, 3:4],
                                           in1=total[0:parts], op0=ALU.mult, op1=ALU.add).then_inc(total_s.sem, 1)

                def step(i, r, parts):
                    if isinstance(i, int) and i == 0:
                        bound(i, r, parts)
                        return
                    before = tile_before(i, r)
                    invert(*before, P)
                    bound(i, r, parts)
                    count(*before, P)

                v.memset(total[:], 0.0).then_inc(total_s.sem, 1)
                run(v, step)
                invert(CT, CT % RING, REST)
                count(CT, CT % RING, REST)

            @block.scalar
            def _(act):
                def step(i, r, parts):
                    act.wait_ge(bias_s.sem, bias_s.at(1) + i)
                    if not early(i):
                        act.wait_ge(update_s.sem, update_s.at(1 - RING) + i)
                        act.wait_ge(total_s.sem, total_s.at(2 - RING) + i)
                    act.activation(probs[0:parts, r, :], scores[r][0:parts].rearrange("p b c -> p (b c)"), ACT.Exp,
                                   bias=small[0:parts, r, 1:2], scale=SLOT_SCALE,
                                   accum_out=small[0:parts, r, 2:3]).then_inc(probs_s.sem, 1)

                run(act, step)
        for s in (scores_s, probs_s, max_s, bias_s, recip_s, scaled_s, update_s):
            s.total += CT + 1
        staged_s.total += 2 * (CT + 1)
        total_s.total += CT + 2


def slot_normalise(k, total, vsum, update):
    summed = k.sig("total_summed")
    with k.nc.Block() as block:
        @block.tensor
        def _(pe):
            for c in range(2):
                pe.matmul(k.ps[:, c, :], k.ones[:], total[:, c * 512:(c + 1) * 512], start=True,
                          stop=True).then_inc(summed.sem, 1)

        @block.vector
        def _(v):
            whole = k.ps[:, 0:2, :].rearrange("p b c -> p (b c)")
            added = k.ps[:, 4:6, :].rearrange("p b c -> p (b c)")
            v.wait_ge(summed.sem, summed.at(2))
            keep(k, v, v.tensor_scalar(update[:], whole, CTX * EPS_ATTN, None, ALU.add))
            keep(k, v, v.reciprocal(update[:], update[:]))
            keep(k, v, v.scalar_tensor_tensor(out=update[:], in0=added, scalar=vsum[:], in1=update[:], op0=ALU.add,
                                              op1=ALU.mult))
    summed.total += 2


def gelu_columns(k, w, src, bias, dst):
    ready, done = k.sig("hidden_ready"), k.sig("hidden_done")
    with k.nc.Block() as block:
        @block.tensor
        def _(pe):
            for half in range(2):
                pe.matmul(k.ps[:, half, :], w, src[:, half * 512:(half + 1) * 512], start=True,
                          stop=True).then_inc(ready.sem, 1)

        @block.scalar
        def _(act):
            for half in range(2):
                act.wait_ge(ready.sem, ready.at(half + 1))
                act.activation(dst[:, half * 512:(half + 1) * 512], k.ps[:, half, :], ACT.Gelu,
                               bias=bias).then_inc(done.sem, 1)
    ready.total += 2
    done.total += 2


def slot_attention(k, A, whole=True):
    with ExitStack() as ctx:
        k_high = k.sb("k_high", [P, CTX], F32R, ctx=ctx)
        k_low = k.sb("k_low", [P, CTX], F32R, ctx=ctx)
        values = k.sb("values", [P, CT + 1, D], ctx=ctx)
        with ExitStack() as inner:
            rows = k.sb("context_rows", [P, CT, D], ctx=inner)
            rest = k.sb("context_rest", [P, 1, D], ctx=inner)
            k.scratch = k.sb("norm_scratch_context", [P, CT * D], ctx=inner)
            load_context(k, A, rows, rest)
            slot_keys_values(k, rows, rest, k_high, k_low, values)
        k.scratch = k.norm_scratch
        if not whole:
            return
        slots = k.sb("slots", [P, TT, D], ctx=ctx)
        normed = k.sb("slots_normed", [P, TT, D], ctx=ctx)
        turned = k.sb("slots_turned", [P, TOKENS], ctx=ctx)
        q_high = k.sb("q_high", [P, TOKENS], F32R, ctx=ctx)
        q_low = k.sb("q_low", [P, TOKENS], F32R, ctx=ctx)
        total = k.sb("attention_total", [P, TOKENS], ctx=ctx)
        vsum = k.sb("value_sum", [P, 1], ctx=ctx)
        sigma = k.sb("slot_sigma", [P, D], ctx=ctx)
        value_sum(k, values, vsum)
        layernorm_rows(k, k.x[:], normed[:])
        exp_s = k.sig("sigma_ready")
        with k.nc.Block() as block:
            @block.scalar
            def _(act):
                act.activation(sigma[:], k.row("L0_xcond_q_logsig"), ACT.Exp).then_inc(exp_s.sem, 1)

            @block.vector
            def _(v):
                v.wait_ge(exp_s.sem, exp_s.at(1))
                over = [P, TT, D]
                keep(k, v, v.tensor_tensor(slots[:], normed[:], sigma[:].unsqueeze(1).to_broadcast(over), ALU.mult))
                keep(k, v, v.tensor_tensor(slots[:], slots[:], k.row_of_tiles("L0_xcond_q_mu", TT), ALU.add))
        exp_s.total += 1

        def take_queries(v, half, bank):
            cols = slice(half * 512, (half + 1) * 512)
            split_columns(k, v, bank, k.col("L0_xcond_bq"), 1.0, turned[:, cols], q_high[:, cols], q_low[:, cols])

        def take_slots(bias):
            def take(v, rows):
                keep(k, v, v.tensor_tensor(slots[:], slots[:], rows, ALU.add))
                keep(k, v, v.tensor_tensor(slots[:], slots[:], k.row_of_tiles(bias, TT), ALU.add))
            return take

        for _ in range(ITERATIONS):
            layernorm_rows(k, slots[:], normed[:])
            transpose_rows(k, normed, total, k.col("L0_xcond_lnq_g"), k.col("L0_xcond_lnq_b"))
            project_columns(k, k.square("L0_xcond_wq"), total, take_queries)
            slot_scores_and_updates(k, k_high, k_low, values, q_high, q_low, total)
            slot_normalise(k, total, vsum, turned)
            project_rows(k, turned, k.square("L0_xcond_wu"), take_slots("L0_xcond_bu"))
            layernorm_rows(k, slots[:], normed[:])
            transpose_rows(k, normed, turned, k.col("L0_xcond_lnm_g"), k.col("L0_xcond_lnm_b"))
            gelu_columns(k, k.square("L0_xcond_w1"), turned, k.col("L0_xcond_b1"), total)
            project_rows(k, total, k.square("L0_xcond_w2"), take_slots("L0_xcond_b2"))
            with k.nc.Block() as block:
                @block.vector
                def _(v):
                    keep(k, v, v.tensor_tensor(normed[:], slots[:], k.row_of_tiles("cond_1024", TT), ALU.add))
            layernorm_rows(k, normed[:], slots[:], gain=k.row("L0_xcond_lnp_g"), shift=k.row("L0_xcond_lnp_b"))
        with k.nc.Block() as block:
            @block.vector
            def _(v):
                keep(k, v, v.tensor_tensor(k.x[:], k.x[:], slots[:], ALU.add))



def causal_attention(k, xaT, values, context):
    nc = k.nc
    parts = nc.dram_tensor("query_key_parts", [4, P, TOKENS], F32, kind="Internal").ap()
    S = {name: k.sig("causal_" + name) for name in (
        "parted", "loaded_even", "loaded_odd", "cleared", "fill", "peak", "negated", "turned", "shift", "score", "expd",
        "added", "kept", "back", "inverted", "context", "grouped")}
    ITEMS = GROUP * TT
    LOADED, LOADS = ("loaded_even", "loaded_odd"), 6 * 16

    def inc(name, instruction):
        instruction.then_inc(S[name].sem, 1)

    def wait(engine, name, n, g=0, per=0):
        engine.wait_ge(S[name].sem, S[name].at(n) + g * per)

    with ExitStack() as ctx:
        queries = [k.sb("queries", [P, GROUP, TOKENS], F32R, ctx=ctx) for _ in range(2)]
        keys = [k.sb("keys", [P, GROUP, TOKENS], F32R, ctx=ctx) for _ in range(2)]
        with ExitStack() as inner:
            whole = k.sb("split_whole", [P, TOKENS], ctx=inner)
            split = k.sb("split_parts", [P, 4, TOKENS], F32R, ctx=inner)
            for n, (w, b, scale) in enumerate((("L0_ffn_q_w", "L0_ffn_q_b", float(HD0) ** -0.5),
                                               ("L0_ffn_k_w", "L0_ffn_k_b", 1.0))):
                def take(v, half, bank):
                    cols = slice(half * 512, (half + 1) * 512)
                    split_columns(k, v, bank, k.col(b), scale, whole[:, cols], split[:, 2 * n, cols],
                                  split[:, 2 * n + 1, cols])
                project_columns(k, k.square(w), xaT, take)

            with nc.Block() as block:
                @block.sync
                def _(sp):
                    sp.dma_start(parts.rearrange("n p t -> p n t"), split[:].bitcast(F32)).then_inc(S["parted"].sem, 16)
                    sp.wait_ge(S["parted"].sem, 16)

                @block.vector
                def _(v):
                    for tile in queries + keys:
                        inc("cleared", v.memset(tile[:].bitcast(F32), 0.0))
                    wait(v, "cleared", 4)
                    for tile in keys:
                        inc("cleared", v.memset(tile[64:65].bitcast(F32), 1.0))
                    wait(v, "cleared", 6)
            S["cleared"].total += 6

        probs = k.sb("causal_probs", [P, 2, GROUP, TOKENS], ctx=ctx)
        value = k.sb("causal_value", [P, TT, 2, GROUP * 32], ctx=ctx)
        peaks = k.sb("causal_peaks", [P, GROUP, 64 + TT], ctx=ctx)
        out_sb = k.sb("causal_out", [P, TOKENS], ctx=ctx)
        inverse = k.sb("causal_inverse", [P, TT, GROUP], ctx=ctx)
        mask = k.sb("causal_mask", [P, 2, P], F32R, ctx=ctx)
        ident = k.sb("identity_r", [P, P], F32R, ctx=ctx)
        whole_mask = k.sb("whole_mask", [P, 2, P], ctx=ctx)
        spread = [k.ps[:, 2 * r:2 * r + 2, :].rearrange("p b c -> p (b c)") for r in range(2)]
        turned = k.ps[:, 4:6, :]
        out = k.ps[:, 6:8, :]

        with nc.Block() as block:
            @block.gpsimd
            def _(pool):
                pool.memset(whole_mask[:], 0.0).then_inc(S["cleared"].sem, 1)
                wait(pool, "cleared", 1)
                for n, sign in enumerate((1, -1)):
                    pool.affine_select(out=whole_mask[:, n, :], in_=whole_mask[:, n, :], compare_op=ALU.is_ge,
                                       fill=NEG, base=0, pattern=[[-sign, P]],
                                       channel_multiplier=sign).then_inc(S["cleared"].sem, 1)
                wait(pool, "cleared", 3)
                pool.tensor_copy(mask[:], whole_mask[:]).then_inc(S["cleared"].sem, 1)
                pool.tensor_copy(ident[:], k.ident[:]).then_inc(S["cleared"].sem, 1)
                pool.memset(peaks[:], 0.0).then_inc(S["cleared"].sem, 1)
                wait(pool, "cleared", 6)
        S["cleared"].total += 6

        def load(sp, g):
            r = g % 2
            if g >= 2:
                wait(sp, "score", ITEMS * (g - 1))
                wait(sp, "added", TT * (g - 1))
            for tile, order in ((queries[r], (0, 1, 0)), (keys[r], (2, 2, 3))):
                for n, part in enumerate(order):
                    sp.dma_start(tile[n * HD0:(n + 1) * HD0].bitcast(F32), parts[part, g * 32:(g + 1) * 32, :]
                                 .rearrange("(h r) t -> r h t", r=HD0)) \
                      .then_inc(S[LOADED[r]].sem, 16)

        def pieces(a, b):
            return [(x, min(b, (x // 512 + 1) * 512)) for x in [a] + [c for c in (512,) if a < c < b]]

        def fill(pe, g, r):
            for n in range(ITEMS):
                h, t = n // TT, n % TT
                if n >= 2:
                    wait(pe, "peak", n - 1, g, ITEMS)
                else:
                    wait(pe, "expd", 0, g, ITEMS)
                width = (t + 1) * P
                for a, b in pieces(0, width):
                    pe.matmul(spread[n % 2][:, a:b], queries[r][:, h, t * P:(t + 1) * P], keys[r][:, h, a:b],
                              start=True, stop=b < width)
                inc("fill", pe.matmul(spread[n % 2][:, width - P:width], ident[:], mask[:, 0, :], start=False, stop=True))
                if t == 1 and h:
                    turn_peaks(pe, g, h - 1)
            turn_peaks(pe, g, GROUP - 1)

        def turn_peaks(pe, g, h):
            wait(pe, "negated", h + 1, g, GROUP)
            if h:
                wait(pe, "shift", h, g, GROUP)
            else:
                wait(pe, "context", 0, g, 1)
            for t in range(TT):
                last = pe.transpose(turned[0:65, t // 4, t % 4 * P:(t % 4 + 1) * P], peaks[:, h, t:t + 65], k.ident[:])
            inc("turned", last)

        def tensor_group(pe, g, r):
            wait(pe, LOADED[r], LOADS - r * LOADS // 2, g, LOADS // 2)
            fill(pe, g, r)
            wait(pe, "shift", GROUP, g, GROUP)
            for j in range(TT + 1):
                if j < TT:
                    for h in range(GROUP):
                        n = GROUP * j + h
                        if n >= 2:
                            wait(pe, "expd", n - 1, g, ITEMS)
                        else:
                            wait(pe, "peak", ITEMS, g, ITEMS)
                        width = TOKENS - j * P
                        for a, b in pieces(0, width):
                            last = pe.matmul(spread[n % 2][:, a:b], keys[r][:, h, j * P:(j + 1) * P],
                                             queries[r][:, h, j * P + a:j * P + b], start=True, stop=a > 0)
                            if a == 0:
                                last = pe.matmul(spread[n % 2][:, 0:P], ident[:], mask[:, 1, :], start=False, stop=True)
                        inc("score", last)
                if j:
                    add(pe, g, r, j - 1)
            wait(pe, "kept", 1, g, 1)
            for t in range(TT):
                last = pe.transpose(turned[:, t // 4, t % 4 * P:(t % 4 + 1) * P], out_sb[:, t * P:(t + 1) * P],
                                    k.ident[:])
            inc("back", last)

        def add(pe, g, r, j):
            wait(pe, "expd", GROUP * (j + 1), g, ITEMS)
            if j == 0:
                wait(pe, "kept", 0, g, 1)
                wait(pe, "grouped", 1, g, 1)
            for a, b in pieces(j * P, TOKENS):
                for h in range(GROUP):
                    last = pe.matmul(out[32 * h:32 * h + 32, a // 512, a % 512:(b - 1) % 512 + 1],
                                     value[:, j, r, 32 * h:32 * h + 32], probs[:, j % 2, h, a - j * P:b - j * P],
                                     start=j == 0, stop=j == (3 if a < 512 else TT - 1))
            inc("added", last)

        def scalar_group(act, g, r):
            for h in range(GROUP):
                wait(act, "turned", h + 1, g, GROUP)
                inc("shift", act.activation(queries[r][64:65, h, :].rearrange("p (b c) -> p b c", b=2),
                                            turned[64:65], ACT.Copy))
            for n in range(ITEMS):
                j, h = n // GROUP, n % GROUP
                wait(act, "score", n + 1, g, ITEMS)
                if h == 0:
                    wait(act, "added", max(j - 1, 0), g, TT)
                width = TOKENS - j * P
                inc("expd", act.activation(probs[:, j % 2, h, 0:width], spread[n % 2][:, 0:width], ACT.Exp))
            wait(act, "added", TT, g, TT)
            wait(act, "back", 0, g, 1)
            inc("kept", act.activation(out_sb[:].rearrange("p (b c) -> p b c", b=2), out, ACT.Copy))

        def vector_group(v, g, r):
            for n in range(ITEMS):
                h, t = n // TT, n % TT
                wait(v, "fill", n + 1, g, ITEMS)
                if n == 0:
                    wait(v, "turned", 0, g, GROUP)
                inc("peak", v.reduce_max(peaks[:, h, 64 + t:65 + t], spread[n % 2][:, 0:(t + 1) * P], axis=AX))
                if t == TT - 1:
                    wait(v, "peak", n + 1, g, ITEMS)
                    inc("negated", v.tensor_scalar(peaks[:, h, 64:64 + TT], peaks[:, h, 64:64 + TT], -1.0, None,
                                                   ALU.mult))
            wait(v, "back", 1, g, 1)
            rows = turned.rearrange("p b (t h c) -> p (b t) h c", t=4, h=GROUP)
            inc("inverted", v.reciprocal(inverse[:], rows[:, :, :, HD0]))
            wait(v, "inverted", 1, g, 1)
            inc("context", v.tensor_tensor(
                context[:, :, ds(g * GROUP * HD0, GROUP * HD0)].rearrange("p t (h c) -> p t h c", h=GROUP),
                rows[:, :, :, 0:HD0], inverse[:].unsqueeze(3).to_broadcast([P, TT, GROUP, HD0]), ALU.mult))

        def pool_group(pool, g, r):
            wait(pool, "added", 0, g, TT)
            inc("grouped", pool.tensor_copy(value[:, :, r, :], values[:, :, ds(g * GROUP * 32, GROUP * 32)]))

        def groups(engine, part):
            with engine.Fori(0, NG // 2) as i:
                for r in range(2):
                    part(engine, i * 2 + r, r)

        with nc.Block() as block:
            @block.sync
            def _(sp):
                for g in range(NG):
                    load(sp, g)

            @block.tensor
            def _(pe):
                groups(pe, tensor_group)

            @block.scalar
            def _(act):
                groups(act, scalar_group)

            @block.vector
            def _(v):
                groups(v, vector_group)

            @block.gpsimd
            def _(pool):
                groups(pool, pool_group)



def route(k, xt, xtT, router, weights, scatter, gather):
    nc = k.nc
    with ExitStack() as ctx:
        sb = lambda name, shape, dtype=F32: k.sb(name, shape, dtype, ctx=ctx)
        logits = sb("logits", [P, TT, E0])
        best = sb("best", [P, TT, 8])
        place = sb("best_place", [P, TT, 8], U32)
        placef = sb("best_placef", [P, TT, 2])
        probs = sb("router_probs", [P, TT, E0])
        total = sb("router_total", [P, TT, 1])
        chosen = sb("chosen", [P, TT, 2 * E0])
        before = sb("chosen_before", [P, TT + 1, 2 * E0])
        location = sb("location", [P, TT, 2 * E0])
        product = sb("route_product", [P, TT, 2 * E0])
        kept = sb("kept", [P, TT, 2])
        slot = sb("slot", [P, TT, 2])
        spare = sb("spare", [P, TT, 2])
        expert = sb("expert_number", [P, E0])
        upper = sb("upper", [P, P])
        made, ready = k.sig("route_constants"), k.sig("route_counted")
        exp_s = k.sig("route_exponential")

        with nc.Block() as block:
            @block.gpsimd
            def _(pool):
                pool.iota(expert[:], [[1, E0]], base=0, channel_multiplier=0,
                          allow_small_or_imprecise_dtypes=True).then_inc(made.sem, 1)
                pool.iota(spare[:], [[2 * P, TT], [1, 2]], base=E0 * CAP, channel_multiplier=2,
                          allow_small_or_imprecise_dtypes=True).then_inc(made.sem, 1)
                pool.memset(upper[:], 1.0).then_inc(made.sem, 1)
                pool.wait_ge(made.sem, made.at(3))
                pool.affine_select(out=upper[:], in_=upper[:], compare_op=ALU.is_ge, fill=0.0, base=0,
                                   pattern=[[1, P]], channel_multiplier=-1).then_inc(made.sem, 1)
                pool.wait_ge(made.sem, made.at(4))

            @block.tensor
            def _(pe):
                for t in range(TT):
                    pe.matmul(k.ps[:, 0, t * E0:(t + 1) * E0], xtT[:, t * P:(t + 1) * P], router[:], start=True,
                              stop=True).then_inc(ready.sem, 1)

            @block.vector
            def _(v):
                v.wait_ge(ready.sem, ready.at(TT))
                keep(k, v, v.tensor_copy(logits[:].rearrange("p t e -> p (t e)"), k.ps[:, 0, 0:TT * E0]))
                for t in range(TT):
                    keep(k, v, v.max(best[:, t, :], logits[:, t, :]))
                    keep(k, v, v.max_index(place[:, t, :], best[:, t, :], logits[:, t, :]))
                keep(k, v, v.tensor_copy(placef[:], place[:, :, 0:2]))
                keep(k, v, v.tensor_tensor(probs[:], logits[:], best[:, :, 0:1].to_broadcast([P, TT, E0]),
                                           ALU.subtract))
        made.total += 4
        ready.total += TT

        with nc.Block() as block:
            @block.scalar
            def _(act):
                act.activation(probs[:], probs[:], ACT.Exp).then_inc(exp_s.sem, 1)

            @block.vector
            def _(v):
                for n in range(2):
                    keep(k, v, v.tensor_tensor(chosen[:, :, n * E0:(n + 1) * E0],
                                               expert[:].unsqueeze(1).to_broadcast([P, TT, E0]),
                                               placef[:, :, n:n + 1].to_broadcast([P, TT, E0]), ALU.is_equal))
                keep(k, v, v.memset(before[:, 0, :], 0.0))
                for t in range(TT):
                    keep(k, v, v.tensor_tensor(before[:, t + 1, :], before[:, t, :], chosen[:, t, :], ALU.add))
                keep(k, v, v.tensor_tensor(before[:, 0:TT, E0:2 * E0], before[:, 0:TT, E0:2 * E0],
                                           before[:, TT:TT + 1, 0:E0].to_broadcast([P, TT, E0]), ALU.add))
                v.wait_ge(exp_s.sem, exp_s.at(1))
                keep(k, v, v.reduce_sum(total[:].squeeze(2), probs[:], axis=AX))
                keep(k, v, v.reciprocal(total[:], total[:]))
                keep(k, v, v.tensor_tensor(probs[:], probs[:], total[:].to_broadcast([P, TT, E0]), ALU.mult))
        exp_s.total += 1

        with nc.Block() as block:
            @block.tensor
            def _(pe):
                pe.matmul(k.ps[:, 1, 0:TT * 2 * E0], upper[:], chosen[:].rearrange("p t e -> p (t e)"), start=True,
                          stop=False)
                pe.matmul(k.ps[:, 1, 0:TT * 2 * E0], k.ones[:], before[:, 0:TT, :].rearrange("p t e -> p (t e)"),
                          start=False, stop=True).then_inc(ready.sem, 1)

            @block.vector
            def _(v):
                both = lambda tile: tile[:].rearrange("p t (n e) -> p t n e", n=2)
                v.wait_ge(ready.sem, ready.at(1))
                keep(k, v, v.tensor_scalar(location[:].rearrange("p t e -> p (t e)"), k.ps[:, 1, 0:TT * 2 * E0], -1.0,
                                           None, ALU.add))
                keep(k, v, v.scalar_tensor_tensor(out=chosen[:].rearrange("p t e -> p (t e)"),
                                                  in0=location[:].rearrange("p t e -> p (t e)"), scalar=float(CAP),
                                                  in1=chosen[:].rearrange("p t e -> p (t e)"), op0=ALU.is_lt,
                                                  op1=ALU.mult))
                keep(k, v, v.tensor_tensor(product[:], location[:], chosen[:], ALU.mult))
                keep(k, v, v.reduce_sum(slot[:], both(product), axis=AX))
                keep(k, v, v.reduce_sum(kept[:], both(chosen), axis=AX))
                for n in range(2):
                    keep(k, v, v.tensor_tensor(product[:, :, n * E0:(n + 1) * E0], probs[:],
                                               chosen[:, :, n * E0:(n + 1) * E0], ALU.mult))
                keep(k, v, v.reduce_sum(weights[:], both(product), axis=AX))
                keep(k, v, v.tensor_tensor(total[:], weights[:, :, 0:1], weights[:, :, 1:2], ALU.add))
                keep(k, v, v.tensor_scalar(total[:], total[:], float(2.0 ** -23), None, ALU.max))
                keep(k, v, v.reciprocal(total[:], total[:]))
                keep(k, v, v.tensor_tensor(weights[:], weights[:], total[:].to_broadcast([P, TT, 2]), ALU.mult))
                flat = lambda tile: tile[:].rearrange("p t n -> p (t n)")
                keep(k, v, v.scalar_tensor_tensor(out=flat(slot), in0=flat(placef), scalar=float(CAP), in1=flat(slot),
                                                  op0=ALU.mult, op1=ALU.add))
                keep(k, v, v.tensor_tensor(slot[:], slot[:], kept[:], ALU.mult))
                keep(k, v, v.tensor_copy(gather[:], slot[:]))
                keep(k, v, v.tensor_scalar(kept[:], kept[:], -1.0, 1.0, ALU.mult, ALU.add))
                keep(k, v, v.tensor_tensor(spare[:], spare[:], kept[:], ALU.mult))
                keep(k, v, v.tensor_tensor(slot[:], slot[:], spare[:], ALU.add))
                keep(k, v, v.tensor_copy(scatter[:], slot[:]))
        ready.total += 1


def sixteen_experts(k, A, xt, weights, scatter, gather, back):
    nc = k.nc
    sent = nc.dram_tensor("experts_in", [E0 * CAP + 2 * TOKENS, D], F32, kind="Internal").ap()
    got = nc.dram_tensor("experts_out", [E0 * CAP, D], F32, kind="Internal").ap()
    S = {name: k.sig("expert_" + name) for name in (
        "zeroed", "sent", "loaded_even", "loaded_odd", "turned", "input", "up", "gelu", "down", "biased", "scaled", "stored_even", "stored_odd", "back")}
    LOADED, LOADS = ("loaded_even", "loaded_odd"), 4 * 16
    STORED = ("stored_even", "stored_odd")
    with ExitStack() as ctx:
        zeros = k.sb("expert_zeros", [P, E0 * CAP * D // P], ctx=ctx)
        rows = k.sb("expert_rows", [P, 2, D], ctx=ctx)
        inputs = k.sb("expert_input", [P, 2, P], ctx=ctx)
        w1 = k.sb("expert_w1", [P, 2, F0], ctx=ctx)
        w2 = k.sb("expert_w2", [P, 2, FB0, D], ctx=ctx)
        b2 = k.sb("expert_b2", [P, 2, D], ctx=ctx)
        hidden = k.sb("expert_hidden", [P, 2, FB0, P], ctx=ctx)
        biased = k.sb("expert_biased", [P, 2, D], ctx=ctx)
        result = k.sb("expert_result", [P, 2, D], ctx=ctx)
        with nc.Block() as block:
            @block.vector
            def _(v):
                keep(k, v, v.memset(zeros[:], 0.0))
        with nc.Block() as block:
            @block.sync
            def _(sp):
                sp.dma_start(sent[0:E0 * CAP, :].rearrange("(p r) d -> p (r d)", p=P), zeros[:]) \
                  .then_inc(S["zeroed"].sem, 16)
                sp.wait_ge(S["zeroed"].sem, 16)

            @block.gpsimd
            def _(pool):
                pool.wait_ge(S["zeroed"].sem, 16)
                for t in range(TT):
                    for n in range(2):
                        pool.indirect_dma_start(
                            out=sent, out_offset=bass.IndirectOffsetOnAxis(ap=scatter[:, t, n:n + 1], axis=0),
                            in_=xt[:, t, :], in_offset=None).then_inc(S["sent"].sem, 16)
                pool.wait_ge(S["sent"].sem, 2 * TT * 16)

        def at(name, e, n, per=1):
            return S[name].at(n) + e * per

        def run(engine, step):
            step(engine, 0, 0, True)
            step(engine, 1, 1, True)
            with engine.Fori(1, E0 // 2) as m:
                for r in range(2):
                    step(engine, m * 2 + r, r, False)

        def sync_step(sp, e, r, first):
            if not first:
                sp.wait_ge(S["scaled"].sem, at("scaled", e, -1))
            for tile, source in ((rows[:, r, :], sent[ds(e * CAP, CAP), :]),
                                 (w1[:, r, :], A["fc1"][ds(e, 1)].squeeze(0)),
                                 (w2[:, r], A["fc2"][ds(e, 1)].squeeze(0)),
                                 (b2[:, r, :], A["fc2_b"][ds(e, 1)].squeeze(0).partition_broadcast(P))):
                sp.dma_start(tile, source).then_inc(S[LOADED[r]].sem, 16)

        def tensor_step(pe, e, r, first):
            pe.wait_ge(S[LOADED[r]].sem, at(LOADED[r], e, LOADS - r * LOADS // 2, LOADS // 2))
            pe.transpose(k.ps[:, r, 0:P], rows[:, r, :], k.ident[:]).then_inc(S["turned"].sem, 1)
            pe.wait_ge(S["input"].sem, at("input", e, 1))
            if not first:
                pe.wait_ge(S["gelu"].sem, at("gelu", e, -1))
            for f in range(FB0):
                last = pe.matmul(k.ps[:, 2 + r, f * P:(f + 1) * P], w1[:, r, f * P:(f + 1) * P], inputs[:, r, :],
                                 start=True, stop=True)
            last.then_inc(S["up"].sem, 1)
            pe.wait_ge(S["gelu"].sem, at("gelu", e, 1))
            if not first:
                pe.wait_ge(S["biased"].sem, at("biased", e, -1))
            for f in range(FB0):
                last = pe.matmul(k.ps[:, 4 + r, 0:D], hidden[:, r, f, :], w2[:, r, f, :], start=f == 0,
                                 stop=f == FB0 - 1)
            last.then_inc(S["down"].sem, 1)

        def vector_step(v, e, r, first):
            v.wait_ge(S["turned"].sem, at("turned", e, 1))
            v.tensor_copy(inputs[:, r, :], k.ps[:, r, 0:P]).then_inc(S["input"].sem, 1)
            v.wait_ge(S["down"].sem, at("down", e, 1))
            v.tensor_tensor(biased[:, r, :], k.ps[:, 4 + r, 0:D], b2[:, r, :], ALU.add).then_inc(S["biased"].sem, 1)
            v.wait_ge(S["biased"].sem, at("biased", e, 1))
            if not first:
                v.wait_ge(S[STORED[r]].sem, at(STORED[r], e, -8 * r, 8))
            v.tensor_scalar(result[:, r, :], biased[:, r, :], KEEP, None, ALU.mult).then_inc(S["scaled"].sem, 1)

        def scalar_step(act, e, r, first):
            act.wait_ge(S["up"].sem, at("up", e, 1))
            for f in range(FB0):
                last = act.activation(hidden[:, r, f, :], k.ps[:, 2 + r, f * P:(f + 1) * P], ACT.Gelu,
                                      bias=k.cols[:, ds(e * FB0 + sum(COL_N[:-1]) + f, 1)])
            last.then_inc(S["gelu"].sem, 1)

        def pool_step(pool, e, r, first):
            pool.wait_ge(S["scaled"].sem, at("scaled", e, 1))
            pool.dma_start(got[ds(e * CAP, CAP), :], result[:, r, :]).then_inc(S[STORED[r]].sem, 16)

        with nc.Block() as block:
            @block.sync
            def _(sp):
                run(sp, sync_step)

            @block.tensor
            def _(pe):
                run(pe, tensor_step)

            @block.vector
            def _(v):
                run(v, vector_step)

            @block.scalar
            def _(act):
                run(act, scalar_step)

            @block.gpsimd
            def _(pool):
                run(pool, pool_step)
                for name in STORED:
                    pool.wait_ge(S[name].sem, 16 * E0 // 2)
                for t in range(TT):
                    for n in range(2):
                        pool.indirect_dma_start(
                            out=back[:, t, n, :], out_offset=None, in_=got,
                            in_offset=bass.IndirectOffsetOnAxis(ap=gather[:, t, n:n + 1], axis=0)) \
                            .then_inc(S["back"].sem, 16)
                pool.wait_ge(S["back"].sem, 2 * TT * 16)


def causal_layer(k, A):
    with ExitStack() as outer:
        hidden = k.sb("hidden", [P, TT, D], ctx=outer)
        normed = k.sb("hidden_normed", [P, TT, D], ctx=outer)
        turned = k.sb("hidden_turned", [P, TOKENS], ctx=outer)
        layernorm_rows(k, k.x[:], hidden[:])
        layernorm_rows(k, hidden[:], normed[:])
        transpose_rows(k, normed, turned, k.col("L0_ffn_ln1_w"), k.col("L0_ffn_ln1_b"))
        with ExitStack() as ctx:
            values = k.sb("values_by_head", [P, TT, H0 * 32], ctx=ctx)
            context = k.sb("attention_context", [P, TT, D], ctx=ctx)
            with k.nc.Block() as block:
                @block.vector
                def _(v):
                    keep(k, v, v.memset(values[:], 0.0))
                    keep(k, v, v.memset(values[:].rearrange("p t (h c) -> p t h c", h=H0)[:, :, :, HD0:HD0 + 1], 1.0))

            def take_values(v, rows):
                to = values[:].rearrange("p t (h c) -> p t h c", h=H0)
                for t in range(TT):
                    keep(k, v, v.tensor_tensor(to[:, t, :, 0:HD0], rows[:, t, :].rearrange("p (h c) -> p h c", h=H0),
                                               k.row("L0_ffn_v_b").rearrange("p (h c) -> p h c", h=H0), ALU.add))
            project_rows(k, turned, k.square("L0_ffn_v_w"), take_values)
            causal_attention(k, turned, values, context)
            transpose_rows(k, context, turned)

        def take_output(v, rows):
            keep(k, v, v.tensor_tensor(hidden[:], hidden[:], rows, ALU.add))
            keep(k, v, v.tensor_tensor(hidden[:], hidden[:], k.row_of_tiles("L0_ffn_o_b", TT), ALU.add))
        project_rows(k, turned, k.square("L0_ffn_o_w"), take_output)
        layernorm_rows(k, hidden[:], normed[:], gain=k.row("L0_ffn_ln2_w"), shift=k.row("L0_ffn_ln2_b"))
        transpose_rows(k, normed, turned)
        with ExitStack() as ctx:
            weights = k.sb("expert_weights", [P, TT, 2], ctx=ctx)
            scatter = k.sb("scatter_rows", [P, TT, 2], U32, ctx=ctx)
            gather = k.sb("gather_rows", [P, TT, 2], U32, ctx=ctx)
            router = k.sb("router", [P, E0], ctx=ctx)
            back = k.sb("experts_back", [P, TT, 2, D], ctx=ctx)
            loaded = k.sig("router_loaded")
            with k.nc.Block() as block:
                @block.sync
                def _(sp):
                    sp.dma_start(router[:], A["router0"]).then_inc(loaded.sem, 16)
                    sp.wait_ge(loaded.sem, 16)
            route(k, normed, turned, router, weights, scatter, gather)
            sixteen_experts(k, A, normed, weights, scatter, gather, back)
            with k.nc.Block() as block:
                @block.vector
                def _(v):
                    over = [P, TT, D]
                    keep(k, v, v.tensor_tensor(k.x[:], k.x[:], hidden[:], ALU.add))
                    for n in range(2):
                        keep(k, v, v.tensor_tensor(normed[:], back[:, :, n, :],
                                                   weights[:, :, n:n + 1].to_broadcast(over), ALU.mult))
                        keep(k, v, v.tensor_tensor(k.x[:], k.x[:], normed[:], ALU.add))



def dense_experts(k, A):
    nc = k.nc
    S = {name: k.sig("dense_" + name) for name in (
        "loaded", "router_up", "router_gelu", "router_down", "up", "gelu", "down", "added", "counted")}
    with ExitStack() as ctx:
        sb = lambda name, shape, dtype=F32: k.sb(name, shape, dtype, ctx=ctx)
        normed = sb("dense_normed", [P, TT, D])
        y = sb("dense_turned", [P, TOKENS])
        rw1 = sb("router_w1", [P, R1])
        rw2 = sb("router_w2", [P, RB1, E1])
        rb2 = sb("router_b2", [P, E1])
        be2 = sb("dense_b2", [E1, D])
        w1 = sb("dense_w1", [P, E1, F1])
        w2 = sb("dense_w2", [P, E1, FB1, D])
        hidden = sb("dense_hidden", [P, 2, FB1, TOKENS])
        logits = sb("dense_logits", [P, TT, 8])
        best = sb("dense_best", [P, TT, 8])
        place = sb("dense_place", [P, TT, 8], U32)
        placef = sb("dense_placef", [P, TT, 2])
        probs = sb("dense_probs", [P, TT, E1])
        total = sb("dense_total", [P, TT, 1])
        chosen = sb("dense_chosen", [P, 2, TT, E1])
        expert = sb("dense_expert", [P, E1])
        weights_t = sb("dense_weights_turned", [E1, TOKENS])
        layernorm_rows(k, k.x[:], normed[:])
        transpose_rows(k, normed, y)
        with nc.Block() as block:
            @block.sync
            def _(sp):
                for tile, source in ((rw1[:], A["rW1"]), (rw2[:], A["rW2"]),
                                     (rb2[:], A["rb2"][0].partition_broadcast(P)), (be2[:], A["be2"]),
                                     (w1[:], A["We1"].rearrange("e d f -> d e f")),
                                     (w2[:], A["We2"].rearrange("e p f d -> p e f d"))):
                    sp.dma_start(tile, source).then_inc(S["loaded"].sem, 16)
                sp.wait_ge(S["loaded"].sem, 96)

            @block.gpsimd
            def _(pool):
                pool.iota(expert[:], [[1, E1]], base=0, channel_multiplier=0,
                          allow_small_or_imprecise_dtypes=True).then_inc(S["counted"].sem, 1)
        with nc.Block() as block:
            @block.tensor
            def _(pe):
                for f in range(RB1):
                    for c in range(2):
                        pe.matmul(k.ps[:, 2 * f + c, :], rw1[:, f * P:(f + 1) * P], y[:, c * 512:(c + 1) * 512],
                                  start=True, stop=True).then_inc(S["router_up"].sem, 1)
                pe.wait_ge(S["router_gelu"].sem, RB1)
                for t in range(TT):
                    for f in range(RB1):
                        last = pe.matmul(k.ps[:, 4, t * E1:(t + 1) * E1], hidden[:, 0, f, t * P:(t + 1) * P],
                                         rw2[:, f, :], start=f == 0, stop=f == RB1 - 1)
                last.then_inc(S["router_down"].sem, 1)

            @block.scalar
            def _(act):
                for f in range(RB1):
                    act.wait_ge(S["router_up"].sem, 2 * f + 2)
                    act.activation(hidden[:, 0, f, :].rearrange("p (b c) -> p b c", b=2), k.ps[:, 2 * f:2 * f + 2, :],
                                   ACT.Gelu, bias=k.col("L1_ffn_rb1", f)).then_inc(S["router_gelu"].sem, 1)

            @block.vector
            def _(v):
                keep(k, v, v.memset(logits[:], NEG))
                v.wait_ge(S["router_down"].sem, 1)
                keep(k, v, v.tensor_tensor(logits[:, :, 0:E1],
                                           k.ps[:, 4, 0:TT * E1].rearrange("p (t e) -> p t e", e=E1),
                                           rb2[:].unsqueeze(1).to_broadcast([P, TT, E1]), ALU.add))
                for t in range(TT):
                    keep(k, v, v.max(best[:, t, :], logits[:, t, :]))
                    keep(k, v, v.max_index(place[:, t, :], best[:, t, :], logits[:, t, :]))
                keep(k, v, v.tensor_copy(placef[:], place[:, :, 0:2]))
                keep(k, v, v.tensor_tensor(probs[:], logits[:, :, 0:E1], best[:, :, 0:1].to_broadcast([P, TT, E1]),
                                           ALU.subtract))
                for n in range(2):
                    keep(k, v, v.tensor_tensor(chosen[:, n], expert[:].unsqueeze(1).to_broadcast([P, TT, E1]),
                                               placef[:, :, n:n + 1].to_broadcast([P, TT, E1]), ALU.is_equal))
                keep(k, v, v.tensor_tensor(chosen[:, 0], chosen[:, 0], chosen[:, 1], ALU.add))
        with nc.Block() as block:
            @block.scalar
            def _(act):
                act.activation(probs[:], probs[:], ACT.Exp).then_inc(S["counted"].sem, 1)

            @block.vector
            def _(v):
                v.wait_ge(S["counted"].sem, 2)
                keep(k, v, v.reduce_sum(total[:].squeeze(2), probs[:], axis=AX))
                keep(k, v, v.reciprocal(total[:], total[:]))
                keep(k, v, v.tensor_tensor(probs[:], probs[:], total[:].to_broadcast([P, TT, E1]), ALU.mult))
                keep(k, v, v.tensor_tensor(probs[:], probs[:], chosen[:, 0], ALU.mult))
        with nc.Block() as block:
            @block.tensor
            def _(pe):
                for t in range(TT):
                    pe.transpose(k.ps[0:E1, t // 4, t % 4 * P:(t % 4 + 1) * P], probs[:, t, :],
                                 k.ident[:]).then_inc(S["down"].sem, 1)

            @block.vector
            def _(v):
                v.wait_ge(S["down"].sem, TT)
                keep(k, v, v.tensor_copy(weights_t[:].rearrange("e (b c) -> e b c", b=2), k.ps[0:E1, 0:2, :]))
        S["down"].total += TT

        def take_bias(v, rows):
            keep(k, v, v.tensor_tensor(k.x[:], k.x[:], rows, ALU.add))
        project_rows(k, weights_t, be2[:], take_bias)

        with nc.Block() as block:
            @block.tensor
            def _(pe):
                def up(e):
                    for f in range(FB1):
                        n = FB1 * e + f
                        if n >= 2:
                            pe.wait_ge(S["gelu"].sem, n - 1)
                        for c in range(2):
                            last = pe.matmul(k.ps[:, 2 * (f % 2) + c, :], w1[:, e, f * P:(f + 1) * P],
                                             y[:, c * 512:(c + 1) * 512], start=True, stop=True)
                        last.then_inc(S["up"].sem, 1)

                def down(e):
                    pe.wait_ge(S["gelu"].sem, FB1 * (e + 1))
                    if e >= 2:
                        pe.wait_ge(S["added"].sem, TT * (e - 1))
                    for t in range(TT):
                        for f in range(FB1):
                            last = pe.matmul(k.ps[:, 4 + 2 * (e % 2) + t // 4, t % 4 * P:(t % 4 + 1) * P],
                                             hidden[:, e % 2, f, t * P:(t + 1) * P], w2[:, e, f, :], start=f == 0,
                                             stop=f == FB1 - 1)
                        if t % 4 == 3:
                            last.then_inc(S["down"].sem, 1)
                up(0)
                for e in range(1, E1):
                    up(e)
                    down(e - 1)
                down(E1 - 1)

            @block.scalar
            def _(act):
                for e in range(E1):
                    for f in range(FB1):
                        act.wait_ge(S["up"].sem, FB1 * e + f + 1)
                        if e >= 2:
                            act.wait_ge(S["down"].sem, S["down"].at(2 * (e - 1)))
                        act.activation(hidden[:, e % 2, f, :].rearrange("p (b c) -> p b c", b=2),
                                       k.ps[:, 2 * (f % 2):2 * (f % 2) + 2, :], ACT.Gelu,
                                       bias=k.col("L1_ffn_be1", e * FB1 + f)).then_inc(S["gelu"].sem, 1)

            @block.vector
            def _(v):
                for e in range(E1):
                    for t in range(TT):
                        v.wait_ge(S["down"].sem, S["down"].at(2 * e + t // 4 + 1))
                        if e:
                            v.wait_ge(S["added"].sem, TT * (e - 1) + t + 1)
                        v.scalar_tensor_tensor(out=k.x[:, t, :],
                                               in0=k.ps[:, 4 + 2 * (e % 2) + t // 4, t % 4 * P:(t % 4 + 1) * P],
                                               scalar=probs[:, t, e:e + 1], in1=k.x[:, t, :], op0=ALU.mult,
                                               op1=ALU.add).then_inc(S["added"].sem, 1)



def latents_turned(k):
    with ExitStack() as ctx:
        normed = k.sb("latents_normed", [P, TT, D], ctx=ctx)
        layernorm_rows(k, k.x[:], normed[:])
        layernorm_rows(k, normed[:], normed[:])
        transpose_rows(k, normed, k.zT[:, LAT0:REST0], k.col("L1_xcond_ln2_w"), k.col("L1_xcond_ln2_b"))
    with k.nc.Block() as block:
        @block.vector
        def _(v):
            modulation, lat = k.stat[:, 0, 0:1], k.zT[:, LAT0:REST0]
            keep(k, v, v.tensor_scalar(modulation, k.col("cond_1024"), 1.0, None, ALU.add))
            keep(k, v, v.tensor_scalar(lat, lat, modulation, k.col("cond_1024"), ALU.mult, ALU.add))
            for part in (k.zT[:, 0:LAT0], k.zT[:, REST0:KEYS]):
                keep(k, v, v.tensor_scalar(part, part, k.col("L1_xcond_ln1_w"), k.col("L1_xcond_ln1_b"),
                                           ALU.mult, ALU.add))


def perceiver_attention(k, A, rows):
    nc = k.nc
    S = {name: k.sig(name) for name in (
        "weights", "staged", "vsource", "kproj", "khigh", "klow", "vproj", "vready", "vodd",
        "score", "expd", "pv", "counted", "fill", "peak", "qproj", "qhigh", "qlow", "peaked", "shifted",
        "shift_row", "folded", "denominators", "inverted", "evacuated", "output", "summed")}
    rate = {"staged": 2, "kproj": 1, "khigh": 1, "klow": 1, "vready": 1, "score": 4, "expd": 4, "pv": 2,
            "counted": 2, "fill": 4, "peak": 4}
    of_rest = {"kproj": 0, "khigh": 0, "klow": 0, "fill": 1, "peak": 1}
    per = {name: n * NS + of_rest.get(name, n) for name, n in rate.items()}

    with ExitStack() as ctx:
        keys = [k.sb("keys", [P, STEPS * STEP], F32R, ctx=ctx) for _ in range(2)]
        key_a = k.sb("key_high_low", [P, 2, STEP], F32R, ctx=ctx)
        key_b = k.sb("key_high_one", [P, 2, STEP], F32R, ctx=ctx)
        source = k.sb("value_source", [P, 2, STEP], ctx=ctx)
        value = k.sb("value_step", [P, 2, 2, HD1], ctx=ctx)
        value_rest = k.sb("value_rest", [P, HD1], ctx=ctx)
        value_odd = k.sb("value_odd_head", [P, STEPS, 2 * HD1], ctx=ctx)
        q_a = [k.sb("query_high_high", [P, TOKENS], F32R, ctx=ctx) for _ in range(2)]
        q_b = [k.sb("query_low_shift", [P, TOKENS], F32R, ctx=ctx) for _ in range(2)]
        probs = k.sb("probs", [P, 4, 512], ctx=ctx)
        total = k.sb("probs_total", [P, 4, 512], ctx=ctx)
        head = k.sb("head_output", [P, 2, 512], ctx=ctx)
        inverse = k.sb("inverse_sums", [P, TT], ctx=ctx)
        peaks = k.sb("peaks", [P, TT, STEPS], ctx=ctx)
        peak = k.sb("peak_columns", [P, 64 + TT], ctx=ctx)
        wq = k.sb("wq", [P, 2, P], ctx=ctx)
        wk = k.sb("wk", [P, 2, P], ctx=ctx)
        wo = k.sb("wo", [P, 2, P], ctx=ctx)
        wv = k.sb("wv", [P, P], ctx=ctx)
        scores = k.ps[:, 0:2, :]
        out = k.ps[:, 2:4, :]
        fills = k.ps[:, 4:6, :]
        kbank, vbank = k.ps[:, 6, :], k.ps[:, 7, :]
        between = k.ps[:, 6:8, :]
        latents = k.zT[:, LAT0:REST0]

        cleared = k.sig("cleared")
        with nc.Block() as block:
            @block.vector
            def _(v):
                v.memset(key_b[:].bitcast(F32), 0.0).then_inc(cleared.sem, 1)
                v.memset(key_a[:].bitcast(F32), 0.0).then_inc(cleared.sem, 1)
                v.memset(peak[:], 0.0).then_inc(cleared.sem, 1)
                for q in q_b:
                    v.memset(q[:].bitcast(F32), 0.0).then_inc(cleared.sem, 1)
                v.wait_ge(cleared.sem, cleared.at(5))
                v.memset(key_b[64:65].bitcast(F32), 1.0).then_inc(cleared.sem, 1)
                for tile in keys:
                    v.memset(tile[:, KEYS:STEPS * STEP].bitcast(F32), 0.0).then_inc(cleared.sem, 1)
                v.memset(value_odd[:, NS, :], 0.0).then_inc(cleared.sem, 1)
                v.memset(value_rest[:], 0.0).then_inc(cleared.sem, 1)
                v.wait_ge(cleared.sem, cleared.at(10))
                v.sem_inc(S["score"].sem, 4)
        cleared.total += 10
        S["score"].total += 4

        def at(name, h, j, n):
            before = 1 if name in ("fill", "peak") else 0
            return S[name].at(n) + before + h * per[name] + j * rate[name]

        def inc(name, instruction, n=1):
            instruction.then_inc(S[name].sem, n)

        def wait(engine, name, value):
            if not isinstance(value, int) or value > 0:
                engine.wait_ge(S[name].sem, value)

        def width(j):
            return (LAST if isinstance(j, int) and j == NS else STEP)


        def stage_keys(pool, h, hp, j, r):
            wait(pool, "score", at("score", h, j, -4))
            for rows_, tile in ((slice(0, P), key_a), (slice(0, HD1), key_b)):
                inc("staged", pool.tensor_copy(tile[rows_, r, :], keys[hp][rows_, ds(j * STEP, STEP)]))

        def stage_odd_value(pool, h, j, r):
            wait(pool, "pv", at("pv", h, j, -2))
            inc("vready", pool.tensor_copy(value[:, r].rearrange("p a d -> p (a d)"),
                                           value_odd[:, ds(j, 1), :].squeeze(1)))

        def stage_source(act, pair, j, r):
            w = width(j)
            wait(act, "vproj", S["vproj"].at(-1) + pair * STEPS + j)
            inc("vsource", act.activation(source[:, r, 0:w], k.zT[:, ds(j * STEP, w)], ACT.Copy))

        def keep_values(act, pair, h, j, r):
            wait(act, "vproj", S["vproj"].at(1) + pair * STEPS + j)
            wait(act, "pv", at("pv", h, j, -2))
            if width(j) == LAST:
                inc("vready", act.activation(value_rest[0:LAST, :], vbank[0:LAST, 0:HD1], ACT.Copy))
                inc("vodd", act.activation(value_odd[0:LAST, NS, 0:HD1], vbank[0:LAST, HD1:P], ACT.Copy))
                return
            made = vbank[:, 0:2 * P].rearrange("p (a h d) -> p a h d", a=2, h=2)
            inc("vready", act.activation(value[:, r], made[:, :, 0, :], ACT.Copy))
            inc("vodd", act.activation(value_odd[:, ds(j, 1), :].rearrange("p o (a d) -> p (o a) d", a=2),
                                       made[:, :, 1, :], ACT.Copy))

        def make_values(pe, pair, j, r):
            rows_ = min(width(j), P)
            wait(pe, "vsource", S["vsource"].at(1) + pair * STEPS + j)
            wait(pe, "vodd", S["vodd"].at(0) + pair * STEPS + j)
            for a in range(width(j) // rows_ if rows_ == P else 1):
                last = pe.matmul(vbank[0:rows_, a * P:(a + 1) * P], source[:, r, a * rows_:(a + 1) * rows_], wv[:],
                                 start=True, stop=True)
            inc("vproj", last)

        def score_unit(pe, hp, r, keys_, bank, c):
            cols = slice(c * 512, (c + 1) * 512)
            rows_ = slice(0, keys_.stop - keys_.start)
            pe.matmul(scores[rows_, bank, :], key_a[:, r, keys_], q_a[hp][:, cols], start=True, stop=False)
            return pe.matmul(scores[rows_, bank, :], key_b[:, r, keys_], q_b[hp][:, cols], start=False, stop=True)

        def make_scores(pe, h, hp, j, r, c):
            if c == 0:
                wait(pe, "staged", at("staged", h, j, 2))
            for a in range(2):
                wait(pe, "expd", at("expd", h, j, 2 * c + a - 1))
                inc("score", score_unit(pe, hp, r, slice(a * P, (a + 1) * P), a, c))

        def make_rest_scores(pe, h, hp):
            wait(pe, "staged", at("staged", h, NS, 2))
            for c in range(2):
                wait(pe, "expd", at("expd", h, NS, c - 1))
                inc("score", score_unit(pe, hp, NS % 2, slice(0, LAST), c, c), 2)

        def add_products(pe, h, j, r, c, start, last_step):
            wait(pe, "vready", at("vready", h, j, 1))
            wait(pe, "expd", at("expd", h, j, 2 * c + 2))
            for a in range(2):
                last = pe.matmul(out[a * HD1:(a + 1) * HD1, c, :], value[:, r, a, :], probs[:, 2 * c + a, :],
                                 start=start, stop=last_step and a != c)
            inc("pv", last)

        def add_rest_products(pe, h, hp):
            wait(pe, "vready", at("vready", h, NS, 1))
            wait(pe, "expd", at("expd", h, NS, 4))
            values = value[:, NS % 2, 0, :] if hp else value_rest[:]
            for c in range(2):
                last = pe.matmul(out[c * HD1:(c + 1) * HD1, c, :], values, probs[:, 2 * c, :], start=False, stop=True)
            inc("pv", last, 2)

        def fill_peaks(pe, g, gp, j, part):
            if part == 0:
                wait(pe, "khigh", at("khigh", g, j, 1))
                wait(pe, "klow", at("klow", g, j, 1))
            for b in range(2):
                wait(pe, "peak", at("peak", g, j, max(0, b - 1) if first_fill(j, part) else 2 * part + b - 1))
                for n in range(2):
                    t = 4 * part + 2 * b + n
                    last = pe.matmul(fills[:, b, n * STEP:(n + 1) * STEP], q_a[gp][:, t * P:(t + 1) * P],
                                     keys[gp][:, ds(j * STEP, STEP)], start=True, stop=True)
                inc("fill", last)

        def first_fill(j, part):
            return isinstance(j, int) and j == 0 and part == 0

        def fill_rest_peaks(pe, g, gp):
            wait(pe, "klow", at("klow", g, 0, 1))
            for t in range(TT):
                last = pe.matmul(fills[:, 0, t * LAST:(t + 1) * LAST], q_a[gp][:, t * P:(t + 1) * P],
                                 keys[gp][:, REST0:KEYS], start=True, stop=True)
            inc("fill", last)

        def make_keys(pe, g, gp, j, first):
            wait(pe, "khigh", at("khigh", g, j, 0))
            wait(pe, "klow", at("klow", g, j, 0))
            last = pe.matmul(kbank[:, 0:STEP], wk[:, gp, :], k.zT[:, ds(j * STEP, STEP)], start=True, stop=True)
            if first:
                last = pe.matmul(kbank[:, STEP:STEP + LAST], wk[:, gp, :], k.zT[:, REST0:KEYS], start=True, stop=True)
            inc("kproj", last)


        def tensor_step(pe, pair, h, hp, g, gp, j, r, first, before):
            if h is not None:
                make_scores(pe, h, hp, j, r, 0)
                if first and before:
                    share_of_rows(pe, h - 1, 1 - hp)
                if first:
                    make_scores(pe, h, hp, j, r, 1)
                if first and before:
                    sum_exponentials(pe, h - 1)
                if first and hp == 0:
                    if g is not None or before:
                        wait(pe, "qlow", S["qlow"].at(1) + (h + 1 if g is not None else h))
                    make_values(pe, pair, 0, 0)
            if g is not None:
                if first and before:
                    wait(pe, "inverted", S["inverted"].at(0) + h)
                if first:
                    wait(pe, "qlow", S["qlow"].at(1) + g)
                make_keys(pe, g, gp, j, first)
            if not first:
                if h is not None:
                    add_products(pe, h, j - 1, 1 - r, 1, isinstance(j, int) and j == 1, False)
                if g is not None:
                    fill_peaks(pe, g, gp, j - 1, 1)
            if h is not None:
                if not first:
                    make_scores(pe, h, hp, j, r, 1)
                if first and before:
                    wait(pe, "evacuated", S["evacuated"].at(0) + h)
                add_products(pe, h, j, r, 0, first, isinstance(j, int) and j == NS - 1)
            if g is not None:
                if first:
                    if before:
                        wait(pe, "summed", S["summed"].at(0) + h)
                    fill_rest_peaks(pe, g, gp)
                fill_peaks(pe, g, gp, j, 0)
            if h is not None and hp == 0:
                make_values(pe, pair, j + 1, 1 - r)

        def scalar_step(act, pair, h, hp, g, gp, j, r, first):
            if h is not None:
                if hp == 0 and not first:
                    stage_source(act, pair, j + 1, 1 - r)
                exponentials(act, h, j, 0)
                if hp == 0 and first:
                    keep_values(act, pair, h, 0, 0)
            if g is not None:
                wait(act, "kproj", at("kproj", g, j, 1))
                if first:
                    act.activation(keys[gp][:, REST0:KEYS], kbank[:, STEP:STEP + LAST], ACT.Copy)
                inc("khigh", act.activation(keys[gp][:, ds(j * STEP, STEP)], kbank[:, 0:STEP], ACT.Copy))
            if h is not None:
                exponentials(act, h, j, 1)
                if hp == 0:
                    keep_values(act, pair, h, j + 1, 1 - r)

        def exponentials(act, h, j, c):
            for a in range(2):
                wait(act, "score", at("score", h, j, 2 * c + a + 1))
                wait(act, "pv", at("pv", h, j, c - 1))
                wait(act, "counted", at("counted", h, j, c - 1))
                inc("expd", act.activation(probs[:, 2 * c + a, :], scores[:, a, :], ACT.Exp, scale=1.0 / 8.0))

        def rest_exponentials(act, h):
            for c in range(2):
                wait(act, "score", at("score", h, NS, 2 * c + 2))
                wait(act, "pv", at("pv", h, NS, c - 1))
                wait(act, "counted", at("counted", h, NS, c - 1))
                inc("expd", act.activation(probs[0:LAST, 2 * c, :], scores[0:LAST, c, :], ACT.Exp, scale=1.0 / 8.0), 2)

        def vector_step(v, h, hp, g, gp, j, r, first, before):
            if first and h is not None:
                if before:
                    wait(v, "folded", S["folded"].at(0) + h)
                    wait(v, "denominators", S["denominators"].at(0) + h)
                    inc("inverted", v.reciprocal(inverse[:], kbank[:, 0:TT]))
                count(v, h, j, 0, first)
            if g is not None:
                wait(v, "khigh", at("khigh", g, j, 1))
                if first:
                    rest = keys[gp][HD1:P, REST0:KEYS]
                    v.tensor_tensor(rest, kbank[HD1:P, STEP:STEP + LAST], rest.bitcast(F32), ALU.subtract)
                low = keys[gp][HD1:P, ds(j * STEP, STEP)]
                inc("klow", v.tensor_tensor(low, kbank[HD1:P, 0:STEP], low.bitcast(F32), ALU.subtract))
                if not first:
                    read_peak(v, g, j - 1, 2)
                    read_peak(v, g, j - 1, 3)
            if h is not None and not first:
                count(v, h, j, 0, first)
            if first and before:
                add_rows(v, h - 1)
            if g is not None:
                if first:
                    wait(v, "fill", at("fill", g, 0, 0))
                    inc("peak", v.reduce_max(peaks[:, :, NS:NS + 1].rearrange("p t o -> p (t o)"),
                                             fills[:, 0, 0:TT * LAST].rearrange("p (t w) -> p t w", w=LAST), axis=AX))
                read_peak(v, g, j, 0)
                read_peak(v, g, j, 1)
            if h is not None:
                count(v, h, j, 1, first)

        def read_peak(v, g, j, f):
            wait(v, "fill", at("fill", g, j, f + 1))
            inc("peak", v.reduce_max(peaks[:, 2 * f:2 * f + 2, ds(j, 1)].rearrange("p t o -> p (t o)"),
                                     fills[:, f % 2, :].rearrange("p (n w) -> p n w", n=2), axis=AX))

        def count(v, h, j, c, first):
            wait(v, "expd", at("expd", h, j, 2 * c + 2))
            units = slice(2 * c, 2 * c + 2)
            if first:
                inc("counted", v.tensor_copy(total[:, units, :], probs[:, units, :]))
            else:
                wait(v, "counted", at("counted", h, j, c - 1))
                inc("counted", v.tensor_tensor(total[:, units, :], total[:, units, :], probs[:, units, :], ALU.add))


        def load_weights(sp, h, slot):
            for tile, name in ((wq, "wq"), (wk, "wk")):
                sp.dma_start(tile[:, slot, :], A[name][ds(h, 1)].squeeze(0)).then_inc(S["weights"].sem, 16)

        def load_output_weights(sp, h, slot):
            sp.dma_start(wo[:, slot, :], A["wo"][ds(h, 1)].squeeze(0)).then_inc(S["weights"].sem, 16)

        def load_value_weights(sp, pair):
            sp.dma_start(wv[:], A["wv"][ds(pair, 1)].squeeze(0)).then_inc(S["weights"].sem, 16)

        def tensor_between(pe, pair, h, hp, g, gp, after, weights):
            if g is not None:
                fill_peaks(pe, g, gp, NS - 1, 1)
            if h is not None:
                make_rest_scores(pe, h, hp)
                add_products(pe, h, NS - 1, (NS - 1) % 2, 1, False, True)
                add_rest_products(pe, h, hp)
            if g is not None:
                wait(pe, "peaked", S["peaked"].at(2) + g * 2)
                for t in range(TT):
                    last = pe.transpose(fills[0:65, t // 4, t % 4 * P:(t % 4 + 1) * P], peak[:, t:t + 65], k.ident[:])
                inc("shifted", last)
            if after:
                wait(pe, "klow", at("klow", g, NS - 1, 1))
                if h is not None and hp == 0:
                    wait(pe, "vodd", S["vodd"].at(STEPS) + pair * STEPS)
                tensor_queries(pe, hp_of(gp), weights)
            if g is not None:
                wait(pe, "shift_row", S["shift_row"].at(1) + g)

        def hp_of(gp):
            return 1 - gp

        def tensor_queries(pe, slot, weights):
            wait(pe, "weights", weights)
            for c in range(2):
                last = pe.matmul(between[:, c, :], wq[:, slot, :], latents[:, c * 512:(c + 1) * 512], start=True,
                                 stop=True)
            inc("qproj", last)

        def scalar_queries(act, h, hp):
            wait(act, "qproj", S["qproj"].at(1) + h)
            inc("qhigh", act.activation(q_a[hp][:].rearrange("p (b c) -> p b c", b=2), between, ACT.Copy))

        def vector_queries(v, h, hp):
            wait(v, "qhigh", S["qhigh"].at(1) + h)
            inc("qlow", v.tensor_tensor(q_b[hp][0:HD1, :].rearrange("p (b c) -> p b c", b=2), between[0:HD1],
                                        q_a[hp][0:HD1, :].rearrange("p (b c) -> p b c", b=2).bitcast(F32),
                                        ALU.subtract))

        def scalar_between(act, next_pair, h, hp, g, gp, after):
            if h is not None:
                rest_exponentials(act, h)
                wait(act, "pv", at("pv", h, NS, 2))
                wait(act, "output", S["output"].at(0) + h)
                inc("evacuated", act.activation(head[:], out, ACT.Copy))
            if g is not None and gp == 0:
                stage_source(act, next_pair, 0, 0)
                stage_source(act, next_pair, 1, 1)
            if g is not None:
                wait(act, "shifted", S["shifted"].at(1) + g)
                inc("shift_row", act.activation(q_b[gp][64:65, :], fills[64:65].rearrange("p b c -> p (b c)"), ACT.Copy))
            if after:
                scalar_queries(act, g + 1, hp_of(gp))

        def vector_between(v, h, hp, g, gp, after):
            if g is not None:
                for f in range(2, 4):
                    read_peak(v, g, NS - 1, f)
                wait(v, "peak", at("peak", g, NS, 0))
                inc("peaked", v.reduce_max(peak[:, 64:64 + TT], peaks[:], axis=AX))
                wait(v, "peaked", S["peaked"].at(1) + g * 2)
                inc("peaked", v.tensor_scalar(peak[:, 64:64 + TT], peak[:, 64:64 + TT], -1.0, None, ALU.mult))
            if h is not None:
                wait(v, "expd", at("expd", h, NS, 4))
                wait(v, "counted", at("counted", h, NS, 0))
                some = total[0:LAST].rearrange("p (c a) q -> p c a q", a=2)[:, :, 0, :]
                inc("counted", v.tensor_tensor(some, some, probs[0:LAST].rearrange("p (c a) q -> p c a q", a=2)[:, :, 0, :],
                                               ALU.add), 2)
                wait(v, "counted", at("counted", h, NS, 2))
                half = total[:].rearrange("p (c a) q -> p c a q", a=2)
                inc("folded", v.tensor_tensor(half[:, :, 0, :], half[:, :, 0, :], half[:, :, 1, :], ALU.add))
            if after:
                vector_queries(v, g + 1, hp_of(gp))

        def sum_exponentials(pe, h):
            wait(pe, "folded", S["folded"].at(1) + h)
            wait(pe, "qlow", S["qlow"].at(min(h + 3, H1)) if isinstance(h, int) else S["qlow"].at(3) + h)
            for t in range(TT):
                last = pe.matmul(kbank[:, t:t + 1], total[:, t // 4 * 2, t % 4 * P:(t % 4 + 1) * P], k.ones[:, 0:1],
                                 start=True, stop=True)
            inc("denominators", last)

        def share_of_rows(pe, h, hp):
            wait(pe, "evacuated", S["evacuated"].at(1) + h)
            for t in range(TT):
                last = pe.matmul(fills[:, t // 4, t % 4 * P:(t % 4 + 1) * P],
                                 head[:, t // 4, t % 4 * P:(t % 4 + 1) * P], wo[:, hp, :], start=True, stop=True)
            inc("output", last)

        def add_rows(v, h):
            wait(v, "output", S["output"].at(1) + h)
            wait(v, "inverted", S["inverted"].at(1) + h)
            wait(v, "summed", S["summed"].at(0) + h)
            for t in range(TT):
                last = v.scalar_tensor_tensor(rows[:, t, :], fills[:, t // 4, t % 4 * P:(t % 4 + 1) * P],
                                              inverse[:, t:t + 1], rows[:, t, :], ALU.mult, ALU.add)
            inc("summed", last)

        PEELED = 3
        LOOPS = (H1 - 1 - PEELED) // 2
        WEIGHTS_FIRST, WEIGHTS_EVEN, WEIGHTS_ODD = 6 * 16, 3 * 16, 4 * 16

        def run(engine, head_part):
            head_part(engine, None, None, 1, 0, 0, True, False)
            head_part(engine, 0, 0, 0, 1, 1, True, False)
            with engine.Fori(0, LOOPS) as i:
                head_part(engine, i, i * 2 + 1, 1, i * 2 + 2, 0, True, True)
                head_part(engine, i + 1, i * 2 + 2, 0, i * 2 + 3, 1, True, True)
            for h in range(H1 - PEELED, H1):
                g = h + 1 if h + 1 < H1 else None
                head_part(engine, h // 2, h, h % 2, g, 1 - h % 2, h + 2 < H1, True)

        def steps(engine, step):
            step(0, 0, True)
            step(1, 1, False)
            with engine.Fori(1, NS // 2) as m:
                step(m * 2, 0, False)
                step(m * 2 + 1, 1, False)
            step(NS - 1, 0, False)

        with nc.Block() as block:
            @block.sync
            def _(sp):
                def part(sp, pair, h, hp, g, gp, after, before):
                    if h is None:
                        load_weights(sp, 0, 0)
                        load_weights(sp, 1, 1)
                        load_output_weights(sp, 0, 0)
                        load_value_weights(sp, 0)
                        return
                    if g is None:
                        return
                    if before:
                        wait(sp, "output", S["output"].at(0) + h)
                    else:
                        wait(sp, "kproj", at("kproj", h, NS, 0))
                    if after:
                        load_weights(sp, h + 2, hp)
                    load_output_weights(sp, g, gp)
                    if hp == 1:
                        load_value_weights(sp, pair + 1)
                run(sp, part)

            @block.gpsimd
            def _(pool):
                def part(pool, pair, h, hp, g, gp, after, before):
                    if h is None:
                        return
                    with pool.Fori(0, STEPS // 2) as m:
                        wait(pool, "khigh", at("khigh", h, NS, 0))
                        wait(pool, "klow", at("klow", h, NS, 0))
                        if hp == 1:
                            wait(pool, "vodd", S["vodd"].at(STEPS) + pair * STEPS)
                        for r in range(2):
                            stage_keys(pool, h, hp, m * 2 + r, r)
                            if hp == 1:
                                stage_odd_value(pool, h, m * 2 + r, r)
                run(pool, part)

            @block.tensor
            def _(pe):
                def part(pe, pair, h, hp, g, gp, after, before):
                    if h is None:
                        tensor_queries(pe, 0, S["weights"].at(WEIGHTS_FIRST))
                        weights = S["weights"].at(WEIGHTS_FIRST)
                    else:
                        weights = (S["weights"].at(WEIGHTS_FIRST) + pair * (WEIGHTS_EVEN + WEIGHTS_ODD) + WEIGHTS_EVEN
                                   + hp * WEIGHTS_ODD)
                    steps(pe, lambda j, r, first: tensor_step(pe, pair, h, hp, g, gp, j, r, first, before))
                    tensor_between(pe, pair, h, hp, g, gp, after, weights)
                run(pe, part)
                wait(pe, "weights", S["weights"].at(WEIGHTS_FIRST) + (H1 // 2 - 1) * (WEIGHTS_EVEN + WEIGHTS_ODD) + 16)
                sum_exponentials(pe, H1 - 1)
                share_of_rows(pe, H1 - 1, (H1 - 1) % 2)

            @block.scalar
            def _(act):
                def part(act, pair, h, hp, g, gp, after, before):
                    if h is None:
                        scalar_queries(act, 0, 0)
                    steps(act, lambda j, r, first: scalar_step(act, pair, h, hp, g, gp, j, r, first))
                    scalar_between(act, 0 if h is None else pair + 1, h, hp, g, gp, after)
                run(act, part)

            @block.vector
            def _(v):
                def part(v, pair, h, hp, g, gp, after, before):
                    if h is None:
                        vector_queries(v, 0, 0)
                    steps(v, lambda j, r, first: vector_step(v, h, hp, g, gp, j, r, first, before))
                    vector_between(v, h, hp, g, gp, after)
                run(v, part)
                wait(v, "denominators", S["denominators"].at(H1))
                inc("inverted", v.reciprocal(inverse[:], kbank[:, 0:TT]))
                add_rows(v, H1 - 1)
        for name, n in per.items():
            S[name].total += H1 * n
        for name, n in (("folded", H1), ("denominators", H1), ("inverted", H1), ("evacuated", H1), ("output", H1), ("summed", H1)):
            S[name].total += n


def build(nc, A, out, stages=(1, 2, 3, 4)):
    with ExitStack() as ctx:
        k = Core(nc, ctx)
        k.cols = k.sb("column_parameters", [P, sum(COL_N)])
        k.rows = k.sb("row_parameters", [P, len(ROWS), D])
        k.squares = k.sb("square_weights", [P, len(SQUARE), D])
        k.ident = k.sb("identity", [P, P])
        k.ones = k.sb("ones", [P, P])
        k.half = k.sb("minus_half", [P, CT])
        k.stat = k.sb("row_statistics", [P, 3, CT])
        k.norm_scratch = k.sb("norm_scratch", [P, TT * D])
        k.x = k.sb("x_rows", [P, TT, D])
        k.zT = k.sb("keys_normed_turned", [P, KEYS])
        load_constants(k, A)
        slot_attention(k, A, 1 in stages)
        if 2 in stages:
            causal_layer(k, A)
        if 3 in stages:
            latents_turned(k)
            perceiver_attention(k, A, k.x)
        if 4 in stages:
            dense_experts(k, A)
        stored = k.sig("stored")
        with nc.Block() as block:
            @block.sync
            def _(sp):
                sp.dma_start(out[0].rearrange("(t p) d -> p t d", p=P), k.x[:]).then_inc(stored.sem, 16)
                sp.wait_ge(stored.sem, 16)



def kernel(**inputs):
    import numpy as np
    import concourse.bacc as bacc
    from concourse.bass_utils import run_bass_kernel_spmd

    a = {name: np.asarray(value) for name, value in inputs.items()}

    def heads(w, n):
        t = w.reshape(n, HD1, D).transpose(0, 2, 1)
        return np.concatenate([t, t], axis=2)

    laid = {
        "x": a["x"],
        "ctx_1024": a["ctx_1024"],
        "cols": np.concatenate([a[name].reshape(n, P) for name, n in zip(COLS, COL_N)]).T,
        "rows": np.stack([a[name].reshape(D) for name in ROWS]),
        "squares": np.stack([a[name] for name in SQUARE], axis=1),
        "router0": a["L0_ffn_router_w"],
        "fc1": a["L0_ffn_fc1_w"],
        "fc2": a["L0_ffn_fc2_w"].reshape(E0, FB0, P, D).transpose(0, 2, 1, 3),
        "fc2_b": a["L0_ffn_fc2_b"],
        "wq": heads(a["L1_xcond_Wq"], H1),
        "wk": heads(a["L1_xcond_Wkv"][0:H1 * HD1], H1),
        "wv": a["L1_xcond_Wkv"][H1 * HD1:].reshape(H1 // 2, 2 * HD1, D).transpose(0, 2, 1),
        "wo": np.concatenate([a["L1_xcond_Wo"].T.reshape(H1, HD1, D)] * 2, axis=1),
        "rW1": a["L1_ffn_rW1"],
        "rW2": a["L1_ffn_rW2"].reshape(RB1, P, E1).transpose(1, 0, 2),
        "rb2": a["L1_ffn_rb2"].reshape(1, E1),
        "We1": a["L1_ffn_We1"],
        "We2": a["L1_ffn_We2"].reshape(E1, FB1, P, D).transpose(0, 2, 1, 3),
        "be2": a["L1_ffn_be2"],
    }
    nc = bacc.Bacc("TRN2", target_bir_lowering=False, num_devices=1)
    arrays, views = {}, {}
    for name, value in laid.items():
        value = np.ascontiguousarray(value)
        arrays["in_" + name] = value
        views[name] = nc.dram_tensor("in_" + name, value.shape, mybir.dt.from_np(value.dtype),
                                     kind="ExternalInput").ap()
    out = nc.dram_tensor("out", (1, TOKENS, D), F32, kind="ExternalOutput").ap()
    build(nc, views, out)
    result = run_bass_kernel_spmd(nc, [arrays], core_ids=[0])
    return result.results[0]["out"]
```

```python
import concourse.bass as bass
from concourse import mybir
from contextlib import ExitStack

F32 = mybir.dt.float32
F32R = mybir.dt.float32r
BF16 = mybir.dt.bfloat16
U32 = mybir.dt.uint32
ALU = mybir.AluOpType
ACT = mybir.ActivationFunctionType
AX = mybir.AxisListType.X
ds = bass.ds

P = 128
D = 128
TOKENS = 1024
TT = TOKENS // P
CTX = 6404
CT = CTX // P
REST = CTX - CT * P
EPS = 1e-5
NEG = -1e30

ITERATIONS = 3
EPS_ATTN = 1e-8
SLOT_SCALE = float(D) ** 0.5
PREP = 5

H0 = 16
HD0 = D // H0
GROUP = 4
NG = H0 // GROUP
E0 = 16
F0 = 512
FB0 = F0 // P
CAP = 2 * (-(-TOKENS // E0))
KEEP = 1.0 - 0.2

H1 = 16
HD1 = 64
KEYS = CTX + TOKENS
STEP = 2 * P
NS = KEYS // STEP
LAST = KEYS - NS * STEP
STEPS = NS + 1
assert STEPS % 2 == 0
LAT0 = CT * P
REST0 = LAT0 + TOKENS
assert CAP == P and REST0 == NS * STEP and LAST == REST and LAST % 2 == 0

E1 = 4
F1 = 512
FB1 = F1 // P
R1 = 256
RB1 = R1 // P

COLS = ["L0_xcond_lnkv_g", "L0_xcond_lnkv_b", "L0_xcond_bk", "L0_xcond_lnq_g", "L0_xcond_lnq_b", "L0_xcond_bq",
        "L0_xcond_lnm_g", "L0_xcond_lnm_b", "L0_xcond_b1", "L0_ffn_ln1_w", "L0_ffn_ln1_b", "L0_ffn_q_b",
        "L0_ffn_k_b", "L1_xcond_ln1_w", "L1_xcond_ln1_b", "L1_xcond_ln2_w", "L1_xcond_ln2_b", "cond_1024",
        "L1_ffn_rb1", "L1_ffn_be1", "L0_ffn_fc1_b"]
COL_N = [1] * 18 + [RB1, E1 * FB1, E0 * FB0]
ROWS = ["L0_xcond_q_mu", "L0_xcond_q_logsig", "L0_xcond_bv", "L0_xcond_bu", "L0_xcond_b2", "L0_xcond_lnp_g",
        "L0_xcond_lnp_b", "cond_1024", "L0_ffn_v_b", "L0_ffn_o_b", "L0_ffn_ln2_w", "L0_ffn_ln2_b"]
SQUARE = ["L0_xcond_wk", "L0_xcond_wv", "L0_xcond_wq", "L0_xcond_wu", "L0_xcond_w1", "L0_xcond_w2",
          "L0_ffn_q_w", "L0_ffn_k_w", "L0_ffn_v_w", "L0_ffn_o_w"]


class Signal:

    def __init__(self, sem):
        self.sem, self.total = sem, 0

    def at(self, n):
        return self.total + n

    def link(self, engine, instruction):
        self.total += 1
        instruction.then_inc(self.sem, 1)
        engine.wait_ge(self.sem, self.total)


class Core:

    def __init__(self, nc, ctx):
        self.nc, self.ctx, self.signals, self.names = nc, ctx, {}, 0
        self.ps = ctx.enter_context(nc.psum_tensor("banks", [P, 8, 512], F32))

    def sb(self, name, shape, dtype=F32, ctx=None):
        self.names += 1
        return (ctx or self.ctx).enter_context(self.nc.sbuf_tensor(f"{name}_{self.names}", shape, dtype))

    def sig(self, name):
        if name not in self.signals:
            self.signals[name] = Signal(self.ctx.enter_context(self.nc.semaphore(name)))
        return self.signals[name]

    def col(self, name, n=0):
        at = sum(COL_N[:COLS.index(name)]) + n
        return self.cols[:, at:at + 1]

    def row(self, name, parts=P):
        return self.rows[0:parts, ROWS.index(name), :]

    def row_of_tiles(self, name, tiles):
        return self.row(name).unsqueeze(1).to_broadcast([P, tiles, D])

    def square(self, name):
        return self.squares[:, SQUARE.index(name), :]


def load_constants(k, A, before):
    loaded, made = k.sig("constants_loaded"), k.sig("constants_made")
    with k.nc.Block() as block:
        @block.sync
        def _(sp):
            before(sp)
            sp.dma_start(k.cols[:], A["cols"]).then_inc(loaded.sem, 16)
            sp.dma_start(k.rows[:], A["rows"].partition_broadcast(P)).then_inc(loaded.sem, 16)
            sp.dma_start(k.squares[:], A["squares"]).then_inc(loaded.sem, 16)
            sp.dma_start(k.x[:], A["x"][0].rearrange("(t p) d -> p t d", p=P)).then_inc(loaded.sem, 16)

        @block.gpsimd
        def _(pool):
            pool.memset(k.ident[:], 0.0).then_inc(made.sem, 1)
            pool.memset(k.ones[:], 1.0).then_inc(made.sem, 1)
            pool.memset(k.half[:], -0.5).then_inc(made.sem, 1)
            pool.wait_ge(made.sem, made.at(3))
            pool.affine_select(out=k.ident[:], in_=k.ident[:], compare_op=ALU.not_equal, fill=1.0, base=0,
                               pattern=[[-1, P]], channel_multiplier=1).then_inc(made.sem, 1)
            pool.wait_ge(made.sem, made.at(4))
    loaded.total += 64
    made.total += 4


def layernorm_rows(k, src, dst, gain=None, shift=None):
    step, rooted = k.sig("norm_step"), k.sig("norm_rooted")
    over = [P, TT, D]
    variance = step.at(3)
    with k.nc.Block() as block:
        @block.vector
        def _(v):
            for t in range(TT):
                last = v.bn_stats(k.bn[:, t, :], src[:, t, :])
            step.link(v, last)
            for t in range(TT):
                last = v.bn_aggr(k.moments[:, t, :], k.bn[:, t, :])
            step.link(v, last)
            step.link(v, v.tensor_scalar(k.moments[:, 0:TT, 1], k.moments[:, 0:TT, 1], EPS, None, ALU.add))
            step.link(v, v.tensor_tensor(dst, src, k.moments[:, 0:TT, 0:1].to_broadcast(over), ALU.subtract))
            if gain is not None:
                step.link(v, v.tensor_tensor(dst, dst, gain.unsqueeze(1).to_broadcast(over), ALU.mult))
            v.wait_ge(rooted.sem, rooted.at(1))
            step.link(v, v.tensor_tensor(dst, dst, k.stat[:, 2, 0:TT].unsqueeze(2).to_broadcast(over), ALU.mult))
            if gain is not None:
                step.link(v, v.tensor_tensor(dst, dst, shift.unsqueeze(1).to_broadcast(over), ALU.add))

        @block.gpsimd
        def _(pool):
            pool.wait_ge(step.sem, variance)
            pool.tensor_tensor(k.stat[:, 2, 0:TT], k.moments[:, 0:TT, 1], k.half[:, 0:TT],
                               ALU.pow).then_inc(rooted.sem, 1)
    rooted.total += 1


def transpose_rows(k, src, dst, gain=None, shift=None):
    turned, kept = k.sig("turned"), k.sig("turned_kept")
    with k.nc.Block() as block:
        @block.tensor
        def _(pe):
            for t in range(TT):
                pe.transpose(k.ps[:, t // 4, t % 4 * P:(t % 4 + 1) * P], src[:, t, :],
                             k.ident[:]).then_inc(turned.sem, 1)

        @block.vector
        def _(v):
            v.wait_ge(turned.sem, turned.at(4))
            if gain is None:
                v.tensor_copy(dst[:, 0:512], k.ps[:, 0, :]).then_inc(kept.sem, 1)
            else:
                v.tensor_scalar(dst[:, 0:512], k.ps[:, 0, :], gain, shift, ALU.mult, ALU.add).then_inc(kept.sem, 1)

        @block.scalar
        def _(act):
            act.wait_ge(turned.sem, turned.at(TT))
            if gain is None:
                act.activation(dst[:, 512:1024], k.ps[:, 1, :], ACT.Copy).then_inc(kept.sem, 1)
            else:
                act.activation(dst[:, 512:1024], k.ps[:, 1, :], ACT.Identity, bias=shift,
                               scale=gain).then_inc(kept.sem, 1)
    turned.total += TT
    kept.total += 2


def project_columns(k, w, src, take):
    ready, taken = k.sig("columns_ready"), k.sig("columns_taken")
    with k.nc.Block() as block:
        @block.tensor
        def _(pe):
            for half in range(2):
                pe.matmul(k.ps[:, half, :], w, src[:, half * 512:(half + 1) * 512], start=True,
                          stop=True).then_inc(ready.sem, 1)

        @block.vector
        def _(v):
            for half in range(2):
                v.wait_ge(ready.sem, ready.at(half + 1))
                take(v, half, k.ps[:, half, :])
    ready.total += 2


def project_rows(k, src, w, take):
    ready = k.sig("rows_ready")
    with k.nc.Block() as block:
        @block.tensor
        def _(pe):
            for t in range(TT):
                pe.matmul(k.ps[:, t // 4, t % 4 * P:(t % 4 + 1) * P], src[:, t * P:(t + 1) * P], w, start=True,
                          stop=True).then_inc(ready.sem, 1)

        @block.vector
        def _(v):
            v.wait_ge(ready.sem, ready.at(TT))
            take(v, k.ps[:, 0:2, :].rearrange("p b (t d) -> p (b t) d", d=D))
    ready.total += TT


def keep(k, v, instruction):
    k.sig("vector_step").link(v, instruction)


def split_columns(k, v, bank, bias, scale, whole, high, low):
    keep(k, v, v.tensor_scalar(whole, bank, bias, scale, ALU.add, ALU.mult))
    keep(k, v, v.tensor_copy(high, whole))
    keep(k, v, v.tensor_tensor(low, whole, high.bitcast(F32), ALU.subtract))



def context_pieces(rows, rest):
    return [(rows[:, a:a + PREP, :], P, a, PREP) for a in range(0, CT, PREP)] + [(rest[0:REST], REST, CT, 1)]


def start_context(k, A, sp, pieces):
    whole = A["ctx_1024"][0, 0:CT * P, :].rearrange("(p t) d -> p t d", t=CT)
    short = A["ctx_1024"][0, CT * P:CTX, :].rearrange("(o p) d -> p o d", o=1)
    for n, (piece, parts, a, tiles) in enumerate(pieces):
        sp.dma_start(piece, whole[:, a:a + tiles, :] if a < CT else short) \
          .then_inc(k.sig(f"context_loaded_{n}").sem, 16)


def normalise_context(k, pieces):
    VECTOR = 1
    varied, rooted, shifted, normed = (k.sig("context_" + name) for name in ("varied", "rooted", "shifted", "normed"))
    loaded = [k.sig(f"context_loaded_{n}") for n in range(len(pieces))]
    constants = k.sig("constants_loaded")
    with k.nc.Block() as block:
        @block.sync
        def _(sp):
            sp.wait_ge(constants.sem, constants.at(0))

        @block.vector
        def _(v):
            def shift(n):
                piece, parts, a, tiles = pieces[n]
                v.wait_ge(rooted.sem, rooted.at(n + 1))
                v.scalar_tensor_tensor(out=k.shift[0:parts, a:a + tiles], in0=k.moments[0:parts, a:a + tiles, 0],
                                       scalar=-1.0, in1=k.stat[0:parts, 2, a:a + tiles], op0=ALU.mult,
                                       op1=ALU.mult).then_inc(shifted.sem, 1)
                if tiles > VECTOR:
                    for t in range(VECTOR):
                        last = v.tensor_scalar(piece[:, t, :], piece[:, t, :], k.moments[:, a + t, 0:1],
                                               k.stat[:, 2, a + t:a + t + 1], ALU.subtract, ALU.mult)
                    keep(k, v, last)

            for n, (piece, parts, a, tiles) in enumerate(pieces):
                v.wait_ge(loaded[n].sem, 16)
                for t in range(tiles):
                    last = v.bn_stats(k.bn[0:parts, a + t, :], piece[:, t, :])
                keep(k, v, last)
                for t in range(tiles):
                    last = v.bn_aggr(k.moments[0:parts, a + t, :], k.bn[0:parts, a + t, :])
                keep(k, v, last)
                variance = k.moments[0:parts, a:a + tiles, 1]
                v.tensor_scalar(variance, variance, EPS, None, ALU.add).then_inc(varied.sem, 1)
                if n:
                    shift(n - 1)
            shift(len(pieces) - 1)

        @block.gpsimd
        def _(pool):
            for n, (piece, parts, a, tiles) in enumerate(pieces):
                pool.wait_ge(varied.sem, varied.at(n + 1))
                pool.tensor_tensor(k.stat[0:parts, 2, a:a + tiles], k.moments[0:parts, a:a + tiles, 1],
                                   k.half[0:parts, 0:tiles], ALU.pow).then_inc(rooted.sem, 1)

        @block.scalar
        def _(act):
            for n, (piece, parts, a, tiles) in enumerate(pieces):
                act.wait_ge(shifted.sem, shifted.at(n + 1))
                for t in range(VECTOR if tiles > VECTOR else 0, tiles):
                    last = act.activation(piece[:, t, :], piece[:, t, :], ACT.Identity,
                                          bias=k.shift[0:parts, a + t:a + t + 1],
                                          scale=k.stat[0:parts, 2, a + t:a + t + 1])
                last.then_inc(normed.sem, 1)
            act.wait_ge(normed.sem, normed.at(len(pieces)))
    for s in (varied, rooted, shifted, normed):
        s.total += len(pieces)


def slot_keys_values(k, rows, rest, k_high, k_low, values):
    nc = k.nc
    staged_s, turned_s, kept_s = k.sig("rows_staged"), k.sig("context_turned"), k.sig("context_kept")
    input_s, keys_s, values_s = k.sig("input_ready"), k.sig("keys_ready"), k.sig("values_ready")
    high_s, low_s, stored_s = k.sig("keys_high"), k.sig("keys_low"), k.sig("values_stored")
    N = CT // PREP
    W = PREP * P
    with ExitStack() as ctx:
        staged = k.sb("staged_rows", [P, 2, PREP, D], ctx=ctx)
        inputs = k.sb("slot_inputs", [P, 2, W], ctx=ctx)
        turned = k.ps[:, 0:2, :].rearrange("p b c -> p (b c)")
        keys = k.ps[:, 2:4, :].rearrange("p b c -> p (b c)")
        vals = k.ps[:, 4:6, :].rearrange("p b c -> p (b c)")

        def pieces(width):
            return [(a, min(a + 512, width)) for a in range(0, width, 512)]

        with nc.Block() as block:
            def number(i):
                return N if i is None else i

            def width(tiles, parts):
                return (tiles - 1) * P + parts


            def stage_and_keep(act, i, r, tiles, parts):
                at = REST0 if i is None else i * W
                if not early(i):
                    act.wait_ge(turned_s.sem, turned_s.at(-1) + number(i))
                act.activation(staged[0:parts, r, 0:tiles, :],
                               rest[0:parts, 0:1, :] if i is None else rows[:, ds(i * PREP, PREP), :],
                               ACT.Copy).then_inc(staged_s.sem, 1)
                act.wait_ge(turned_s.sem, turned_s.at(1) + number(i))
                act.activation(k.zT[:, ds(at, width(tiles, parts))], turned[:, 0:width(tiles, parts)],
                               ACT.Copy).then_inc(kept_s.sem, 1)

            def keep_high(act, i, r, tiles, parts):
                act.wait_ge(keys_s.sem, keys_s.at(1) + number(i))
                act.activation(k_high[:, ds(CT * P if i is None else i * W, width(tiles, parts))],
                               keys[:, 0:width(tiles, parts)], ACT.Identity,
                               bias=k.col("L0_xcond_bk")).then_inc(high_s.sem, 1)

            def early(i):
                return isinstance(i, int) and i < 2

            def first(i):
                return isinstance(i, int) and i == 0

            def turn(pe, i, r, tiles, parts):
                pe.wait_ge(staged_s.sem, staged_s.at(1) + number(i))
                if not first(i):
                    pe.wait_ge(kept_s.sem, kept_s.at(0) + number(i))
                    pe.wait_ge(input_s.sem, input_s.at(0) + number(i))
                for t in range(tiles):
                    last = pe.transpose(turned[:, t * P:t * P + parts], staged[0:parts, r, t, :],
                                        k.ident[0:parts, 0:parts])
                last.then_inc(turned_s.sem, 1)

            def project(pe, i, r, tiles, parts):
                pe.wait_ge(input_s.sem, input_s.at(1) + number(i))
                if not first(i):
                    pe.wait_ge(high_s.sem, high_s.at(0) + number(i))
                    pe.wait_ge(low_s.sem, low_s.at(0) + number(i))
                for a, b in pieces(width(tiles, parts)):
                    last = pe.matmul(keys[:, a:b], k.square("L0_xcond_wk"), inputs[:, r, a:b], start=True, stop=True)
                last.then_inc(keys_s.sem, 1)
                if not first(i):
                    pe.wait_ge(stored_s.sem, stored_s.at(0) + number(i))
                for t in range(tiles):
                    last = pe.matmul(vals[0:parts, t * P:(t + 1) * P], inputs[:, r, t * P:t * P + parts],
                                     k.square("L0_xcond_wv"), start=True, stop=True)
                last.then_inc(values_s.sem, 1)

            def take_input(v, i, r, tiles, parts):
                v.wait_ge(kept_s.sem, kept_s.at(1) + number(i))
                if not early(i):
                    v.wait_ge(values_s.sem, values_s.at(-1) + number(i))
                v.tensor_scalar(inputs[:, r, 0:width(tiles, parts)], turned[:, 0:width(tiles, parts)],
                                k.col("L0_xcond_lnkv_g"), k.col("L0_xcond_lnkv_b"), ALU.mult,
                                ALU.add).then_inc(input_s.sem, 1)

            def keep_low_and_values(v, i, r, tiles, parts):
                v.wait_ge(high_s.sem, high_s.at(1) + number(i))
                to = CT * P if i is None else i * W
                high = k_high[:, ds(to, width(tiles, parts))]
                v.scalar_tensor_tensor(out=k_low[:, ds(to, width(tiles, parts))], in0=keys[:, 0:width(tiles, parts)],
                                       scalar=k.col("L0_xcond_bk"), in1=high.bitcast(F32), op0=ALU.add,
                                       op1=ALU.subtract).then_inc(low_s.sem, 1)
                v.wait_ge(values_s.sem, values_s.at(1) + number(i))
                v.tensor_tensor(values[0:parts, ds(CT if i is None else i * PREP, tiles), :],
                                vals[0:parts, 0:tiles * D].rearrange("p (t d) -> p t d", d=D),
                                k.row("L0_xcond_bv", parts).unsqueeze(1).to_broadcast([parts, tiles, D]),
                                ALU.add).then_inc(stored_s.sem, 1)

            def steps(engine, ahead, behind):
                ahead(engine, 0, 0, PREP, P)
                ahead(engine, 1, 1, PREP, P)
                behind(engine, 0, 0, PREP, P)
                with engine.Fori(1, N // 2) as m:
                    i = m * 2
                    ahead(engine, i, 0, PREP, P)
                    behind(engine, i - 1, 1, PREP, P)
                    ahead(engine, i + 1, 1, PREP, P)
                    behind(engine, i, 0, PREP, P)
                ahead(engine, None, 0, 1, REST)
                behind(engine, N - 1, 1, PREP, P)
                behind(engine, None, 0, 1, REST)

            @block.scalar
            def _(act):
                steps(act, stage_and_keep, keep_high)

            @block.tensor
            def _(pe):
                steps(pe, turn, project)

            @block.vector
            def _(v):
                steps(v, take_input, keep_low_and_values)
        for s in (staged_s, turned_s, kept_s, input_s, keys_s, values_s, high_s, low_s, stored_s):
            s.total += N + 1


def value_sum(k, values, vsum):
    summed = k.sig("values_summed")
    with ExitStack() as ctx:
        part = k.sb("values_part", [P, D], ctx=ctx)
        with k.nc.Block() as block:
            @block.vector
            def _(v):
                keep(k, v, v.reduce_sum(part[:], values[:, 0:CT, :].rearrange("p t d -> p d t"), axis=AX))
                keep(k, v, v.tensor_tensor(part[0:REST], part[0:REST], values[0:REST, CT, :], ALU.add))
        with k.nc.Block() as block:
            @block.tensor
            def _(pe):
                pe.matmul(k.ps[:, 0, 0:1], part[:], k.ones[:, 0:1], start=True, stop=True).then_inc(summed.sem, 1)

            @block.vector
            def _(v):
                v.wait_ge(summed.sem, summed.at(1))
                keep(k, v, v.tensor_scalar(vsum[:], k.ps[:, 0, 0:1], EPS_ATTN, None, ALU.mult))
        summed.total += 1


def slot_scores_and_updates(k, k_high, k_low, values, q_high, q_low, total, meanwhile):
    nc = k.nc
    staged_s, scores_s, probs_s = k.sig("key_staged"), k.sig("scores_ready"), k.sig("probs_ready")
    max_s, bias_s, recip_s = k.sig("slot_max"), k.sig("slot_bias"), k.sig("slot_recip")
    total_s, scaled_s, update_s = k.sig("total_added"), k.sig("value_scaled"), k.sig("update_added")
    RING = 3
    with ExitStack() as ctx:
        key = k.sb("key_tile", [P, RING, 2, P], F32R, ctx=ctx)
        probs = k.sb("slot_probs", [P, RING, TOKENS], ctx=ctx)
        value = k.sb("value_tile", [P, RING, D], ctx=ctx)
        small = k.sb("slot_small", [P, RING, 4], ctx=ctx)
        scores = [k.ps[:, bank:bank + 2, :] for bank in (0, 2, 6)]
        update = k.ps[:, 4:6, :]

        def early(i):
            return isinstance(i, int) and i < RING

        def run(engine, step):
            for i in range(RING):
                step(i, i, P)
            with engine.Fori(1, CT // RING) as m:
                for r in range(RING):
                    step(m * RING + r, r, P)
            for i in range(CT // RING * RING, CT + 1):
                step(i, i % RING, P if i < CT else REST)

        def tile_before(i, r):
            return i - 1, (r - 1) % RING

        with nc.Block() as block:
            @block.gpsimd
            def _(pool):
                def stage(i, r, parts):
                    if not early(i):
                        pool.wait_ge(scores_s.sem, scores_s.at(1 - RING) + i)
                    for n, source in enumerate((k_high, k_low)):
                        pool.tensor_copy(key[:, r, n, 0:parts], source[:, ds(i * P, parts)]).then_inc(staged_s.sem, 1)

                def step(i, r, parts):
                    pool.wait_ge(recip_s.sem, recip_s.at(1) + i)
                    if not early(i):
                        pool.wait_ge(update_s.sem, update_s.at(1 - RING) + i)
                    pool.tensor_tensor(value[0:parts, r, :], values[0:parts, ds(i, 1), :].squeeze(1),
                                       small[0:parts, r, 3:4].to_broadcast([parts, D]),
                                       ALU.mult).then_inc(scaled_s.sem, 1)
                    if not isinstance(i, int) or i + RING <= CT:
                        stage(i + RING, r, REST if isinstance(i, int) and i + RING == CT else P)

                for i in range(RING):
                    stage(i, i, P)
                for i in range(RING):
                    step(i, i, P)
                assert CT // RING * RING + RING > CT
                with pool.Fori(1, CT // RING - 1) as m:
                    for r in range(RING):
                        step(m * RING + r, r, P)
                for i in range((CT // RING - 1) * RING, CT + 1):
                    step(i, i % RING, P if i < CT else REST)

            @block.tensor
            def _(pe):
                def score(i, r):
                    pe.wait_ge(staged_s.sem, staged_s.at(2) + i * 2)
                    if not early(i):
                        pe.wait_ge(probs_s.sem, probs_s.at(1 - RING) + i)
                    for c in range(2):
                        cols = slice(c * 512, (c + 1) * 512)
                        pe.matmul(scores[r][:, c, :], key[:, r, 0, :], q_high[:, cols], start=True, stop=False)
                        pe.matmul(scores[r][:, c, :], key[:, r, 1, :], q_high[:, cols], start=False, stop=False)
                        last = pe.matmul(scores[r][:, c, :], key[:, r, 0, :], q_low[:, cols], start=False, stop=True)
                    last.then_inc(scores_s.sem, 1)

                def add(i, r, parts):
                    first, final = isinstance(i, int) and i == 0, isinstance(i, int) and i == CT
                    pe.wait_ge(scaled_s.sem, scaled_s.at(1) + i)
                    pe.wait_ge(probs_s.sem, probs_s.at(1) + i)
                    for c in range(2):
                        last = pe.matmul(update[:, c, :], value[0:parts, r, :], probs[0:parts, r, c * 512:(c + 1) * 512],
                                         start=first, stop=final)
                    last.then_inc(update_s.sem, 1)

                def step(i, r, parts):
                    score(i, r)
                    if not isinstance(i, int) or i >= 2:
                        add(i - 2, (r - 2) % RING, P)

                run(pe, step)
                add(CT - 1, (CT - 1) % RING, P)
                add(CT, CT % RING, REST)

            @block.vector
            def _(v):
                def bound(i, r, parts):
                    v.wait_ge(scores_s.sem, scores_s.at(1) + i)
                    v.reduce_max(small[0:parts, r, 0:1], scores[r][0:parts].rearrange("p b c -> p (b c)"),
                                 axis=AX).then_inc(max_s.sem, 1)
                    v.wait_ge(max_s.sem, max_s.at(1) + i)
                    v.tensor_scalar(small[0:parts, r, 1:2], small[0:parts, r, 0:1], -SLOT_SCALE, None,
                                    ALU.mult).then_inc(bias_s.sem, 1)

                def invert(i, r, parts):
                    v.wait_ge(probs_s.sem, probs_s.at(1) + i)
                    if not early(i):
                        v.wait_ge(scaled_s.sem, scaled_s.at(1 - RING) + i)
                    v.reciprocal(small[0:parts, r, 3:4], small[0:parts, r, 2:3]).then_inc(recip_s.sem, 1)

                def count(i, r, parts):
                    v.wait_ge(recip_s.sem, recip_s.at(1) + i)
                    v.wait_ge(total_s.sem, total_s.at(1) + i)
                    v.scalar_tensor_tensor(out=total[0:parts], in0=probs[0:parts, r, :], scalar=small[0:parts, r, 3:4],
                                           in1=total[0:parts], op0=ALU.mult, op1=ALU.add).then_inc(total_s.sem, 1)

                def step(i, r, parts):
                    if isinstance(i, int) and i == 0:
                        bound(i, r, parts)
                        return
                    before = tile_before(i, r)
                    invert(*before, P)
                    bound(i, r, parts)
                    count(*before, P)

                v.memset(total[:], 0.0).then_inc(total_s.sem, 1)
                meanwhile(v)
                run(v, step)
                invert(CT, CT % RING, REST)
                count(CT, CT % RING, REST)

            @block.scalar
            def _(act):
                def step(i, r, parts):
                    act.wait_ge(bias_s.sem, bias_s.at(1) + i)
                    if not early(i):
                        act.wait_ge(update_s.sem, update_s.at(1 - RING) + i)
                        act.wait_ge(total_s.sem, total_s.at(2 - RING) + i)
                    act.activation(probs[0:parts, r, :], scores[r][0:parts].rearrange("p b c -> p (b c)"), ACT.Exp,
                                   bias=small[0:parts, r, 1:2], scale=SLOT_SCALE,
                                   accum_out=small[0:parts, r, 2:3]).then_inc(probs_s.sem, 1)

                run(act, step)
        for s in (scores_s, probs_s, max_s, bias_s, recip_s, scaled_s, update_s):
            s.total += CT + 1
        staged_s.total += 2 * (CT + 1)
        total_s.total += CT + 2


def slot_normalise(k, total, vsum, update, inverse):
    summed, updated = k.sig("total_summed"), k.sig("update_taken")
    with k.nc.Block() as block:
        @block.tensor
        def _(pe):
            for t in range(TT):
                last = pe.matmul(k.ps[:, 0, t:t + 1], total[:, t * P:(t + 1) * P], k.ones[:, 0:1], start=True, stop=True)
            last.then_inc(summed.sem, 1)

        @block.scalar
        def _(act):
            act.activation(update[:].rearrange("p (b c) -> p b c", b=2), k.ps[:, 4:6, :], ACT.Identity,
                           bias=vsum[:]).then_inc(updated.sem, 1)
            act.wait_ge(updated.sem, updated.at(1))

        @block.vector
        def _(v):
            v.wait_ge(summed.sem, summed.at(1))
            keep(k, v, v.tensor_scalar(inverse[:], k.ps[:, 0, 0:TT], CTX * EPS_ATTN, None, ALU.add))
            keep(k, v, v.reciprocal(inverse[:], inverse[:]))
    summed.total += 1
    updated.total += 1


def gelu_columns(k, w, src, bias, dst, meanwhile):
    ready, done = k.sig("hidden_ready"), k.sig("hidden_done")
    with k.nc.Block() as block:
        @block.tensor
        def _(pe):
            for half in range(2):
                pe.matmul(k.ps[:, half, :], w, src[:, half * 512:(half + 1) * 512], start=True,
                          stop=True).then_inc(ready.sem, 1)

        @block.vector
        def _(v):
            meanwhile(v)

        @block.scalar
        def _(act):
            for half in range(2):
                act.wait_ge(ready.sem, ready.at(half + 1))
                act.activation(dst[:, half * 512:(half + 1) * 512], k.ps[:, half, :], ACT.Gelu,
                               bias=bias).then_inc(done.sem, 1)
    ready.total += 2
    done.total += 2


def slot_attention(k, A, whole=True):
    with ExitStack() as ctx:
        k_high = k.sb("k_high", [P, CTX], F32R, ctx=ctx)
        k_low = k.sb("k_low", [P, CTX], F32R, ctx=ctx)
        values = k.sb("values", [P, CT + 1, D], ctx=ctx)
        with ExitStack() as inner:
            rows = k.sb("context_rows", [P, CT, D], ctx=inner)
            rest = k.sb("context_rest", [P, 1, D], ctx=inner)
            pieces = context_pieces(rows, rest)
            load_constants(k, A, lambda sp: start_context(k, A, sp, pieces))
            normalise_context(k, pieces)
            slot_keys_values(k, rows, rest, k_high, k_low, values)
        if not whole:
            return
        slots = k.sb("slots", [P, TT, D], ctx=ctx)
        normed = k.sb("slots_normed", [P, TT, D], ctx=ctx)
        turned = k.sb("slots_turned", [P, TOKENS], ctx=ctx)
        q_high = k.sb("q_high", [P, TOKENS], F32R, ctx=ctx)
        q_low = k.sb("q_low", [P, TOKENS], F32R, ctx=ctx)
        total = k.sb("attention_total", [P, TOKENS], ctx=ctx)
        vsum = k.sb("value_sum", [P, 1], ctx=ctx)
        inverse = k.sb("inverse_attention_total", [P, TT], ctx=ctx)
        sigma = k.sb("slot_sigma", [P, D], ctx=ctx)
        value_sum(k, values, vsum)
        layernorm_rows(k, k.x[:], normed[:])
        exp_s = k.sig("sigma_ready")
        with k.nc.Block() as block:
            @block.scalar
            def _(act):
                act.activation(sigma[:], k.row("L0_xcond_q_logsig"), ACT.Exp).then_inc(exp_s.sem, 1)

            @block.vector
            def _(v):
                v.wait_ge(exp_s.sem, exp_s.at(1))
                over = [P, TT, D]
                keep(k, v, v.tensor_tensor(slots[:], normed[:], sigma[:].unsqueeze(1).to_broadcast(over), ALU.mult))
                keep(k, v, v.tensor_tensor(slots[:], slots[:], k.row_of_tiles("L0_xcond_q_mu", TT), ALU.add))
        exp_s.total += 1

        def take_queries(v, half, bank):
            cols = slice(half * 512, (half + 1) * 512)
            split_columns(k, v, bank, k.col("L0_xcond_bq"), 1.0, turned[:, cols], q_high[:, cols], q_low[:, cols])

        def add_to_slots(*names):
            def add(v):
                for name in names:
                    keep(k, v, v.tensor_tensor(slots[:], slots[:], k.row_of_tiles(name, TT), ALU.add))
            return add

        def take_update(v, rows):
            for t in range(TT):
                last = v.scalar_tensor_tensor(slots[:, t, :], rows[:, t, :], inverse[:, t:t + 1], slots[:, t, :],
                                              ALU.mult, ALU.add)
            keep(k, v, last)

        def take_sum(v, rows):
            keep(k, v, v.tensor_tensor(normed[:], slots[:], rows, ALU.add))

        for _ in range(ITERATIONS):
            layernorm_rows(k, slots[:], normed[:])
            transpose_rows(k, normed, total, k.col("L0_xcond_lnq_g"), k.col("L0_xcond_lnq_b"))
            project_columns(k, k.square("L0_xcond_wq"), total, take_queries)
            slot_scores_and_updates(k, k_high, k_low, values, q_high, q_low, total, add_to_slots("L0_xcond_bu"))
            slot_normalise(k, total, vsum, turned, inverse)
            project_rows(k, turned, k.square("L0_xcond_wu"), take_update)
            layernorm_rows(k, slots[:], normed[:])
            transpose_rows(k, normed, turned, k.col("L0_xcond_lnm_g"), k.col("L0_xcond_lnm_b"))
            gelu_columns(k, k.square("L0_xcond_w1"), turned, k.col("L0_xcond_b1"), total,
                         add_to_slots("L0_xcond_b2", "cond_1024"))
            project_rows(k, total, k.square("L0_xcond_w2"), take_sum)
            layernorm_rows(k, normed[:], slots[:], gain=k.row("L0_xcond_lnp_g"), shift=k.row("L0_xcond_lnp_b"))
        with k.nc.Block() as block:
            @block.vector
            def _(v):
                keep(k, v, v.tensor_tensor(k.x[:], k.x[:], slots[:], ALU.add))



def causal_attention(k, xaT, values, context, sent):
    nc = k.nc
    parts = nc.dram_tensor("query_key_parts", [4, P, TOKENS], F32, kind="Internal").ap()
    S = {name: k.sig("causal_" + name) for name in (
        "parted", "loaded_even", "loaded_odd", "cleared", "fill", "peak", "peaked", "negated", "turned", "shift", "score", "expd",
        "added", "kept", "back", "inverted", "context", "grouped")}
    LOADED, LOADS = ("loaded_even", "loaded_odd"), 6 * 16

    def inc(name, instruction):
        instruction.then_inc(S[name].sem, 1)

    def wait(engine, name, n):
        if n > 0:
            engine.wait_ge(S[name].sem, S[name].at(n))

    zeroed, keys_cleared, ones_laid = (k.sig(name) for name in ("experts_zeroed", "causal_keys_cleared",
                                                                "causal_ones_laid"))
    with ExitStack() as ctx:
        zeros = k.sb("expert_zeros", [P, E0 * CAP * D // P], ctx=ctx)
        queries = [k.sb("queries", [P, GROUP, TOKENS], F32R, ctx=ctx) for _ in range(2)]
        keys = [k.sb("keys", [P, GROUP, TOKENS], F32R, ctx=ctx) for _ in range(2)]
        with ExitStack() as inner:
            whole = k.sb("split_whole", [P, TOKENS], ctx=inner)
            split = k.sb("split_parts", [P, 4, TOKENS], F32R, ctx=inner)
            for n, (w, b, scale) in enumerate((("L0_ffn_q_w", "L0_ffn_q_b", float(HD0) ** -0.5),
                                               ("L0_ffn_k_w", "L0_ffn_k_b", 1.0))):
                def take(v, half, bank):
                    cols = slice(half * 512, (half + 1) * 512)
                    split_columns(k, v, bank, k.col(b), scale, whole[:, cols], split[:, 2 * n, cols],
                                  split[:, 2 * n + 1, cols])
                project_columns(k, k.square(w), xaT, take)

            with nc.Block() as block:
                @block.sync
                def _(sp):
                    sp.dma_start(parts.rearrange("n p t -> p n t"), split[:].bitcast(F32)).then_inc(S["parted"].sem, 16)
                    sp.wait_ge(S["parted"].sem, 16)

                @block.gpsimd
                def _(pool):
                    for tile in keys:
                        pool.memset(tile[:].bitcast(F32), 0.0).then_inc(keys_cleared.sem, 1)

                @block.scalar
                def _(act):
                    for n, tile in enumerate(keys):
                        act.wait_ge(keys_cleared.sem, n + 1)
                        act.activation(tile[64:65].rearrange("p h (t c) -> p (h t) c", c=P),
                                       k.ones[64:65].unsqueeze(1).to_broadcast([1, GROUP * TT, P]),
                                       ACT.Copy).then_inc(ones_laid.sem, 1)
                    act.wait_ge(ones_laid.sem, 2)

                @block.vector
                def _(v):
                    inc("cleared", v.memset(zeros[:], 0.0))
                    for tile in queries:
                        inc("cleared", v.memset(tile[:].bitcast(F32), 0.0))
                    wait(v, "cleared", 3)
            S["cleared"].total += 3

        probs = k.sb("causal_probs", [P, 2, GROUP, TOKENS], ctx=ctx)
        value = k.sb("causal_value", [P, TT, 2, GROUP * 32], ctx=ctx)
        peaks = k.sb("causal_peaks", [P, GROUP, 64 + TT], ctx=ctx)
        out_sb = k.sb("causal_out", [P, TOKENS], ctx=ctx)
        inverse = k.sb("causal_inverse", [P, TT, GROUP], ctx=ctx)
        mask = k.sb("causal_mask", [P, 2, P], BF16, ctx=ctx)
        ident = k.sb("identity_short", [P, P], BF16, ctx=ctx)
        whole_mask = k.sb("whole_mask", [P, 2, P], ctx=ctx)
        piece_peaks = k.sb("causal_piece_peaks", [P, GROUP, TT, 2], ctx=ctx)
        spread = k.ps[:, 0:4, :]
        turned = k.ps[:, 4:6, :]
        out = k.ps[:, 6:8, :]

        with nc.Block() as block:
            @block.gpsimd
            def _(pool):
                pool.memset(whole_mask[:], 0.0).then_inc(S["cleared"].sem, 1)
                wait(pool, "cleared", 1)
                for n, sign in enumerate((1, -1)):
                    pool.affine_select(out=whole_mask[:, n, :], in_=whole_mask[:, n, :], compare_op=ALU.is_ge,
                                       fill=NEG, base=0, pattern=[[-sign, P]],
                                       channel_multiplier=sign).then_inc(S["cleared"].sem, 1)
                wait(pool, "cleared", 3)
                pool.tensor_copy(mask[:], whole_mask[:]).then_inc(S["cleared"].sem, 1)
                pool.tensor_copy(ident[:], k.ident[:]).then_inc(S["cleared"].sem, 1)
                pool.memset(peaks[:], 0.0).then_inc(S["cleared"].sem, 1)
                pool.memset(piece_peaks[:], NEG).then_inc(S["cleared"].sem, 1)
                wait(pool, "cleared", 7)
        S["cleared"].total += 7

        def pieces(a, b):
            return [(x, min(b, (x // 512 + 1) * 512)) for x in [a] + [c for c in (512,) if a < c < b]]

        for_peaks = [(h, t, a, b) for h in range(GROUP) for t in range(TT) for a, b in pieces(0, (t + 1) * P)]
        for_probs = [(j, h, a, b) for j in range(TT) for h in range(GROUP) for a, b in pieces(0, TOKENS - j * P)]
        NP = len(for_peaks)
        assert len(for_probs) == NP
        PER_HEAD = NP // GROUP
        until = [sum(piece[0] < j for piece in for_probs) for j in range(TT + 1)]
        BEHIND = 2

        def load(sp, g):
            r = g % 2
            wait(sp, "score", NP * (g - 1))
            for tile, order in ((queries[r], (0, 1, 0)), (keys[r], (2, 2, 3))):
                for n, part in enumerate(order):
                    sp.dma_start(tile[n * HD0:(n + 1) * HD0].bitcast(F32), parts[part, g * 32:(g + 1) * 32, :]
                                 .rearrange("(h r) t -> r h t", r=HD0)) \
                      .then_inc(S[LOADED[r]].sem, 16)

        def fill(pe, g, n):
            h, t, a, b = for_peaks[n]
            r = g % 2
            if n == 0:
                wait(pe, LOADED[r], LOADS * (g // 2 + 1))
            wait(pe, "peak", NP * g + n - 1)
            diagonal = b == (t + 1) * P
            last = pe.matmul(spread[:, n % 2, 0:b - a], queries[r][:, h, t * P:(t + 1) * P], keys[r][:, h, a:b],
                             start=True, stop=not diagonal)
            if diagonal:
                last = pe.matmul(spread[:, n % 2, b - a - P:b - a], ident[:], mask[:, 0, :], start=False, stop=True)
            inc("fill", last)

        def turn_peaks(pe, g, h):
            wait(pe, "negated", GROUP * g + h + 1)
            if h:
                wait(pe, "shift", GROUP * g + h)
            else:
                wait(pe, "context", g - 1)
            for t in range(TT):
                last = pe.transpose(turned[0:65, t // 4, t % 4 * P:(t % 4 + 1) * P], peaks[:, h, t:t + 65], k.ident[:])
            inc("turned", last)

        def score(pe, g, n):
            j, h, a, b = for_probs[n]
            r = g % 2
            if n == 0:
                wait(pe, "shift", GROUP * (g + 1))
            wait(pe, "expd", NP * g + n - 1)
            last = pe.matmul(spread[:, 2 + n % 2, 0:b - a], keys[r][:, h, j * P:(j + 1) * P],
                             queries[r][:, h, j * P + a:j * P + b], start=True, stop=a > 0)
            if a == 0:
                last = pe.matmul(spread[:, 2 + n % 2, 0:P], ident[:], mask[:, 1, :], start=False, stop=True)
            inc("score", last)

        def add(pe, g, j):
            wait(pe, "expd", NP * g + until[j + 1])
            if j == 0:
                wait(pe, "kept", g)
                wait(pe, "grouped", g + 1)
            for a, b in pieces(j * P, TOKENS):
                for h in range(GROUP):
                    last = pe.matmul(out[32 * h:32 * h + 32, a // 512, a % 512:(b - 1) % 512 + 1],
                                     value[:, j, g % 2, 32 * h:32 * h + 32], probs[:, j % 2, h, a - j * P:b - j * P],
                                     start=j == 0, stop=j == (3 if a < 512 else TT - 1))
            inc("added", last)

        def tensor_group(pe, g):
            after = None if g == NG - 1 else 0 if g is None else g + 1
            behind = 0 if g is None else BEHIND
            for n in range(NP + behind):
                if g is not None and n < NP:
                    score(pe, g, n)
                if g is not None and n + 1 - 4 in until[1:TT]:
                    add(pe, g, until.index(n + 1 - 4) - 1)
                if g and n == BEHIND + 1:
                    turn_back(pe, g - 1)
                m = n - behind
                if after is not None and m >= 0:
                    fill(pe, after, m)
                    if m > PER_HEAD and m % PER_HEAD == 3:
                        turn_peaks(pe, after, m // PER_HEAD - 1)
            if g is not None:
                add(pe, g, TT - 1)
            if after is not None:
                turn_peaks(pe, after, GROUP - 1)
            if g is not None and after is None:
                turn_back(pe, g)

        def turn_back(pe, g):
            wait(pe, "kept", g + 1)
            wait(pe, "shift", GROUP * min(g + 2, NG))
            wait(pe, "context", g)
            for t in range(TT):
                last = pe.transpose(turned[:, t // 4, t % 4 * P:(t % 4 + 1) * P], out_sb[:, t * P:(t + 1) * P],
                                    k.ident[:])
            inc("back", last)

        def shift(act, g, h):
            wait(act, "turned", GROUP * g + h + 1)
            inc("shift", act.activation(queries[g % 2][64:65, h, :].rearrange("p (b c) -> p b c", b=2),
                                        turned[64:65], ACT.Copy))

        def scalar_group(act, g):
            after = None if g == NG - 1 else 0 if g is None else g + 1
            behind = 0 if g is None else BEHIND
            for n in range(NP + behind):
                if g is not None and n < NP:
                    j, h, a, b = for_probs[n]
                    wait(act, "score", NP * g + n + 1)
                    if h == 0 and a == 0:
                        wait(act, "added", TT * g + max(j - 1, 0))
                    inc("expd", act.activation(probs[:, j % 2, h, a:b], spread[:, 2 + n % 2, 0:b - a], ACT.Exp))
                m = n - behind - 2
                if after is not None and m > PER_HEAD and m % PER_HEAD == 3:
                    shift(act, after, m // PER_HEAD - 1)
            if after is not None:
                shift(act, after, GROUP - 1)
            if g is not None:
                wait(act, "added", TT * (g + 1))
                wait(act, "back", g)
                inc("kept", act.activation(out_sb[:].rearrange("p (b c) -> p b c", b=2), out, ACT.Copy))

        def vector_group(v, g):
            after = None if g == NG - 1 else 0 if g is None else g + 1
            if after is not None:
                for n, (h, t, a, b) in enumerate(for_peaks):
                    wait(v, "fill", NP * after + n + 1)
                    inc("peak", v.reduce_max(piece_peaks[:, h, t, a // 512:a // 512 + 1], spread[:, n % 2, 0:b - a],
                                             axis=AX))
                    if b == TOKENS:
                        wait(v, "peak", NP * after + n + 1)
                        wait(v, "turned", GROUP * after)
                        inc("peaked", v.reduce_max(peaks[:, h, 64:64 + TT], piece_peaks[:, h], axis=AX))
                        wait(v, "peaked", GROUP * after + h + 1)
                        inc("negated", v.tensor_scalar(peaks[:, h, 64:64 + TT], peaks[:, h, 64:64 + TT], -1.0, None,
                                                       ALU.mult))
            if g is not None:
                wait(v, "back", g + 1)
                rows = turned.rearrange("p b (t h c) -> p (b t) h c", t=4, h=GROUP)
                inc("inverted", v.reciprocal(inverse[:], rows[:, :, :, HD0]))
                wait(v, "inverted", g + 1)
                inc("context", v.tensor_tensor(
                    context[:, :, g * GROUP * HD0:(g + 1) * GROUP * HD0].rearrange("p t (h c) -> p t h c", h=GROUP),
                    rows[:, :, :, 0:HD0], inverse[:].unsqueeze(3).to_broadcast([P, TT, GROUP, HD0]), ALU.mult))

        def pool_group(pool, g):
            if g is not None:
                wait(pool, "added", TT * (g - 1))
                inc("grouped", pool.tensor_copy(value[:, :, g % 2, :], values[:, :, g * GROUP * 32:(g + 1) * GROUP * 32]))

        def groups(engine, part):
            for g in (None,) + tuple(range(NG)):
                part(engine, g)

        with nc.Block() as block:
            @block.sync
            def _(sp):
                load(sp, 0)
                sp.dma_start(sent[0:E0 * CAP, :].rearrange("(p r) d -> p (r d)", p=P), zeros[:]).then_inc(zeroed.sem, 16)
                for g in range(1, NG):
                    load(sp, g)
                sp.wait_ge(zeroed.sem, 16)

            @block.tensor
            def _(pe):
                groups(pe, tensor_group)

            @block.scalar
            def _(act):
                groups(act, scalar_group)

            @block.vector
            def _(v):
                groups(v, vector_group)

            @block.gpsimd
            def _(pool):
                groups(pool, pool_group)



def route(k, xt, xtT, router, weights, scatter, gather):
    nc = k.nc
    with ExitStack() as ctx:
        sb = lambda name, shape, dtype=F32: k.sb(name, shape, dtype, ctx=ctx)
        logits = sb("logits", [P, TT, E0])
        best = sb("best", [P, TT, 8])
        place = sb("best_place", [P, TT, 8], U32)
        placef = sb("best_placef", [P, TT, 2])
        probs = sb("router_probs", [P, TT, E0])
        total = sb("router_total", [P, TT, 1])
        chosen = sb("chosen", [P, TT, 2 * E0])
        before = sb("chosen_before", [P, TT + 1, 2 * E0])
        location = sb("location", [P, TT, 2 * E0])
        product = sb("route_product", [P, TT, 2 * E0])
        kept = sb("kept", [P, TT, 2])
        slot = sb("slot", [P, TT, 2])
        spare = sb("spare", [P, TT, 2])
        expert = sb("expert_number", [P, E0])
        upper = sb("upper", [P, P])
        made, ready = k.sig("route_constants"), k.sig("route_counted")
        exp_s = k.sig("route_exponential")

        with nc.Block() as block:
            @block.gpsimd
            def _(pool):
                pool.iota(expert[:], [[1, E0]], base=0, channel_multiplier=0,
                          allow_small_or_imprecise_dtypes=True).then_inc(made.sem, 1)
                pool.iota(spare[:], [[2 * P, TT], [1, 2]], base=E0 * CAP, channel_multiplier=2,
                          allow_small_or_imprecise_dtypes=True).then_inc(made.sem, 1)
                pool.memset(upper[:], 1.0).then_inc(made.sem, 1)
                pool.wait_ge(made.sem, made.at(3))
                pool.affine_select(out=upper[:], in_=upper[:], compare_op=ALU.is_ge, fill=0.0, base=0,
                                   pattern=[[1, P]], channel_multiplier=-1).then_inc(made.sem, 1)
                pool.wait_ge(made.sem, made.at(4))

            @block.tensor
            def _(pe):
                pe.wait_ge(k.sig("router_loaded").sem, 16)
                for t in range(TT):
                    pe.matmul(k.ps[:, 0, t * E0:(t + 1) * E0], xtT[:, t * P:(t + 1) * P], router[:], start=True,
                              stop=True).then_inc(ready.sem, 1)

            @block.vector
            def _(v):
                v.wait_ge(ready.sem, ready.at(TT))
                keep(k, v, v.tensor_copy(logits[:].rearrange("p t e -> p (t e)"), k.ps[:, 0, 0:TT * E0]))
                for t in range(TT):
                    keep(k, v, v.max(best[:, t, :], logits[:, t, :]))
                    keep(k, v, v.max_index(place[:, t, :], best[:, t, :], logits[:, t, :]))
                keep(k, v, v.tensor_copy(placef[:], place[:, :, 0:2]))
                keep(k, v, v.tensor_tensor(probs[:], logits[:], best[:, :, 0:1].to_broadcast([P, TT, E0]),
                                           ALU.subtract))
        made.total += 4
        ready.total += TT

        with nc.Block() as block:
            @block.scalar
            def _(act):
                act.activation(probs[:], probs[:], ACT.Exp).then_inc(exp_s.sem, 1)

            @block.vector
            def _(v):
                for n in range(2):
                    keep(k, v, v.tensor_tensor(chosen[:, :, n * E0:(n + 1) * E0],
                                               expert[:].unsqueeze(1).to_broadcast([P, TT, E0]),
                                               placef[:, :, n:n + 1].to_broadcast([P, TT, E0]), ALU.is_equal))
                keep(k, v, v.memset(before[:, 0, :], 0.0))
                for t in range(TT):
                    keep(k, v, v.tensor_tensor(before[:, t + 1, :], before[:, t, :], chosen[:, t, :], ALU.add))
                keep(k, v, v.tensor_tensor(before[:, 0:TT, E0:2 * E0], before[:, 0:TT, E0:2 * E0],
                                           before[:, TT:TT + 1, 0:E0].to_broadcast([P, TT, E0]), ALU.add))
                v.wait_ge(exp_s.sem, exp_s.at(1))
                keep(k, v, v.reduce_sum(total[:].squeeze(2), probs[:], axis=AX))
                keep(k, v, v.reciprocal(total[:], total[:]))
                keep(k, v, v.tensor_tensor(probs[:], probs[:], total[:].to_broadcast([P, TT, E0]), ALU.mult))
        exp_s.total += 1

        with nc.Block() as block:
            @block.tensor
            def _(pe):
                pe.matmul(k.ps[:, 1, 0:TT * 2 * E0], upper[:], chosen[:].rearrange("p t e -> p (t e)"), start=True,
                          stop=False)
                pe.matmul(k.ps[:, 1, 0:TT * 2 * E0], k.ones[:], before[:, 0:TT, :].rearrange("p t e -> p (t e)"),
                          start=False, stop=True).then_inc(ready.sem, 1)

            @block.vector
            def _(v):
                both = lambda tile: tile[:].rearrange("p t (n e) -> p t n e", n=2)
                v.wait_ge(ready.sem, ready.at(1))
                keep(k, v, v.tensor_scalar(location[:].rearrange("p t e -> p (t e)"), k.ps[:, 1, 0:TT * 2 * E0], -1.0,
                                           None, ALU.add))
                keep(k, v, v.scalar_tensor_tensor(out=chosen[:].rearrange("p t e -> p (t e)"),
                                                  in0=location[:].rearrange("p t e -> p (t e)"), scalar=float(CAP),
                                                  in1=chosen[:].rearrange("p t e -> p (t e)"), op0=ALU.is_lt,
                                                  op1=ALU.mult))
                keep(k, v, v.tensor_tensor(product[:], location[:], chosen[:], ALU.mult))
                keep(k, v, v.reduce_sum(slot[:], both(product), axis=AX))
                keep(k, v, v.reduce_sum(kept[:], both(chosen), axis=AX))
                for n in range(2):
                    keep(k, v, v.tensor_tensor(product[:, :, n * E0:(n + 1) * E0], probs[:],
                                               chosen[:, :, n * E0:(n + 1) * E0], ALU.mult))
                keep(k, v, v.reduce_sum(weights[:], both(product), axis=AX))
                keep(k, v, v.tensor_tensor(total[:], weights[:, :, 0:1], weights[:, :, 1:2], ALU.add))
                keep(k, v, v.tensor_scalar(total[:], total[:], float(2.0 ** -23), None, ALU.max))
                keep(k, v, v.reciprocal(total[:], total[:]))
                keep(k, v, v.tensor_tensor(weights[:], weights[:], total[:].to_broadcast([P, TT, 2]), ALU.mult))
                flat = lambda tile: tile[:].rearrange("p t n -> p (t n)")
                keep(k, v, v.scalar_tensor_tensor(out=flat(slot), in0=flat(placef), scalar=float(CAP), in1=flat(slot),
                                                  op0=ALU.mult, op1=ALU.add))
                keep(k, v, v.tensor_tensor(slot[:], slot[:], kept[:], ALU.mult))
                keep(k, v, v.tensor_copy(gather[:], slot[:]))
                keep(k, v, v.tensor_scalar(kept[:], kept[:], -1.0, 1.0, ALU.mult, ALU.add))
                keep(k, v, v.tensor_tensor(spare[:], spare[:], kept[:], ALU.mult))
                keep(k, v, v.tensor_tensor(slot[:], slot[:], spare[:], ALU.add))
                keep(k, v, v.tensor_copy(scatter[:], slot[:]))
        ready.total += 1


def sixteen_experts(k, A, xt, weights, scatter, gather, sent, back):
    nc = k.nc
    got = nc.dram_tensor("experts_out", [E0 * CAP, D], F32, kind="Internal").ap()
    RING = 4
    S = {name: k.sig("expert_" + name) for name in (
        "sent", "rows", "biases", "bias_scaled", "turned", "input", "up", "gelu", "down", "scaled", "stored", "back")}
    LOADED = [k.sig(f"expert_loaded_{r}") for r in range(RING)]
    with ExitStack() as ctx:
        rows = k.sb("expert_rows", [P, E0, D], ctx=ctx)
        inputs = k.sb("expert_inputs_turned", [P, E0, P], ctx=ctx)
        w1 = k.sb("expert_w1", [P, RING, F0], ctx=ctx)
        w2 = k.sb("expert_w2", [P, RING, FB0, D], ctx=ctx)
        b2 = k.sb("expert_b2", [P, E0, D], ctx=ctx)
        hidden = k.sb("expert_hidden", [P, 2, FB0, P], ctx=ctx)
        result = k.sb("expert_result", [P, E0, D], ctx=ctx)

        def load(sp, e, q):
            for tile, source in ((w1[:, q, :], A["fc1"][ds(e, 1)].squeeze(0)),
                                 (w2[:, q], A["fc2"][ds(e, 1)].squeeze(0))):
                sp.dma_start(tile, source).then_inc(LOADED[q].sem, 16)

        with nc.Block() as block:
            @block.sync
            def _(sp):
                for half in range(2):
                    experts = slice(half * E0 // 2, (half + 1) * E0 // 2)
                    sp.dma_start(b2[:, experts, :], A["fc2_b"][experts, :].partition_broadcast(P)) \
                      .then_inc(S["biases"].sem, 16)
                for e in range(RING):
                    load(sp, e, e)

            @block.vector
            def _(v):
                v.wait_ge(S["biases"].sem, 2 * 16)
                v.tensor_scalar(b2[:], b2[:], KEEP, None, ALU.mult).then_inc(S["bias_scaled"].sem, 1)
                v.wait_ge(S["bias_scaled"].sem, S["bias_scaled"].at(1))

            @block.gpsimd
            def _(pool):
                for t in range(TT):
                    for n in range(2):
                        pool.indirect_dma_start(
                            out=sent, out_offset=bass.IndirectOffsetOnAxis(ap=scatter[:, t, n:n + 1], axis=0),
                            in_=xt[:, t, :], in_offset=None).then_inc(S["sent"].sem, 16)
                pool.wait_ge(S["sent"].sem, 2 * TT * 16)

        def run(engine, step):
            for e in range(RING):
                step(engine, e, e % 2, e)
            with engine.Fori(1, E0 // RING) as m:
                for q in range(RING):
                    step(engine, m * RING + q, q % 2, q)

        def early(e):
            return isinstance(e, int) and e < 2

        def turn_rows(pe):
            pe.wait_ge(S["rows"].sem, 16 * E0)
            for e in range(E0):
                pe.transpose(k.ps[:, e // 4, e % 4 * P:(e % 4 + 1) * P], rows[:, e, :], k.ident[:]) \
                  .then_inc(S["turned"].sem, 1)
            pe.wait_ge(S["input"].sem, S["input"].at(4))

        def keep_turned(copy, engine, banks):
            for b in banks:
                engine.wait_ge(S["turned"].sem, S["turned"].at(4 * b + 4))
                copy(inputs[:, 4 * b:4 * b + 4, :].rearrange("p e c -> p (e c)"), k.ps[:, b, :]) \
                    .then_inc(S["input"].sem, 1)

        def tensor_step(pe, e, r, q):
            if isinstance(e, int):
                pe.wait_ge(LOADED[q].sem, (e // RING + 1) * 2 * 16)
            else:
                pe.wait_ge(LOADED[q].sem, (e - q) * (2 * 16 // RING) + 2 * 16)
            if not early(e):
                pe.wait_ge(S["gelu"].sem, S["gelu"].at(-1) + e)
            for f in range(FB0):
                last = pe.matmul(k.ps[:, 4 + r, f * P:(f + 1) * P], w1[:, q, f * P:(f + 1) * P],
                                 inputs[:, ds(e, 1), :].squeeze(1), start=True, stop=True)
            last.then_inc(S["up"].sem, 1)
            if not (isinstance(e, int) and e == 0):
                down(pe, e - 1, 1 - r, (q - 1) % RING)

        def down(pe, e, r, q):
            pe.wait_ge(S["gelu"].sem, S["gelu"].at(1) + e)
            if not early(e):
                pe.wait_ge(S["scaled"].sem, S["scaled"].at(-1) + e)
            for f in range(FB0):
                last = pe.matmul(k.ps[:, 6 + r, 0:D], hidden[:, r, f, :], w2[:, q, f, :], start=f == 0,
                                 stop=f == FB0 - 1)
            last.then_inc(S["down"].sem, 1)

        def vector_step(v, e, r, q):
            v.wait_ge(S["down"].sem, S["down"].at(1) + e)
            one = lambda tile: tile[:, ds(e, 1), :].squeeze(1)
            v.scalar_tensor_tensor(out=one(result), in0=k.ps[:, 6 + r, 0:D], scalar=KEEP, in1=one(b2), op0=ALU.mult,
                                   op1=ALU.add).then_inc(S["scaled"].sem, 1)

        def scalar_step(act, e, r, q):
            act.wait_ge(S["up"].sem, S["up"].at(1) + e)
            if not early(e):
                act.wait_ge(S["down"].sem, S["down"].at(-1) + e)
            for f in range(FB0):
                last = act.activation(hidden[:, r, f, :], k.ps[:, 4 + r, f * P:(f + 1) * P], ACT.Gelu,
                                      bias=k.cols[:, ds(e * FB0 + sum(COL_N[:-1]) + f, 1)])
            last.then_inc(S["gelu"].sem, 1)

        with nc.Block() as block:
            @block.sync
            def _(sp):
                for e in range(E0):
                    sp.dma_start(rows[:, e, :], sent[e * CAP:(e + 1) * CAP, :]).then_inc(S["rows"].sem, 16)
                with sp.Fori(1, E0 // RING) as m:
                    for q in range(RING):
                        sp.wait_ge(S["down"].sem, S["down"].at(q + 1 - RING) + m * RING)
                        load(sp, m * RING + q, q)

            @block.tensor
            def _(pe):
                turn_rows(pe)
                run(pe, tensor_step)
                down(pe, E0 - 1, (E0 - 1) % 2, RING - 1)

            @block.vector
            def _(v):
                keep_turned(v.tensor_copy, v, (0, 1))
                run(v, vector_step)

            @block.scalar
            def _(act):
                keep_turned(lambda to, bank: act.activation(to, bank, ACT.Copy), act, (2, 3))
                run(act, scalar_step)

            @block.gpsimd
            def _(pool):
                for m in range(E0 // RING):
                    a = m * RING
                    pool.wait_ge(S["scaled"].sem, S["scaled"].at(a + RING))
                    pool.dma_start(got[a * CAP:(a + RING) * CAP, :].rearrange("(e p) d -> p e d", p=CAP),
                                   result[:, a:a + RING, :]).then_inc(S["stored"].sem, 16)
                pool.wait_ge(S["stored"].sem, 16 * E0 // RING)
                for t in range(TT):
                    for n in range(2):
                        pool.indirect_dma_start(
                            out=back[:, t, n, :], out_offset=None, in_=got,
                            in_offset=bass.IndirectOffsetOnAxis(ap=gather[:, t, n:n + 1], axis=0)) \
                            .then_inc(S["back"].sem, 16)
                pool.wait_ge(S["back"].sem, 2 * TT * 16)


def causal_layer(k, A):
    with ExitStack() as outer:
        hidden = k.sb("hidden", [P, TT, D], ctx=outer)
        normed = k.sb("hidden_normed", [P, TT, D], ctx=outer)
        sent = k.nc.dram_tensor("experts_in", [E0 * CAP + 2 * TOKENS, D], F32, kind="Internal").ap()
        turned = k.sb("hidden_turned", [P, TOKENS], ctx=outer)
        router = k.sb("router", [P, E0], ctx=outer)
        layernorm_rows(k, k.x[:], hidden[:])
        layernorm_rows(k, hidden[:], normed[:])
        transpose_rows(k, normed, turned, k.col("L0_ffn_ln1_w"), k.col("L0_ffn_ln1_b"))
        with ExitStack() as ctx:
            values = k.sb("values_by_head", [P, TT, H0 * 32], ctx=ctx)
            context = k.sb("attention_context", [P, TT, D], ctx=ctx)
            with k.nc.Block() as block:
                @block.sync
                def _(sp):
                    sp.dma_start(router[:], A["router0"]).then_inc(k.sig("router_loaded").sem, 16)

                @block.vector
                def _(v):
                    keep(k, v, v.memset(values[:], 0.0))
                    keep(k, v, v.memset(values[:].rearrange("p t (h c) -> p t h c", h=H0)[:, :, :, HD0:HD0 + 1], 1.0))

            def take_values(v, rows):
                to = values[:].rearrange("p t (h c) -> p t h c", h=H0)
                for t in range(TT):
                    keep(k, v, v.tensor_tensor(to[:, t, :, 0:HD0], rows[:, t, :].rearrange("p (h c) -> p h c", h=H0),
                                               k.row("L0_ffn_v_b").rearrange("p (h c) -> p h c", h=H0), ALU.add))
            project_rows(k, turned, k.square("L0_ffn_v_w"), take_values)
            causal_attention(k, turned, values, context, sent)
            transpose_rows(k, context, turned)

        def take_output(v, rows):
            keep(k, v, v.tensor_tensor(hidden[:], hidden[:], rows, ALU.add))
            keep(k, v, v.tensor_tensor(hidden[:], hidden[:], k.row_of_tiles("L0_ffn_o_b", TT), ALU.add))
        project_rows(k, turned, k.square("L0_ffn_o_w"), take_output)
        layernorm_rows(k, hidden[:], normed[:], gain=k.row("L0_ffn_ln2_w"), shift=k.row("L0_ffn_ln2_b"))
        transpose_rows(k, normed, turned)
        with ExitStack() as ctx:
            weights = k.sb("expert_weights", [P, TT, 2], ctx=ctx)
            scatter = k.sb("scatter_rows", [P, TT, 2], U32, ctx=ctx)
            gather = k.sb("gather_rows", [P, TT, 2], U32, ctx=ctx)
            back = k.sb("experts_back", [P, TT, 2, D], ctx=ctx)
            route(k, normed, turned, router, weights, scatter, gather)
            sixteen_experts(k, A, normed, weights, scatter, gather, sent, back)
            with k.nc.Block() as block:
                @block.vector
                def _(v):
                    over = [P, TT, D]
                    keep(k, v, v.tensor_tensor(k.x[:], k.x[:], hidden[:], ALU.add))
                    for n in range(2):
                        keep(k, v, v.tensor_tensor(normed[:], back[:, :, n, :],
                                                   weights[:, :, n:n + 1].to_broadcast(over), ALU.mult))
                        keep(k, v, v.tensor_tensor(k.x[:], k.x[:], normed[:], ALU.add))



def dense_experts(k, A):
    nc = k.nc
    S = {name: k.sig("dense_" + name) for name in (
        "loaded", "router_up", "router_gelu", "router_down", "up", "gelu", "down", "added", "counted")}
    with ExitStack() as ctx:
        sb = lambda name, shape, dtype=F32: k.sb(name, shape, dtype, ctx=ctx)
        normed = sb("dense_normed", [P, TT, D])
        y = sb("dense_turned", [P, TOKENS])
        rw1 = sb("router_w1", [P, R1])
        rw2 = sb("router_w2", [P, RB1, E1])
        rb2 = sb("router_b2", [P, E1])
        be2 = sb("dense_b2", [E1, D])
        w1 = sb("dense_w1", [P, E1, F1])
        w2 = sb("dense_w2", [P, E1, FB1, D])
        hidden = sb("dense_hidden", [P, 2, FB1, TOKENS])
        logits = sb("dense_logits", [P, TT, 8])
        best = sb("dense_best", [P, TT, 8])
        place = sb("dense_place", [P, TT, 8], U32)
        placef = sb("dense_placef", [P, TT, 2])
        probs = sb("dense_probs", [P, TT, E1])
        total = sb("dense_total", [P, TT, 1])
        chosen = sb("dense_chosen", [P, 2, TT, E1])
        expert = sb("dense_expert", [P, E1])
        weights_t = sb("dense_weights_turned", [E1, TOKENS])
        with nc.Block() as block:
            @block.sync
            def _(sp):
                for tile, source in ((rw1[:], A["rW1"]), (rw2[:], A["rW2"]),
                                     (rb2[:], A["rb2"][0].partition_broadcast(P)), (be2[:], A["be2"]),
                                     (w1[:], A["We1"].rearrange("e d f -> d e f")),
                                     (w2[:], A["We2"].rearrange("e p f d -> p e f d"))):
                    sp.dma_start(tile, source).then_inc(S["loaded"].sem, 16)

            @block.gpsimd
            def _(pool):
                pool.iota(expert[:], [[1, E1]], base=0, channel_multiplier=0,
                          allow_small_or_imprecise_dtypes=True).then_inc(S["counted"].sem, 1)
        layernorm_rows(k, k.x[:], normed[:])
        transpose_rows(k, normed, y)
        LOADED = 6 * 16
        with nc.Block() as block:
            @block.tensor
            def _(pe):
                pe.wait_ge(S["loaded"].sem, LOADED)
                for f in range(RB1):
                    for c in range(2):
                        pe.matmul(k.ps[:, 2 * f + c, :], rw1[:, f * P:(f + 1) * P], y[:, c * 512:(c + 1) * 512],
                                  start=True, stop=True).then_inc(S["router_up"].sem, 1)
                pe.wait_ge(S["router_gelu"].sem, RB1)
                for t in range(TT):
                    for f in range(RB1):
                        last = pe.matmul(k.ps[:, 4, t * E1:(t + 1) * E1], hidden[:, 0, f, t * P:(t + 1) * P],
                                         rw2[:, f, :], start=f == 0, stop=f == RB1 - 1)
                last.then_inc(S["router_down"].sem, 1)

            @block.scalar
            def _(act):
                for f in range(RB1):
                    act.wait_ge(S["router_up"].sem, 2 * f + 2)
                    act.activation(hidden[:, 0, f, :].rearrange("p (b c) -> p b c", b=2), k.ps[:, 2 * f:2 * f + 2, :],
                                   ACT.Gelu, bias=k.col("L1_ffn_rb1", f)).then_inc(S["router_gelu"].sem, 1)

            @block.vector
            def _(v):
                keep(k, v, v.memset(logits[:], NEG))
                v.wait_ge(S["loaded"].sem, LOADED)
                v.wait_ge(S["router_down"].sem, 1)
                keep(k, v, v.tensor_tensor(logits[:, :, 0:E1],
                                           k.ps[:, 4, 0:TT * E1].rearrange("p (t e) -> p t e", e=E1),
                                           rb2[:].unsqueeze(1).to_broadcast([P, TT, E1]), ALU.add))
                for t in range(TT):
                    keep(k, v, v.max(best[:, t, :], logits[:, t, :]))
                    keep(k, v, v.max_index(place[:, t, :], best[:, t, :], logits[:, t, :]))
                keep(k, v, v.tensor_copy(placef[:], place[:, :, 0:2]))
                keep(k, v, v.tensor_tensor(probs[:], logits[:, :, 0:E1], best[:, :, 0:1].to_broadcast([P, TT, E1]),
                                           ALU.subtract))
                for n in range(2):
                    keep(k, v, v.tensor_tensor(chosen[:, n], expert[:].unsqueeze(1).to_broadcast([P, TT, E1]),
                                               placef[:, :, n:n + 1].to_broadcast([P, TT, E1]), ALU.is_equal))
                keep(k, v, v.tensor_tensor(chosen[:, 0], chosen[:, 0], chosen[:, 1], ALU.add))
        with nc.Block() as block:
            @block.scalar
            def _(act):
                act.activation(probs[:], probs[:], ACT.Exp).then_inc(S["counted"].sem, 1)

            @block.vector
            def _(v):
                v.wait_ge(S["counted"].sem, 2)
                keep(k, v, v.reduce_sum(total[:].squeeze(2), probs[:], axis=AX))
                keep(k, v, v.reciprocal(total[:], total[:]))
                keep(k, v, v.tensor_tensor(probs[:], probs[:], total[:].to_broadcast([P, TT, E1]), ALU.mult))
                keep(k, v, v.tensor_tensor(probs[:], probs[:], chosen[:, 0], ALU.mult))
        with nc.Block() as block:
            @block.tensor
            def _(pe):
                for t in range(TT):
                    pe.transpose(k.ps[0:E1, t // 4, t % 4 * P:(t % 4 + 1) * P], probs[:, t, :],
                                 k.ident[:]).then_inc(S["down"].sem, 1)

            @block.vector
            def _(v):
                v.wait_ge(S["down"].sem, TT)
                keep(k, v, v.tensor_copy(weights_t[:].rearrange("e (b c) -> e b c", b=2), k.ps[0:E1, 0:2, :]))
        S["down"].total += TT

        def take_bias(v, rows):
            keep(k, v, v.tensor_tensor(k.x[:], k.x[:], rows, ALU.add))
        project_rows(k, weights_t, be2[:], take_bias)

        with nc.Block() as block:
            @block.tensor
            def _(pe):
                def up(e):
                    for f in range(FB1):
                        n = FB1 * e + f
                        if n >= 2:
                            pe.wait_ge(S["gelu"].sem, n - 1)
                        for c in range(2):
                            last = pe.matmul(k.ps[:, 2 * (f % 2) + c, :], w1[:, e, f * P:(f + 1) * P],
                                             y[:, c * 512:(c + 1) * 512], start=True, stop=True)
                        last.then_inc(S["up"].sem, 1)

                def down(e):
                    pe.wait_ge(S["gelu"].sem, FB1 * (e + 1))
                    if e >= 2:
                        pe.wait_ge(S["added"].sem, TT * (e - 1))
                    for t in range(TT):
                        for f in range(FB1):
                            last = pe.matmul(k.ps[:, 4 + 2 * (e % 2) + t // 4, t % 4 * P:(t % 4 + 1) * P],
                                             hidden[:, e % 2, f, t * P:(t + 1) * P], w2[:, e, f, :], start=f == 0,
                                             stop=f == FB1 - 1)
                        if t % 4 == 3:
                            last.then_inc(S["down"].sem, 1)
                up(0)
                for e in range(1, E1):
                    up(e)
                    down(e - 1)
                down(E1 - 1)

            @block.scalar
            def _(act):
                for e in range(E1):
                    for f in range(FB1):
                        act.wait_ge(S["up"].sem, FB1 * e + f + 1)
                        if e >= 2:
                            act.wait_ge(S["down"].sem, S["down"].at(2 * (e - 1)))
                        act.activation(hidden[:, e % 2, f, :].rearrange("p (b c) -> p b c", b=2),
                                       k.ps[:, 2 * (f % 2):2 * (f % 2) + 2, :], ACT.Gelu,
                                       bias=k.col("L1_ffn_be1", e * FB1 + f)).then_inc(S["gelu"].sem, 1)

            @block.vector
            def _(v):
                for e in range(E1):
                    for t in range(TT):
                        v.wait_ge(S["down"].sem, S["down"].at(2 * e + t // 4 + 1))
                        if e:
                            v.wait_ge(S["added"].sem, TT * (e - 1) + t + 1)
                        v.scalar_tensor_tensor(out=k.x[:, t, :],
                                               in0=k.ps[:, 4 + 2 * (e % 2) + t // 4, t % 4 * P:(t % 4 + 1) * P],
                                               scalar=probs[:, t, e:e + 1], in1=k.x[:, t, :], op0=ALU.mult,
                                               op1=ALU.add).then_inc(S["added"].sem, 1)



def latents_turned(k):
    with ExitStack() as ctx:
        normed = k.sb("latents_normed", [P, TT, D], ctx=ctx)
        layernorm_rows(k, k.x[:], normed[:])
        layernorm_rows(k, normed[:], normed[:])
        transpose_rows(k, normed, k.zT[:, LAT0:REST0], k.col("L1_xcond_ln2_w"), k.col("L1_xcond_ln2_b"))
    with k.nc.Block() as block:
        @block.vector
        def _(v):
            modulation, lat = k.stat[:, 0, 0:1], k.zT[:, LAT0:REST0]
            keep(k, v, v.tensor_scalar(modulation, k.col("cond_1024"), 1.0, None, ALU.add))
            keep(k, v, v.tensor_scalar(lat, lat, modulation, k.col("cond_1024"), ALU.mult, ALU.add))
            for part in (k.zT[:, 0:LAT0], k.zT[:, REST0:KEYS]):
                keep(k, v, v.tensor_scalar(part, part, k.col("L1_xcond_ln1_w"), k.col("L1_xcond_ln1_b"),
                                           ALU.mult, ALU.add))


def perceiver_attention(k, A, rows):
    nc = k.nc
    S = {name: k.sig(name) for name in (
        "weights", "staged", "vsource", "kproj", "khigh", "klow", "vproj", "vready", "vodd",
        "score", "expd", "pv", "counted", "fill", "peak", "qproj", "qhigh", "qlow", "klaid", "peaked", "shifted",
        "shift_row", "folded", "denominators", "inverted", "evacuated", "output", "summed")}
    rate = {"klaid": 1, "staged": 2, "kproj": 1, "khigh": 1, "klow": 1, "vready": 1, "score": 4, "expd": 4, "pv": 2,
            "counted": 2, "fill": 4, "peak": 4}
    of_rest = {"fill": 1, "peak": 1}
    per = {name: n * NS + of_rest.get(name, n) for name, n in rate.items()}

    with ExitStack() as ctx:
        keys = [k.sb("keys", [P, STEPS * STEP], F32R, ctx=ctx) for _ in range(2)]
        pair_keys = k.sb("pair_keys", [P, 2, STEP], F32R, ctx=ctx)
        key_a = k.sb("key_high_low", [P, 2, STEP], F32R, ctx=ctx)
        key_b = k.sb("key_high_one", [P, 2, STEP], F32R, ctx=ctx)
        source = k.sb("value_source", [P, 2, STEP], ctx=ctx)
        value = k.sb("value_step", [P, 2, 2, HD1], ctx=ctx)
        value_rest = k.sb("value_rest", [P, HD1], ctx=ctx)
        value_odd = k.sb("value_odd_head", [P, STEPS, 2 * HD1], ctx=ctx)
        q_a = [k.sb("query_high_high", [P, TOKENS], F32R, ctx=ctx) for _ in range(2)]
        q_b = [k.sb("query_low_shift", [P, TOKENS], F32R, ctx=ctx) for _ in range(2)]
        probs = k.sb("probs", [P, 4, 512], ctx=ctx)
        total = k.sb("probs_total", [P, 4, 512], ctx=ctx)
        head = k.sb("head_output", [P, 2, 512], ctx=ctx)
        inverse = k.sb("inverse_sums", [P, TT], ctx=ctx)
        peaks = k.sb("peaks", [P, TT, STEPS], ctx=ctx)
        peak = k.sb("peak_columns", [P, 64 + TT], ctx=ctx)
        wq = k.sb("wq", [P, 2, P], ctx=ctx)
        wk = k.sb("wk_pair", [P, P], ctx=ctx)
        wo = k.sb("wo", [P, 2, P], ctx=ctx)
        wv = k.sb("wv", [P, P], ctx=ctx)
        scores = k.ps[:, 0:2, :]
        out = k.ps[:, 2:4, :]
        fills = k.ps[:, 4:6, :]
        kbank, vbank = k.ps[:, 6, :], k.ps[:, 7, :]
        between = k.ps[:, 6:8, :]
        halves = (slice(0, HD1), slice(HD1, P))
        latents = k.zT[:, LAT0:REST0]

        cleared = k.sig("cleared")
        with nc.Block() as block:
            @block.vector
            def _(v):
                v.memset(key_a[:].bitcast(F32), 0.0).then_inc(cleared.sem, 1)
                v.memset(peak[:], 0.0).then_inc(cleared.sem, 1)
                for tile in [key_b] + q_b:
                    v.memset(tile[:].bitcast(F32), 0.0).then_inc(cleared.sem, 1)
                v.wait_ge(cleared.sem, cleared.at(5))
                v.memset(key_b[64:65].bitcast(F32), 1.0).then_inc(cleared.sem, 1)
                for tile in keys:
                    v.memset(tile[:, KEYS:STEPS * STEP].bitcast(F32), 0.0).then_inc(cleared.sem, 1)
                v.memset(value_odd[:, NS, :], 0.0).then_inc(cleared.sem, 1)
                v.memset(value_rest[:], 0.0).then_inc(cleared.sem, 1)
                v.wait_ge(cleared.sem, cleared.at(10))
                v.sem_inc(S["score"].sem, 4)
        cleared.total += 10
        S["score"].total += 4

        def at(name, h, j, n):
            return S[name].at(n) + h * per[name] + j * rate[name]

        def inc(name, instruction, n=1):
            instruction.then_inc(S[name].sem, n)

        def wait(engine, name, value):
            if not isinstance(value, int) or value > 0:
                engine.wait_ge(S[name].sem, value)

        def width(j):
            return (LAST if isinstance(j, int) and j == NS else STEP)


        def stage_keys(pool, h, hp, j, r):
            wait(pool, "score", at("score", h, j, -4))
            for rows_, tile in ((slice(0, P), key_a), (slice(0, HD1), key_b)):
                inc("staged", pool.tensor_copy(tile[rows_, r, :], keys[hp][rows_, ds(j * STEP, STEP)]))

        def stage_odd_value(pool, h, j, r):
            wait(pool, "pv", at("pv", h, j, -2))
            inc("vready", pool.tensor_copy(value[:, r].rearrange("p a d -> p (a d)"),
                                           value_odd[:, ds(j, 1), :].squeeze(1)))

        def stage_source(act, pair, j, r):
            w = width(j)
            wait(act, "vproj", S["vproj"].at(-1) + pair * STEPS + j)
            inc("vsource", act.activation(source[:, r, 0:w], k.zT[:, ds(j * STEP, w)], ACT.Copy))

        def keep_values(act, pair, h, j, r):
            wait(act, "vproj", S["vproj"].at(1) + pair * STEPS + j)
            wait(act, "pv", at("pv", h, j, -2))
            if width(j) == LAST:
                inc("vready", act.activation(value_rest[0:LAST, :], vbank[0:LAST, 0:HD1], ACT.Copy))
                inc("vodd", act.activation(value_odd[0:LAST, NS, 0:HD1], vbank[0:LAST, HD1:P], ACT.Copy))
                return
            made = vbank[:, 0:2 * P].rearrange("p (a h d) -> p a h d", a=2, h=2)
            inc("vready", act.activation(value[:, r], made[:, :, 0, :], ACT.Copy))
            inc("vodd", act.activation(value_odd[:, ds(j, 1), :].rearrange("p o (a d) -> p (o a) d", a=2),
                                       made[:, :, 1, :], ACT.Copy))

        def make_values(pe, pair, j, r):
            rows_ = min(width(j), P)
            wait(pe, "vsource", S["vsource"].at(1) + pair * STEPS + j)
            wait(pe, "vodd", S["vodd"].at(0) + pair * STEPS + j)
            for a in range(width(j) // rows_ if rows_ == P else 1):
                last = pe.matmul(vbank[0:rows_, a * P:(a + 1) * P], source[:, r, a * rows_:(a + 1) * rows_], wv[:],
                                 start=True, stop=True)
            inc("vproj", last)

        def score_unit(pe, hp, r, keys_, bank, c):
            cols = slice(c * 512, (c + 1) * 512)
            rows_ = slice(0, keys_.stop - keys_.start)
            pe.matmul(scores[rows_, bank, :], key_a[:, r, keys_], q_a[hp][:, cols], start=True, stop=False)
            return pe.matmul(scores[rows_, bank, :], key_b[:, r, keys_], q_b[hp][:, cols], start=False, stop=True)

        def make_scores(pe, h, hp, j, r, c):
            if c == 0:
                wait(pe, "staged", at("staged", h, j, 2))
            for a in range(2):
                wait(pe, "expd", at("expd", h, j, 2 * c + a - 1))
                inc("score", score_unit(pe, hp, r, slice(a * P, (a + 1) * P), a, c))

        def make_rest_scores(pe, h, hp):
            wait(pe, "staged", at("staged", h, NS, 2))
            for c in range(2):
                wait(pe, "expd", at("expd", h, NS, c - 1))
                inc("score", score_unit(pe, hp, NS % 2, slice(0, LAST), c, c), 2)

        def add_products(pe, h, j, r, c, start, last_step):
            wait(pe, "vready", at("vready", h, j, 1))
            wait(pe, "expd", at("expd", h, j, 2 * c + 2))
            for a in range(2):
                last = pe.matmul(out[a * HD1:(a + 1) * HD1, c, :], value[:, r, a, :], probs[:, 2 * c + a, :],
                                 start=start, stop=last_step and a != c)
            inc("pv", last)

        def add_rest_products(pe, h, hp):
            wait(pe, "vready", at("vready", h, NS, 1))
            wait(pe, "expd", at("expd", h, NS, 4))
            values = value[:, NS % 2, 0, :] if hp else value_rest[:]
            for c in range(2):
                last = pe.matmul(out[c * HD1:(c + 1) * HD1, c, :], values, probs[:, 2 * c, :], start=False, stop=True)
            inc("pv", last, 2)

        def fill_peaks(pe, kp, g, gp, j, part):
            if part == 0 and gp == 0:
                wait(pe, "klaid", at("klaid", kp, j, 1))
            for b in range(2):
                wait(pe, "peak", at("peak", g, j, max(0, b - 1) if first_fill(j, part) else 2 * part + b - 1))
                for n in range(2):
                    t = 4 * part + 2 * b + n
                    last = pe.matmul(fills[:, b, n * STEP:(n + 1) * STEP], q_a[gp][:, t * P:(t + 1) * P],
                                     keys[gp][:, ds(j * STEP, STEP)], start=True, stop=True)
                inc("fill", last)

        def first_fill(j, part):
            return isinstance(j, int) and j == 0 and part == 0

        def fill_rest_peaks(pe, kp, g, gp):
            if gp == 0:
                wait(pe, "klaid", at("klaid", kp, NS, 1))
            wait(pe, "peak", at("peak", g, NS, -1))
            for t in range(TT):
                last = pe.matmul(fills[:, 0, t * LAST:(t + 1) * LAST], q_a[gp][:, t * P:(t + 1) * P],
                                 keys[gp][:, REST0:KEYS], start=True, stop=True)
            inc("fill", last)

        def make_keys(pe, kp, j):
            w = width(j)
            wait(pe, "khigh", at("khigh", kp, j, 0))
            wait(pe, "klow", at("klow", kp, j, 0))
            inc("kproj", pe.matmul(kbank[:, 0:w], wk[:], k.zT[:, ds(j * STEP, w)], start=True, stop=True))

        def keep_high_keys(act, kp, j):
            w = width(j)
            wait(act, "kproj", at("kproj", kp, j, 1))
            wait(act, "klaid", at("klaid", kp, j, 0))
            inc("khigh", act.activation(pair_keys[:, 0, 0:w], kbank[:, 0:w], ACT.Copy))

        def keep_low_keys(v, kp, j):
            w = width(j)
            wait(v, "khigh", at("khigh", kp, j, 1))
            wait(v, "klaid", at("klaid", kp, j, 0))
            inc("klow", v.tensor_tensor(pair_keys[:, 1, 0:w], kbank[:, 0:w], pair_keys[:, 0, 0:w].bitcast(F32),
                                        ALU.subtract))

        def lay_keys(act, kp, j):
            w = width(j)
            wait(act, "klow", at("klow", kp, j, 1))
            for n in range(2):
                for part in range(2):
                    last = act.activation(keys[n][halves[part], ds(j * STEP, w)],
                                          pair_keys[halves[n], part, 0:w].bitcast(F32), ACT.Copy)
            inc("klaid", last)


        def tensor_step(pe, pair, kp, h, hp, g, gp, j, r, first, before):
            if h is not None:
                make_scores(pe, h, hp, j, r, 0)
                if first and before:
                    share_of_rows(pe, h - 1, 1 - hp)
                if first:
                    make_scores(pe, h, hp, j, r, 1)
                if first and before:
                    sum_exponentials(pe, h - 1)
                if first and hp == 0:
                    if g is not None or before:
                        wait(pe, "qlow", S["qlow"].at(1) + (h + 1 if g is not None else h))
                    make_values(pe, pair, 0, 0)
            if first and g is not None:
                if before:
                    wait(pe, "inverted", S["inverted"].at(0) + h)
                wait(pe, "qlow", S["qlow"].at(1) + g)
            if g is not None and gp == 0:
                make_keys(pe, kp, j)
            if not first:
                if h is not None:
                    add_products(pe, h, j - 1, 1 - r, 1, isinstance(j, int) and j == 1, False)
                if g is not None:
                    if gp == 0 and before and isinstance(j, int) and j == 1:
                        wait(pe, "summed", S["summed"].at(0) + h)
                    fill_peaks(pe, kp, g, gp, j - 1, 1 - (gp == 0))
            if h is not None:
                if not first:
                    make_scores(pe, h, hp, j, r, 1)
                if first and before:
                    wait(pe, "evacuated", S["evacuated"].at(0) + h)
                add_products(pe, h, j, r, 0, first, isinstance(j, int) and j == NS - 1)
            if g is not None:
                if gp == 1:
                    if first and before:
                        wait(pe, "summed", S["summed"].at(0) + h)
                    fill_peaks(pe, kp, g, gp, j, 0)
                elif not first:
                    fill_peaks(pe, kp, g, gp, j - 1, 1)
            if h is not None and hp == 0:
                make_values(pe, pair, j + 1, 1 - r)

        def scalar_step(act, pair, kp, h, hp, g, gp, j, r, first):
            if h is not None:
                if hp == 0 and not first:
                    stage_source(act, pair, j + 1, 1 - r)
                exponentials(act, h, j, 0)
                if hp == 0 and first:
                    keep_values(act, pair, h, 0, 0)
            if g is not None and gp == 0:
                keep_high_keys(act, kp, j)
            if h is not None:
                exponentials(act, h, j, 1)
            if g is not None and gp == 0:
                lay_keys(act, kp, j)
            if h is not None:
                if hp == 0:
                    keep_values(act, pair, h, j + 1, 1 - r)

        def exponentials(act, h, j, c):
            for a in range(2):
                wait(act, "score", at("score", h, j, 2 * c + a + 1))
                wait(act, "pv", at("pv", h, j, c - 1))
                wait(act, "counted", at("counted", h, j, c - 1))
                inc("expd", act.activation(probs[:, 2 * c + a, :], scores[:, a, :], ACT.Exp, scale=1.0 / 8.0))

        def rest_exponentials(act, h):
            for c in range(2):
                wait(act, "score", at("score", h, NS, 2 * c + 2))
                wait(act, "pv", at("pv", h, NS, c - 1))
                wait(act, "counted", at("counted", h, NS, c - 1))
                inc("expd", act.activation(probs[0:LAST, 2 * c, :], scores[0:LAST, c, :], ACT.Exp, scale=1.0 / 8.0), 2)

        def vector_step(v, kp, h, hp, g, gp, j, r, first, before):
            if first and h is not None:
                if before:
                    wait(v, "folded", S["folded"].at(0) + h)
                    wait(v, "denominators", S["denominators"].at(0) + h)
                    inc("inverted", v.reciprocal(inverse[:], kbank[:, 0:TT]))
                count(v, h, j, 0, first)
            if g is not None:
                if gp == 0:
                    keep_low_keys(v, kp, j)
                if not first:
                    for f in range(2):
                        read_peak(v, g, j - 1, f + 2 * gp)
            if h is not None and not first:
                count(v, h, j, 0, first)
            if first and before:
                add_rows(v, h - 1)
            if g is not None:
                for f in range(2):
                    if gp == 1:
                        read_peak(v, g, j, f)
                    elif not first:
                        read_peak(v, g, j - 1, f + 2)
            if h is not None:
                count(v, h, j, 1, first)

        def read_peak(v, g, j, f):
            wait(v, "fill", at("fill", g, j, f + 1))
            inc("peak", v.reduce_max(peaks[:, 2 * f:2 * f + 2, ds(j, 1)].rearrange("p t o -> p (t o)"),
                                     fills[:, f % 2, :].rearrange("p (n w) -> p n w", n=2), axis=AX))

        def count(v, h, j, c, first):
            wait(v, "expd", at("expd", h, j, 2 * c + 2))
            units = slice(2 * c, 2 * c + 2)
            if first:
                inc("counted", v.tensor_copy(total[:, units, :], probs[:, units, :]))
            else:
                wait(v, "counted", at("counted", h, j, c - 1))
                inc("counted", v.tensor_tensor(total[:, units, :], total[:, units, :], probs[:, units, :], ALU.add))


        def load_weights(sp, tile, name, n):
            sp.dma_start(tile, A[name][ds(n, 1)].squeeze(0)).then_inc(S["weights"].sem, 16)

        def tensor_between(pe, pair, kp, h, hp, g, gp, after, before, weights):
            if g is not None:
                if gp == 0:
                    fill_peaks(pe, kp, g, gp, NS - 1, 0)
                fill_peaks(pe, kp, g, gp, NS - 1, 1)
            if h is not None:
                make_rest_scores(pe, h, hp)
            if g is not None and gp == 0:
                make_keys(pe, kp, NS)
            if h is not None:
                add_products(pe, h, NS - 1, (NS - 1) % 2, 1, False, True)
            if g is not None:
                fill_rest_peaks(pe, kp, g, gp)
            if h is not None:
                add_rest_products(pe, h, hp)
            if after:
                if gp == 0:
                    wait(pe, "klow", at("klow", kp, NS, 1))
                if before:
                    wait(pe, "inverted", S["inverted"].at(0) + h)
                if h is not None and hp == 0:
                    wait(pe, "vodd", S["vodd"].at(STEPS) + pair * STEPS)
                tensor_queries(pe, hp_of(gp), weights)
            if g is not None:
                wait(pe, "peaked", S["peaked"].at(2) + g * 2)
                for t in range(TT):
                    last = pe.transpose(fills[0:65, t // 4, t % 4 * P:(t % 4 + 1) * P], peak[:, t:t + 65], k.ident[:])
                inc("shifted", last)
                wait(pe, "shift_row", S["shift_row"].at(1) + g)

        def hp_of(gp):
            return 1 - gp

        def tensor_queries(pe, slot, weights):
            wait(pe, "weights", weights)
            for c in range(2):
                last = pe.matmul(between[:, c, :], wq[:, slot, :], latents[:, c * 512:(c + 1) * 512], start=True,
                                 stop=True)
            inc("qproj", last)

        def scalar_queries(act, h, hp):
            wait(act, "qproj", S["qproj"].at(1) + h)
            inc("qhigh", act.activation(q_a[hp][:].rearrange("p (b c) -> p b c", b=2), between, ACT.Copy))

        def vector_queries(v, h, hp):
            wait(v, "qhigh", S["qhigh"].at(1) + h)
            inc("qlow", v.tensor_tensor(q_b[hp][0:HD1, :].rearrange("p (b c) -> p b c", b=2), between[0:HD1],
                                        q_a[hp][0:HD1, :].rearrange("p (b c) -> p b c", b=2).bitcast(F32),
                                        ALU.subtract))

        def scalar_between(act, kp, h, hp, g, gp, after):
            if g is not None and gp == 0:
                keep_high_keys(act, kp, NS)
            if h is not None:
                rest_exponentials(act, h)
            if g is not None and gp == 0:
                lay_keys(act, kp, NS)
            if h is not None:
                wait(act, "pv", at("pv", h, NS, 2))
                wait(act, "output", S["output"].at(0) + h)
                inc("evacuated", act.activation(head[:], out, ACT.Copy))
            if g is not None and gp == 0:
                stage_source(act, kp, 0, 0)
                stage_source(act, kp, 1, 1)
            if after:
                scalar_queries(act, g + 1, hp_of(gp))
            if g is not None:
                wait(act, "shifted", S["shifted"].at(1) + g)
                inc("shift_row", act.activation(q_b[gp][64:65, :], fills[64:65].rearrange("p b c -> p (b c)"),
                                                ACT.Copy))

        def vector_between(v, kp, h, hp, g, gp, after):
            if g is not None:
                for f in range(2 * gp, 4):
                    read_peak(v, g, NS - 1, f)
                if gp == 0:
                    keep_low_keys(v, kp, NS)
            if h is not None:
                wait(v, "expd", at("expd", h, NS, 4))
                wait(v, "counted", at("counted", h, NS, 0))
                some = total[0:LAST].rearrange("p (c a) q -> p c a q", a=2)[:, :, 0, :]
                inc("counted", v.tensor_tensor(some, some, probs[0:LAST].rearrange("p (c a) q -> p c a q", a=2)[:, :, 0, :],
                                               ALU.add), 2)
            if g is not None:
                wait(v, "fill", at("fill", g, NS, 1))
                inc("peak", v.reduce_max(peaks[:, :, NS:NS + 1].rearrange("p t o -> p (t o)"),
                                         fills[:, 0, 0:TT * LAST].rearrange("p (t w) -> p t w", w=LAST), axis=AX))
                wait(v, "peak", at("peak", g, NS, 1))
                inc("peaked", v.reduce_max(peak[:, 64:64 + TT], peaks[:], axis=AX))
                wait(v, "peaked", S["peaked"].at(1) + g * 2)
                inc("peaked", v.tensor_scalar(peak[:, 64:64 + TT], peak[:, 64:64 + TT], -1.0, None, ALU.mult))
            if h is not None:
                wait(v, "counted", at("counted", h, NS, 2))
                half = total[:].rearrange("p (c a) q -> p c a q", a=2)
                inc("folded", v.tensor_tensor(half[:, :, 0, :], half[:, :, 0, :], half[:, :, 1, :], ALU.add))
            if after:
                vector_queries(v, g + 1, hp_of(gp))

        def sum_exponentials(pe, h):
            wait(pe, "folded", S["folded"].at(1) + h)
            wait(pe, "qlow", S["qlow"].at(min(h + 3, H1)) if isinstance(h, int) else S["qlow"].at(3) + h)
            for t in range(TT):
                last = pe.matmul(kbank[:, t:t + 1], total[:, t // 4 * 2, t % 4 * P:(t % 4 + 1) * P], k.ones[:, 0:1],
                                 start=True, stop=True)
            inc("denominators", last)

        def share_of_rows(pe, h, hp):
            wait(pe, "evacuated", S["evacuated"].at(1) + h)
            for t in range(TT):
                last = pe.matmul(fills[:, t // 4, t % 4 * P:(t % 4 + 1) * P],
                                 head[:, t // 4, t % 4 * P:(t % 4 + 1) * P], wo[:, hp, :], start=True, stop=True)
            inc("output", last)

        def add_rows(v, h):
            wait(v, "output", S["output"].at(1) + h)
            wait(v, "inverted", S["inverted"].at(1) + h)
            wait(v, "summed", S["summed"].at(0) + h)
            for t in range(TT):
                last = v.scalar_tensor_tensor(rows[:, t, :], fills[:, t // 4, t % 4 * P:(t % 4 + 1) * P],
                                              inverse[:, t:t + 1], rows[:, t, :], ALU.mult, ALU.add)
            inc("summed", last)

        PEELED = 3
        LOOPS = (H1 - 1 - PEELED) // 2
        WEIGHTS_FIRST, WEIGHTS_HEAD = 5 * 16, 3 * 16

        def run(engine, head_part):
            head_part(engine, None, None, 1, 0, 0, True, False)
            head_part(engine, 0, 0, 0, 1, 1, True, False)
            with engine.Fori(0, LOOPS) as i:
                head_part(engine, i, i * 2 + 1, 1, i * 2 + 2, 0, True, True)
                head_part(engine, i + 1, i * 2 + 2, 0, i * 2 + 3, 1, True, True)
            for h in range(H1 - PEELED, H1):
                g = h + 1 if h + 1 < H1 else None
                head_part(engine, h // 2, h, h % 2, g, 1 - h % 2, h + 2 < H1, True)

        def next_pair(pair):
            return 0 if pair is None else pair + 1

        def steps(engine, step):
            step(0, 0, True)
            step(1, 1, False)
            with engine.Fori(1, NS // 2) as m:
                step(m * 2, 0, False)
                step(m * 2 + 1, 1, False)
            step(NS - 1, 0, False)

        with nc.Block() as block:
            @block.sync
            def _(sp):
                def part(sp, pair, h, hp, g, gp, after, before):
                    if h is None:
                        load_weights(sp, wk[:], "wk", 0)
                        for n in range(2):
                            load_weights(sp, wq[:, n, :], "wq", n)
                        load_weights(sp, wo[:, 0, :], "wo", 0)
                        load_weights(sp, wv[:], "wv", 0)
                        return
                    if g is None:
                        return
                    if before:
                        wait(sp, "output", S["output"].at(0) + h)
                    else:
                        wait(sp, "kproj", at("kproj", 0, NS, 1))
                    if after:
                        load_weights(sp, wq[:, hp, :], "wq", h + 2)
                    load_weights(sp, wo[:, gp, :], "wo", g)
                    if hp == 1:
                        load_weights(sp, wv[:], "wv", pair + 1)
                    elif after:
                        load_weights(sp, wk[:], "wk", pair + 1)
                run(sp, part)

            @block.gpsimd
            def _(pool):
                def part(pool, pair, h, hp, g, gp, after, before):
                    if h is None:
                        return
                    with pool.Fori(0, STEPS // 2) as m:
                        wait(pool, "klaid", at("klaid", pair, NS, 1))
                        if hp == 1:
                            wait(pool, "vodd", S["vodd"].at(STEPS) + pair * STEPS)
                        for r in range(2):
                            stage_keys(pool, h, hp, m * 2 + r, r)
                            if hp == 1:
                                stage_odd_value(pool, h, m * 2 + r, r)
                run(pool, part)

            @block.tensor
            def _(pe):
                def part(pe, pair, h, hp, g, gp, after, before):
                    if h is None:
                        tensor_queries(pe, 0, S["weights"].at(WEIGHTS_FIRST))
                        weights = S["weights"].at(WEIGHTS_FIRST)
                    else:
                        weights = S["weights"].at(WEIGHTS_FIRST + WEIGHTS_HEAD) + h * WEIGHTS_HEAD
                    steps(pe, lambda j, r, first: tensor_step(pe, pair, next_pair(pair), h, hp, g, gp, j, r, first, before))
                    tensor_between(pe, pair, next_pair(pair), h, hp, g, gp, after, before, weights)
                run(pe, part)
                wait(pe, "weights", S["weights"].at(WEIGHTS_FIRST + (H1 - 2) * WEIGHTS_HEAD + 16))
                sum_exponentials(pe, H1 - 1)
                share_of_rows(pe, H1 - 1, (H1 - 1) % 2)

            @block.scalar
            def _(act):
                def part(act, pair, h, hp, g, gp, after, before):
                    if h is None:
                        scalar_queries(act, 0, 0)
                    steps(act, lambda j, r, first: scalar_step(act, pair, next_pair(pair), h, hp, g, gp, j, r, first))
                    scalar_between(act, next_pair(pair), h, hp, g, gp, after)
                run(act, part)

            @block.vector
            def _(v):
                def part(v, pair, h, hp, g, gp, after, before):
                    if h is None:
                        vector_queries(v, 0, 0)
                    steps(v, lambda j, r, first: vector_step(v, next_pair(pair), h, hp, g, gp, j, r, first, before))
                    vector_between(v, next_pair(pair), h, hp, g, gp, after)
                run(v, part)
                wait(v, "denominators", S["denominators"].at(H1))
                inc("inverted", v.reciprocal(inverse[:], kbank[:, 0:TT]))
                add_rows(v, H1 - 1)


def build(nc, A, out, stages=(1, 2, 3, 4)):
    with ExitStack() as ctx:
        k = Core(nc, ctx)
        k.cols = k.sb("column_parameters", [P, sum(COL_N)])
        k.rows = k.sb("row_parameters", [P, len(ROWS), D])
        k.squares = k.sb("square_weights", [P, len(SQUARE), D])
        k.ident = k.sb("identity", [P, P])
        k.ones = k.sb("ones", [P, P])
        k.half = k.sb("minus_half", [P, CT])
        k.stat = k.sb("row_statistics", [P, 3, CT + 1])
        k.bn = k.sb("row_bn_stats", [P, CT + 1, 6])
        k.moments = k.sb("row_moments", [P, CT + 1, 2])
        k.shift = k.sb("row_shift", [P, CT + 1])
        k.x = k.sb("x_rows", [P, TT, D])
        k.zT = k.sb("keys_normed_turned", [P, KEYS])
        slot_attention(k, A, 1 in stages)
        if 2 in stages:
            causal_layer(k, A)
        if 3 in stages:
            latents_turned(k)
            perceiver_attention(k, A, k.x)
        if 4 in stages:
            dense_experts(k, A)
        stored = k.sig("stored")
        with nc.Block() as block:
            @block.sync
            def _(sp):
                sp.dma_start(out[0].rearrange("(t p) d -> p t d", p=P), k.x[:]).then_inc(stored.sem, 16)
                sp.wait_ge(stored.sem, 16)



def kernel(**inputs):
    import numpy as np
    import concourse.bacc as bacc
    from concourse.bass_utils import run_bass_kernel_spmd

    a = {name: np.asarray(value) for name, value in inputs.items()}

    def heads(w, n):
        t = w.reshape(n, HD1, D).transpose(0, 2, 1)
        return np.concatenate([t, t], axis=2)

    laid = {
        "x": a["x"],
        "ctx_1024": a["ctx_1024"],
        "cols": np.concatenate([a[name].reshape(n, P) for name, n in zip(COLS, COL_N)]).T,
        "rows": np.stack([a[name].reshape(D) for name in ROWS]),
        "squares": np.stack([a[name] for name in SQUARE], axis=1),
        "router0": a["L0_ffn_router_w"],
        "fc1": a["L0_ffn_fc1_w"],
        "fc2": a["L0_ffn_fc2_w"].reshape(E0, FB0, P, D).transpose(0, 2, 1, 3),
        "fc2_b": a["L0_ffn_fc2_b"],
        "wq": heads(a["L1_xcond_Wq"], H1),
        "wk": a["L1_xcond_Wkv"][0:H1 * HD1].reshape(H1 // 2, 2 * HD1, D).transpose(0, 2, 1),
        "wv": a["L1_xcond_Wkv"][H1 * HD1:].reshape(H1 // 2, 2 * HD1, D).transpose(0, 2, 1),
        "wo": np.concatenate([a["L1_xcond_Wo"].T.reshape(H1, HD1, D)] * 2, axis=1),
        "rW1": a["L1_ffn_rW1"],
        "rW2": a["L1_ffn_rW2"].reshape(RB1, P, E1).transpose(1, 0, 2),
        "rb2": a["L1_ffn_rb2"].reshape(1, E1),
        "We1": a["L1_ffn_We1"],
        "We2": a["L1_ffn_We2"].reshape(E1, FB1, P, D).transpose(0, 2, 1, 3),
        "be2": a["L1_ffn_be2"],
    }
    nc = bacc.Bacc("TRN2", target_bir_lowering=False, num_devices=1)
    arrays, views = {}, {}
    for name, value in laid.items():
        value = np.ascontiguousarray(value)
        arrays["in_" + name] = value
        views[name] = nc.dram_tensor("in_" + name, value.shape, mybir.dt.from_np(value.dtype),
                                     kind="ExternalInput").ap()
    out = nc.dram_tensor("out", (1, TOKENS, D), F32, kind="ExternalOutput").ap()
    build(nc, views, out)
    result = run_bass_kernel_spmd(nc, [arrays], core_ids=[0])
    return result.results[0]["out"]
```
